# Optimizing a Trainium2 kernel written in Bass

```python
import numpy as np
import jax
import jax.numpy as jnp

def _softmax(x, axis=-1):
    return jax.nn.softmax(x, axis=axis)

def _gelu(x):
    return jax.nn.gelu(x, approximate=True)

def _silu(x):
    return jax.nn.silu(x)

def _sigmoid(x):
    return jax.nn.sigmoid(x)

def _layernorm(x, axis=-1, eps=1e-05):
    m = jnp.mean(x, axis=axis, keepdims=True)
    v = jnp.var(x, axis=axis, keepdims=True)
    return (x - m) / jnp.sqrt(v + eps)

def _scatter_add(tgt, idx, src, axis=0):
    return tgt.at[idx].add(src)

def _segment_sum(src, seg, n):
    return jax.ops.segment_sum(src, seg, n)
kernel_name = 'mk_vit_tower_cls_d2_tok_img512_r4_736758'

def setup_inputs(seed: int=0):
    np.random.seed(seed)
    _w = jnp.asarray

    def _rec_inputs():
        import jax
        import jax.numpy as jnp
        _rk = jax.random.key(seed)
        x = -0.000178447 + 0.99995 * jax.random.normal(jax.random.fold_in(_rk, 1), (64, 3, 176, 208), jnp.float32)
        cls_tok = 0.02 * jax.random.normal(jax.random.fold_in(_rk, 5), (1, 1, 128), jnp.float32)
        return (x, cls_tok)
    x, cls_tok = _rec_inputs()

    def _L0_tok_setup():
        import jax, jax.numpy as jnp
        import numpy as np
        P1, P2, C = (16, 16, 3)
        PW, PH = (176 // P1, 208 // P2)
        key = jax.random.key(seed)
        k1, k2, k3, k4, k5 = jax.random.split(key, 5)
        B, D = (64, 128)
        patch_dim = P1 * P2 * C
        return {'x': jax.random.normal(k1, (B, C, PW * P1, PH * P2), dtype=jnp.float32), 'W': jax.random.normal(k2, (D, patch_dim), dtype=jnp.float32) * 0.02, 'b': jax.random.normal(k3, (D,), dtype=jnp.float32) * 0.02, 'cls_token': jax.random.uniform(k4, (1, 1, D), dtype=jnp.float32), 'pos_emb': jax.random.normal(k5, (1, PW * PH + 1, 1), dtype=jnp.float32)}
    _L0_tok_all = _L0_tok_setup()
    _L0_tok_in = {k: v for k, v in _L0_tok_all.items() if k in ('W', 'b', 'cls_token', 'pos_emb')}
    del _L0_tok_all

    def _L0_attn_setup():
        import jax, jax.numpy as jnp
        import numpy as np
        B, N, W, H = (8, 1024, 128, 8)
        D = W // H
        INNER_LR = 1.0

        def _reference_tuple_inner(x, W_phi, b_phi, W_e, b_e, W_g, g_bias, W_psi, b_psi, W_h, h_bias):
            Bn, Nn, Wd = x.shape
            Hh = W_phi.shape[0]
            Z = jnp.einsum('bnw,hwd->bhnd', x, W_phi) + b_phi[None, :, None, :]
            Y = jnp.einsum('bhnd,hde->bhne', Z, W_e) + b_e[None, :, None, :]
            O = jnp.einsum('bhne,hew->bhnw', Y, W_g) + g_bias
            R = O - x[:, None]
            scale = Hh / (Nn * Wd)
            loss0 = 0.5 * scale * jnp.sum(R * R, axis=(-2, -1))
            dO = R * scale
            Gy = jnp.einsum('bhnw,hew->bhne', dO, W_g)
            dWe = jnp.einsum('bhnd,bhne->bhde', Z, Gy)
            dbe = Gy.sum(axis=2)
            We_new = W_e[None] - INNER_LR * dWe
            be_new = b_e[None] - INNER_LR * dbe
            Y2 = jnp.einsum('bhnd,bhde->bhne', Z, We_new) + be_new[:, :, None, :]
            O2 = jnp.einsum('bhne,hew->bhnw', Y2, W_g) + g_bias
            R2 = O2 - x[:, None]
            loss_final = 0.5 * scale * jnp.sum(R2 * R2, axis=(-2, -1))
            P = jnp.einsum('bnw,hwd->bhnd', x, W_psi) + b_psi[None, :, None, :]
            Q = jnp.einsum('bhnd,bhde->bhne', P, We_new) + be_new[:, :, None, :]
            out = jnp.einsum('bhne,hew->bnw', Q, W_h) + h_bias
            return (out, loss0, loss_final)
        key = jax.random.key(seed)
        ks = jax.random.split(key, 11)

        def init(k, shape, fan_in):
            return jax.random.normal(k, shape, jnp.float32) * (1.0 / fan_in) ** 0.5
        return {'x': jax.random.normal(ks[0], (B, N, W), jnp.float32), 'W_phi': init(ks[1], (H, W, D), W), 'b_phi': jnp.zeros((H, D), jnp.float32), 'W_e': init(ks[2], (H, D, D), D), 'b_e': jnp.zeros((H, D), jnp.float32), 'W_g': init(ks[3], (H, D, W), D), 'g_bias': jnp.zeros((1, W), jnp.float32), 'W_psi': init(ks[4], (H, W, D), W), 'b_psi': jnp.zeros((H, D), jnp.float32), 'W_h': init(ks[5], (H, D, W), D), 'h_bias': jnp.zeros((1, W), jnp.float32)}
    _L0_attn_all = _L0_attn_setup()
    _L0_attn_in = {k: v for k, v in _L0_attn_all.items() if k in ('W_phi', 'b_phi', 'W_e', 'b_e', 'W_g', 'g_bias', 'W_psi', 'b_psi', 'W_h', 'h_bias')}
    del _L0_attn_all

    def _L0_ffn_setup():
        import jax, jax.numpy as jnp
        import numpy as np
        LUT_SIZE = 1024
        TWO_PI = 2.0 * np.pi

        def _lut_tables():
            ang = jnp.arange(LUT_SIZE, dtype=jnp.float32) * (TWO_PI / LUT_SIZE)
            return (jnp.sin(ang), jnp.cos(ang))

        def _lookup_sin_cos(theta):
            sin_t, cos_t = _lut_tables()
            idx = jnp.mod(jnp.round(theta * (LUT_SIZE / TWO_PI)), LUT_SIZE).astype(jnp.int32)
            return (sin_t[idx], cos_t[idx])
        key = jax.random.key(seed)
        ks = jax.random.split(key, 5)
        B, S, D, N = (2, 128, 128, 64)
        x = jax.random.normal(ks[0], (B, S, D), dtype=jnp.float32)
        W = jax.random.normal(ks[1], (N, D), dtype=jnp.float32) * 0.02
        B_param = jnp.zeros((N, D), dtype=jnp.float32)
        attn_cos = jnp.ones((N, D), dtype=jnp.float32)
        attn_sin = jnp.ones((N, D), dtype=jnp.float32)
        bound = 0.5 * np.sqrt(6.0 / (N + D))
        proj_cos_w = jax.random.uniform(ks[2], (D, N), jnp.float32, -bound, bound)
        proj_sin_w = jax.random.uniform(ks[3], (D, N), jnp.float32, -bound, bound)
        return {'x': x, 'W': W, 'B_param': B_param, 'attn_cos': attn_cos, 'attn_sin': attn_sin, 'proj_cos_w': proj_cos_w, 'proj_sin_w': proj_sin_w}
    _L0_ffn_all = _L0_ffn_setup()
    _L0_ffn_in = {k: v for k, v in _L0_ffn_all.items() if k in ('W', 'B_param', 'attn_cos', 'attn_sin', 'proj_cos_w', 'proj_sin_w')}
    del _L0_ffn_all

    def _L1_attn_setup():
        import jax, jax.numpy as jnp
        import numpy as np
        B, S, D_MODEL, D_ATT = (4, 1024, 128, 64)
        EPS = 1e-05
        key = jax.random.key(seed)
        ks = jax.random.split(key, 10)
        s_in = 1.0 / np.sqrt(D_MODEL)
        return {'x': jax.random.normal(ks[0], (B, S, D_MODEL), jnp.float32), 'Wq': jax.random.uniform(ks[1], (D_MODEL, D_ATT), jnp.float32, -s_in, s_in), 'bq': jax.random.uniform(ks[2], (D_ATT,), jnp.float32, -s_in, s_in), 'Wk': jax.random.uniform(ks[3], (D_MODEL, D_ATT), jnp.float32, -s_in, s_in), 'bk': jax.random.uniform(ks[4], (D_ATT,), jnp.float32, -s_in, s_in), 'Wv': jax.random.uniform(ks[5], (D_MODEL, D_MODEL), jnp.float32, -s_in, s_in), 'bv': jax.random.uniform(ks[6], (D_MODEL,), jnp.float32, -s_in, s_in), 'gamma': jnp.ones((D_MODEL,), jnp.float32), 'beta': jnp.zeros((D_MODEL,), jnp.float32)}
    _L1_attn_all = _L1_attn_setup()
    _L1_attn_in = {k: v for k, v in _L1_attn_all.items() if k in ('Wq', 'bq', 'Wk', 'bk', 'Wv', 'bv', 'gamma', 'beta')}
    del _L1_attn_all

    def _L1_ffn_setup():
        import jax, jax.numpy as jnp
        import numpy as np
        B, S, D, H, E = (4, 512, 128, 8, 8)
        FF = 4 * D
        HD = D // H
        EPS = 1e-05

        def _layernorm(x, g, b):
            mu = jnp.mean(x, axis=-1, keepdims=True)
            var = jnp.mean((x - mu) ** 2, axis=-1, keepdims=True)
            return (x - mu) * jax.lax.rsqrt(var + EPS) * g + b
        key = jax.random.key(seed)
        ks = jax.random.split(key, 16)
        s = 0.02
        return {'x': jax.random.normal(ks[0], (B, S, D), dtype=jnp.float32), 'ln1_g': jnp.ones((D,), jnp.float32), 'ln1_b': jnp.zeros((D,), jnp.float32), 'Wq': jax.random.normal(ks[1], (D, D), jnp.float32) * s, 'bq': jnp.zeros((D,), jnp.float32), 'Wk': jax.random.normal(ks[2], (D, D), jnp.float32) * s, 'bk': jnp.zeros((D,), jnp.float32), 'Wv': jax.random.normal(ks[3], (D, D), jnp.float32) * s, 'bv': jnp.zeros((D,), jnp.float32), 'Wo': jax.random.normal(ks[4], (D, D), jnp.float32) * s, 'bo': jnp.zeros((D,), jnp.float32), 'gate_W': jax.random.normal(ks[5], (D, E), jnp.float32) * s, 'gate_b': jnp.zeros((E,), jnp.float32), 'W1': jax.random.normal(ks[6], (E, D, FF), jnp.float32) * s, 'b1': jnp.zeros((E, FF), jnp.float32), 'W2': jax.random.normal(ks[7], (E, FF, D), jnp.float32) * s, 'b2': jnp.zeros((E, D), jnp.float32)}
    _L1_ffn_all = _L1_ffn_setup()
    _L1_ffn_in = {k: v for k, v in _L1_ffn_all.items() if k in ('ln1_g', 'ln1_b', 'Wq', 'bq', 'Wk', 'bk', 'Wv', 'bv', 'Wo', 'bo', 'gate_W', 'gate_b', 'W1', 'b1', 'W2', 'b2')}
    del _L1_ffn_all
    return {'x': x, 'cls_tok': cls_tok, 'L0_tok_W': _L0_tok_in['W'], 'L0_tok_b': _L0_tok_in['b'], 'L0_tok_cls_token': _L0_tok_in['cls_token'], 'L0_tok_pos_emb': _L0_tok_in['pos_emb'], 'L0_attn_W_phi': _L0_attn_in['W_phi'], 'L0_attn_b_phi': _L0_attn_in['b_phi'], 'L0_attn_W_e': _L0_attn_in['W_e'], 'L0_attn_b_e': _L0_attn_in['b_e'], 'L0_attn_W_g': _L0_attn_in['W_g'], 'L0_attn_g_bias': _L0_attn_in['g_bias'], 'L0_attn_W_psi': _L0_attn_in['W_psi'], 'L0_attn_b_psi': _L0_attn_in['b_psi'], 'L0_attn_W_h': _L0_attn_in['W_h'], 'L0_attn_h_bias': _L0_attn_in['h_bias'], 'L0_ffn_W': _L0_ffn_in['W'], 'L0_ffn_B_param': _L0_ffn_in['B_param'], 'L0_ffn_attn_cos': _L0_ffn_in['attn_cos'], 'L0_ffn_attn_sin': _L0_ffn_in['attn_sin'], 'L0_ffn_proj_cos_w': _L0_ffn_in['proj_cos_w'], 'L0_ffn_proj_sin_w': _L0_ffn_in['proj_sin_w'], 'L1_attn_Wq': _L1_attn_in['Wq'], 'L1_attn_bq': _L1_attn_in['bq'], 'L1_attn_Wk': _L1_attn_in['Wk'], 'L1_attn_bk': _L1_attn_in['bk'], 'L1_attn_Wv': _L1_attn_in['Wv'], 'L1_attn_bv': _L1_attn_in['bv'], 'L1_attn_gamma': _L1_attn_in['gamma'], 'L1_attn_beta': _L1_attn_in['beta'], 'L1_ffn_ln1_g': _L1_ffn_in['ln1_g'], 'L1_ffn_ln1_b': _L1_ffn_in['ln1_b'], 'L1_ffn_Wq': _L1_ffn_in['Wq'], 'L1_ffn_bq': _L1_ffn_in['bq'], 'L1_ffn_Wk': _L1_ffn_in['Wk'], 'L1_ffn_bk': _L1_ffn_in['bk'], 'L1_ffn_Wv': _L1_ffn_in['Wv'], 'L1_ffn_bv': _L1_ffn_in['bv'], 'L1_ffn_Wo': _L1_ffn_in['Wo'], 'L1_ffn_bo': _L1_ffn_in['bo'], 'L1_ffn_gate_W': _L1_ffn_in['gate_W'], 'L1_ffn_gate_b': _L1_ffn_in['gate_b'], 'L1_ffn_W1': _L1_ffn_in['W1'], 'L1_ffn_b1': _L1_ffn_in['b1'], 'L1_ffn_W2': _L1_ffn_in['W2'], 'L1_ffn_b2': _L1_ffn_in['b2']}

def reference(x, cls_tok, L0_tok_W, L0_tok_b, L0_tok_cls_token, L0_tok_pos_emb, L0_attn_W_phi, L0_attn_b_phi, L0_attn_W_e, L0_attn_b_e, L0_attn_W_g, L0_attn_g_bias, L0_attn_W_psi, L0_attn_b_psi, L0_attn_W_h, L0_attn_h_bias, L0_ffn_W, L0_ffn_B_param, L0_ffn_attn_cos, L0_ffn_attn_sin, L0_ffn_proj_cos_w, L0_ffn_proj_sin_w, L1_attn_Wq, L1_attn_bq, L1_attn_Wk, L1_attn_bk, L1_attn_Wv, L1_attn_bv, L1_attn_gamma, L1_attn_beta, L1_ffn_ln1_g, L1_ffn_ln1_b, L1_ffn_Wq, L1_ffn_bq, L1_ffn_Wk, L1_ffn_bk, L1_ffn_Wv, L1_ffn_bv, L1_ffn_Wo, L1_ffn_bo, L1_ffn_gate_W, L1_ffn_gate_b, L1_ffn_W1, L1_ffn_b1, L1_ffn_W2, L1_ffn_b2):
    import jax
    import jax.numpy as jnp

    def _L0_tok_ref(x, W, b, cls_token, pos_emb):
        import jax, jax.numpy as jnp
        import numpy as np
        P1, P2, C = (16, 16, 3)
        PW, PH = (176 // P1, 208 // P2)
        B = x.shape[0]
        patches = x.reshape(B, C, PW, P1, PH, P2)
        patches = patches.transpose(0, 2, 4, 3, 5, 1).reshape(B, PW * PH, P1 * P2 * C)
        proj = jnp.einsum('bnp,dp->bnd', patches, W) + b
        cls = jnp.broadcast_to(cls_token, (B, 1, cls_token.shape[-1]))
        out = jnp.concatenate([cls, proj], axis=1) + pos_emb
        return out

    def _L0_attn_ref(x, W_phi, b_phi, W_e, b_e, W_g, g_bias, W_psi, b_psi, W_h, h_bias):
        import jax, jax.numpy as jnp
        import numpy as np
        B, N, W, H = (8, 1024, 128, 8)
        D = W // H
        INNER_LR = 1.0

        def _reference_tuple_inner(x, W_phi, b_phi, W_e, b_e, W_g, g_bias, W_psi, b_psi, W_h, h_bias):
            Bn, Nn, Wd = x.shape
            Hh = W_phi.shape[0]
            Z = jnp.einsum('bnw,hwd->bhnd', x, W_phi) + b_phi[None, :, None, :]
            Y = jnp.einsum('bhnd,hde->bhne', Z, W_e) + b_e[None, :, None, :]
            O = jnp.einsum('bhne,hew->bhnw', Y, W_g) + g_bias
            R = O - x[:, None]
            scale = Hh / (Nn * Wd)
            loss0 = 0.5 * scale * jnp.sum(R * R, axis=(-2, -1))
            dO = R * scale
            Gy = jnp.einsum('bhnw,hew->bhne', dO, W_g)
            dWe = jnp.einsum('bhnd,bhne->bhde', Z, Gy)
            dbe = Gy.sum(axis=2)
            We_new = W_e[None] - INNER_LR * dWe
            be_new = b_e[None] - INNER_LR * dbe
            Y2 = jnp.einsum('bhnd,bhde->bhne', Z, We_new) + be_new[:, :, None, :]
            O2 = jnp.einsum('bhne,hew->bhnw', Y2, W_g) + g_bias
            R2 = O2 - x[:, None]
            loss_final = 0.5 * scale * jnp.sum(R2 * R2, axis=(-2, -1))
            P = jnp.einsum('bnw,hwd->bhnd', x, W_psi) + b_psi[None, :, None, :]
            Q = jnp.einsum('bhnd,bhde->bhne', P, We_new) + be_new[:, :, None, :]
            out = jnp.einsum('bhne,hew->bnw', Q, W_h) + h_bias
            return (out, loss0, loss_final)
        return _reference_tuple_inner(x, W_phi, b_phi, W_e, b_e, W_g, g_bias, W_psi, b_psi, W_h, h_bias)[0]

    def _L0_ffn_ref(x, W, B_param, attn_cos, attn_sin, proj_cos_w, proj_sin_w):
        import jax, jax.numpy as jnp
        import numpy as np
        LUT_SIZE = 1024
        TWO_PI = 2.0 * np.pi

        def _lut_tables():
            ang = jnp.arange(LUT_SIZE, dtype=jnp.float32) * (TWO_PI / LUT_SIZE)
            return (jnp.sin(ang), jnp.cos(ang))

        def _lookup_sin_cos(theta):
            sin_t, cos_t = _lut_tables()
            idx = jnp.mod(jnp.round(theta * (LUT_SIZE / TWO_PI)), LUT_SIZE).astype(jnp.int32)
            return (sin_t[idx], cos_t[idx])
        wavelength = 1.0 + jnp.abs(W)
        theta = x[..., None, :] / wavelength + B_param
        sin_theta, cos_theta = _lookup_sin_cos(theta)
        cos_sum = jnp.sum(cos_theta * attn_cos, axis=-1)
        sin_sum = jnp.sum(sin_theta * attn_sin, axis=-1)
        out = jnp.einsum('bsn,dn->bsd', cos_sum, proj_cos_w) + jnp.einsum('bsn,dn->bsd', sin_sum, proj_sin_w)
        return jax.nn.silu(out)

    def _L1_attn_ref(x, Wq, bq, Wk, bk, Wv, bv, gamma, beta):
        import jax, jax.numpy as jnp
        import numpy as np
        B, S, D_MODEL, D_ATT = (4, 1024, 128, 64)
        EPS = 1e-05
        q = jnp.einsum('bsd,de->bse', x, Wq) + bq
        k = jnp.einsum('bsd,de->bse', x, Wk) + bk
        v = jnp.einsum('bsd,de->bse', x, Wv) + bv
        scores = jnp.einsum('bqe,bke->bqk', q, k)
        seq = x.shape[1]
        causal = jnp.tril(jnp.ones((seq, seq), dtype=bool))
        scores = jnp.where(causal, scores, -jnp.inf)
        attn = jax.nn.softmax(scores, axis=-1)
        o = jnp.einsum('bqk,bkd->bqd', attn, v)
        y = x + o
        mu = jnp.mean(y, axis=-1, keepdims=True)
        var = jnp.mean(jnp.square(y - mu), axis=-1, keepdims=True)
        return (y - mu) * jax.lax.rsqrt(var + EPS) * gamma + beta

    def _L1_ffn_ref(x, ln1_g, ln1_b, Wq, bq, Wk, bk, Wv, bv, Wo, bo, gate_W, gate_b, W1, b1, W2, b2):
        import jax, jax.numpy as jnp
        import numpy as np
        B, S, D, H, E = (4, 512, 128, 8, 8)
        FF = 4 * D
        HD = D // H
        EPS = 1e-05

        def _layernorm(x, g, b):
            mu = jnp.mean(x, axis=-1, keepdims=True)
            var = jnp.mean((x - mu) ** 2, axis=-1, keepdims=True)
            return (x - mu) * jax.lax.rsqrt(var + EPS) * g + b
        b, s, d = x.shape
        q = (x @ Wq + bq).reshape(b, s, H, HD)
        k = (x @ Wk + bk).reshape(b, s, H, HD)
        v = (x @ Wv + bv).reshape(b, s, H, HD)
        scores = jnp.einsum('bqhd,bkhd->bhqk', q, k) / jnp.sqrt(jnp.float32(HD))
        attn = jax.nn.softmax(scores, axis=-1)
        o = jnp.einsum('bhqk,bkhd->bqhd', attn, v).reshape(b, s, d) @ Wo + bo
        h = _layernorm(x + o, ln1_g, ln1_b)
        t = h.reshape(b * s, d)
        probs = jax.nn.softmax(t @ gate_W + gate_b, axis=-1)
        idx = jnp.argmax(probs, axis=-1)
        gw = jnp.max(probs, axis=-1)
        hid = jax.nn.gelu(jnp.einsum('nd,edf->enf', t, W1) + b1[:, None, :])
        out_all = jnp.einsum('enf,efd->end', hid, W2) + b2[:, None, :]
        onehot = jax.nn.one_hot(idx, E, dtype=t.dtype)
        out = jnp.einsum('ne,end->nd', onehot, out_all)
        out = out * gw[:, None]
        return out.reshape(b, s, d)
    h = _L0_tok_ref(x, L0_tok_W, L0_tok_b, L0_tok_cls_token, L0_tok_pos_emb)
    h = jnp.concatenate([jnp.broadcast_to(cls_tok, (h.shape[0], 1, h.shape[2])), h], axis=1)
    h = h + _L0_attn_ref(_layernorm(h, axis=-1), L0_attn_W_phi, L0_attn_b_phi, L0_attn_W_e, L0_attn_b_e, L0_attn_W_g, L0_attn_g_bias, L0_attn_W_psi, L0_attn_b_psi, L0_attn_W_h, L0_attn_h_bias)
    h = h + _L0_ffn_ref(_layernorm(h, axis=-1), L0_ffn_W, L0_ffn_B_param, L0_ffn_attn_cos, L0_ffn_attn_sin, L0_ffn_proj_cos_w, L0_ffn_proj_sin_w)
    h = h + _L1_attn_ref(_layernorm(h, axis=-1), L1_attn_Wq, L1_attn_bq, L1_attn_Wk, L1_attn_bk, L1_attn_Wv, L1_attn_bv, L1_attn_gamma, L1_attn_beta)
    h = h + _L1_ffn_ref(_layernorm(h, axis=-1), L1_ffn_ln1_g, L1_ffn_ln1_b, L1_ffn_Wq, L1_ffn_bq, L1_ffn_Wk, L1_ffn_bk, L1_ffn_Wv, L1_ffn_bv, L1_ffn_Wo, L1_ffn_bo, L1_ffn_gate_W, L1_ffn_gate_b, L1_ffn_W1, L1_ffn_b1, L1_ffn_W2, L1_ffn_b2)
    return h

_drawn_inputs = setup_inputs


def setup_inputs(seed=0):
    import zlib

    import numpy as np

    out = dict(_drawn_inputs(seed))
    spreads = {'L0_attn_b_phi': (0.0, 0.564),
     'L0_attn_b_e': (0.0, 0.618),
     'L0_attn_g_bias': (0.0, 0.8),
     'L0_attn_b_psi': (0.0, 0.612),
     'L0_attn_h_bias': (0.0, 0.8),
     'L0_ffn_B_param': (0.0, 0.446),
     'L0_ffn_attn_cos': (1.0, 0.2),
     'L0_ffn_attn_sin': (1.0, 0.6),
     'L1_attn_gamma': (1.0, 0.6),
     'L1_attn_beta': (0.0, 0.8),
     'L1_ffn_ln1_g': (1.0, 0.6),
     'L1_ffn_ln1_b': (0.0, 0.8),
     'L1_ffn_bq': (0.0, 0.8),
     'L1_ffn_bk': (0.0, 2.0),
     'L1_ffn_bv': (0.0, 0.8),
     'L1_ffn_bo': (0.0, 0.8),
     'L1_ffn_gate_b': (0.0, 0.8),
     'L1_ffn_b1': (0.0, 0.8),
     'L1_ffn_b2': (0.0, 2.0)}
    factors = {'cls_tok': 5.742,
     'L0_tok_b': 8.0,
     'L0_tok_cls_token': 7.028,
     'L0_ffn_W': 8.0,
     'L1_attn_Wq': 8.0,
     'L1_attn_bq': 51.489,
     'L1_attn_Wk': 21.425,
     'L1_attn_bk': 64.0,
     'L1_attn_bv': 8.0,
     'L1_ffn_Wq': 8.0,
     'L1_ffn_Wk': 8.0,
     'L1_ffn_Wv': 8.0,
     'L1_ffn_Wo': 8.0,
     'L1_ffn_gate_W': 8.0,
     'L1_ffn_W1': 8.0,
     'L1_ffn_W2': 8.0}
    for name, (base, spread) in spreads.items():
        noise = np.random.default_rng([zlib.crc32(name.encode()), seed]).standard_normal(out[name].shape)
        drawn = base * np.exp(spread * noise) if base else spread * noise
        out[name] = jnp.asarray(drawn.astype(out[name].dtype))
    for name, factor in factors.items():
        out[name] = (out[name] * factor).astype(out[name].dtype)
    return out
```

```python
from contextlib import ExitStack

import numpy as np

import concourse.bass as bass
from concourse import mybir

ALU = mybir.AluOpType
ACT = mybir.ActivationFunctionType
F32 = mybir.dt.float32
I16 = mybir.dt.int16
AX = mybir.AxisListType.X

B, C, IH, IW = 64, 3, 176, 208
PS = 16
PW, PH = IH // PS, IW // PS
NPATCH = PW * PH
N = NPATCH + 2
D = 128
IMGS = 4
CHUNKS = B // IMGS
T = IMGS * N
HALF = T // 2
TT = 116
NT = T // TT
QA = 73
QB = N - QA
QS = ((0, QA), (QA, QB))
H, HD = 8, 16
E, FF = 8, 512
FC = FF // 128
DA = 64
NW = 64
NJ = 4
NI = NW // NJ
LUT = 1024
EPS = 1e-5
MASKED = -1e30
MAGIC = 12582912.0
LR_SCALE = H / (N * D)
TO_LUT = float(np.float32(LUT / (2.0 * np.pi)))
FROM_LUT = float(np.float32(2.0 * np.pi / LUT))
MINUS_PI = -3.1415925

FRONT_PE = ("embed0", "embed1", "h0", "x1T", "zg0", "zg1", "cross", "pT", "qT", "attn", "x2T")
FRONT_ACT = ("h0", "x1Ta", "x1Tb", "pT", "qT0", "qT1", "qT2", "qT3", "x2Ta", "x2Tb")
FRONT_DVE = ("cls", "emb0", "emb1", "bn1", "ln1", "x1", "zg0a", "zg0b", "zg1a", "zg1b", "masked", "wnew", "bnew",
             "h1", "bn2", "ln2", "x2")
FRONT_POOL = ("eps1", "rstd1", "hb", "eps2", "rstd2", "h1hold")
BACK_PE = ("x3T", "q3", "k3", "s3", "v3a", "v3b", "pTa", "oT", "o3", "x4T", "q4", "k4", "v4",
           *(f"s4_{r}" for r in range(2 * IMGS)), "mT",
           *(f"{s}_{i}" for i in range(IMGS) for s in ("stA", "stB", "pv")),
           "sums", "wo", "tT", "gate", "coefT", "b2",
           *(f"{s}_{e}" for e in range(E) for s in ("hid0", "hid1", "hid2", "hid3", "hid4", "hid5", "hid6", "hid7", "out")))
BACK_ACT = ("x3Ta", "x3Tb", "q3", "k3", "v3a", "v3b", "e3", "pTa", "pTb", "oT", "x4Ta", "x4Tb",
            "q4a", "q4b", "k4a", "k4b", "v4a", "v4b", "mT",
            *(f"{s}_{i}" for i in range(IMGS) for s in ("expA", "expB", "pv")),
            "tTa", "tTb", "gexp", "coefTa", "coefTb",
            *(f"gelu{k}_{e}" for e in range(E) for k in range(8)))
BACK_DVE = ("bn3", "ln3", "x3", "mask3a", "mask3b", "max3", "sub3", "sum3", "rec3", "p3", "y3",
            "bny", "lny", "zy", "h3", "bn4", "ln4", "x4",
            *(f"s4_{r}" for r in range(2 * IMGS)), "rsum", "onT", "y4", "bn5", "ln5", "z5", "t5",
            "glog", "gmax", "gsub", "gsum", "gemax", "grec", "gmask", "gscore", "gsmax", "goh", "gw", "coef",
            "acc0", *(f"acc_{e}" for e in range(E)))
BACK_POOL = ("s3", "eps3", "rstd3", "hb3", "epsy", "rstdy", "eps4", "rstd4", "x4b", "eps5", "rstd5")
TRIG_DVE = tuple(f"{s}{g}" for g in range(NI) for s in ("k", "add", "and"))
TRIG_ACT = (*(f"{s}{g}" for g in range(NI) for s in ("cos", "sin")), "csT", "silu")
TRIG_PE = (*(f"{s}{g}" for g in range(NI) for s in ("mmcos", "mmsin")), "proj")
TRIG_POOL = ("h2",)


def value(steps, name, chunk):
    return chunk * len(steps) + steps.index(name) + 1


def need(engine, sem, steps, name, chunk):
    v = value(steps, name, chunk)
    if not isinstance(v, int) or v > 0:
        engine.wait_ge(sem, v)


def vit_tower(nc, x, cls_tok, tok_W, tok_b, tok_cls, tok_pos, W_phi, b_phi, W_e, b_e, W_g, g_bias, W_psi, b_psi,
              W_h, h_bias, ffn_W, ffn_B, ffn_cos, ffn_sin, pcos, psin, Wq3, bq3, Wk3, bk3, Wv3, bv3, gamma3, beta3,
              ln_g, ln_b, Wq4, bq4, Wk4, bk4, Wv4, bv4, Wo4, bo4, gate_W, gate_b, W1, b1, W2, b2, out):
    with ExitStack() as ctx:
        def sb(name, shape, dt=F32):
            return ctx.enter_context(nc.sbuf_tensor(name, shape, dt))

        def sem(name):
            return ctx.enter_context(nc.semaphore(name))

        ident = sb("ident", [128, 128])
        ones = sb("ones", [128, 128])
        block_mask = sb("block_mask", [128, 128])
        maskA = sb("maskA", [QA, QA])
        maskB = sb("maskB", [QB, N])
        rank = sb("rank", [TT, E])
        sum_sel = sb("sum_sel", [128, 128])
        neg_sel = sb("neg_sel", [128, 2, QA])
        patch_w = sb("patch_w", [128, PS, D])
        addend = sb("addend", [128, N])
        zg_w = sb("zg_w", [D, 256])
        zg_b = sb("zg_b", [128, 256])
        bd_we = sb("bd_we", [128, 128])
        be_col = sb("be_col", [128, 1])
        psi_w = sb("psi_w", [D, 128])
        psi_b = sb("psi_b", [128, 1])
        wh = sb("wh", [128, D])
        hbias_row = sb("hbias_row", [128, D])
        lut_s = sb("lut_s", [D, NW])
        lut_b = sb("lut_b", [D, NW])
        trig_w = sb("trig_w", [D, NW * 64 + 64])
        proj_w = sb("proj_w", [128, D])
        wqq = sb("wqq", [D, 2, DA])
        wkk = sb("wkk", [D, 2, DA])
        bqq = sb("bqq", [128, 1])
        bkk = sb("bkk", [128, 1])
        wv3 = sb("wv3", [D, D])
        bv3c = sb("bv3c", [D, 1])
        gamma_row = sb("gamma_row", [128, D])
        beta_row = sb("beta_row", [128, D])
        wq4 = sb("wq4", [D, 2, NJ, 32])
        wk4 = sb("wk4", [D, 2, NJ, 32])
        bq4c = sb("bq4c", [128, 2])
        bk4c = sb("bk4c", [128, 2])
        wv4 = sb("wv4", [D, D])
        wo4 = sb("wo4", [128, 2, D])
        bo_row = sb("bo_row", [128, D])
        g5_row = sb("g5_row", [128, D])
        b5_row = sb("b5_row", [128, D])
        gate_w = sb("gate_w", [D, E])
        gate_row = sb("gate_row", [128, E])
        w1 = sb("w1", [D, E, FF])
        b1c = sb("b1c", [128, E, FC])
        w2 = sb("w2", [128, E, FC, D])
        b2s = sb("b2s", [E, D])

        patches = sb("patches", [128, PW, IW])
        h0T = sb("h0T", [D, IMGS, N])
        h0_tok = sb("h0_tok", [TT, NT, D])
        hb_tok = h0_tok
        x1_tok = sb("x1_tok", [TT, NT, D])
        x1T = h0T[:, :, :].rearrange("d i n -> d (i n)")
        zg = sb("zg", [QA, 2, IMGS, 256])
        wnew = sb("wnew", [128, IMGS, 128])
        bnew = sb("bnew", [128, IMGS])
        pT = sb("pT", [128, T])
        qT = x1T
        h1_tok = sb("h1_tok", [TT, NT, D])
        h1_hold = sb("h1_hold", [TT, NT, D])
        x2T = sb("x2T", [D, T])
        kbuf = sb("kbuf", [D, 2, 2, NJ, T], I16)
        trig = sb("trig", [D, 2, NJ, T])
        csT = trig[:, 0, 0]
        h2_tok = sb("h2_tok", [TT, NT, D])
        silu_tok = h2_tok
        x3_tok = sb("x3_tok", [TT, NT, D])
        x4_tok = x3_tok
        hid = sb("hid", [128, 2, FC, T])
        hidf = hid[:, :, :, :].rearrange("p a f k -> p (a f k)")
        q3T, k3T, oT, pTa = (hidf[0:n, T * i:T * i + T] for i, n in enumerate((128, 128, D, QA)))
        pTb = hidf[0:QB, 4 * T:4 * T + IMGS * QB]
        v3 = hidf[0:QA, 5 * T:5 * T + 2 * IMGS * D].rearrange("p (a i d) -> p a i d", a=2, i=IMGS)
        q4T, k4T, o4T, r4T = (hidf[:, 2 * T * i:2 * T * i + 2 * T].rearrange("p (g k) -> p g k", g=2) for i in range(4))
        on4T = r4T
        p4 = sb("p4", [QA, 2, NJ, 2 * N])
        e3, s3 = (p4[:, i].rearrange("p j (g k) -> p (j g) k", g=2).rearrange("p (a i) k -> p a i k", a=2)
                  for i in range(2))
        xT = sb("xT", [D, T])
        m3 = sb("m3", [QA, 2 * IMGS])
        sum3 = sb("sum3", [QA, 2 * IMGS])
        rec3 = sb("rec3", [QA, 2 * IMGS])
        y_tok = sb("y_tok", [TT, NT, D])
        z_tok = y_tok
        hb3_tok = sb("hb3_tok", [TT, NT, D])
        x4b_tok = hb3_tok
        h3_tok = sb("h3_tok", [TT, NT, D])
        acc = h3_tok
        v4 = sb("v4", [QA, 2, IMGS, H, 32])
        m4 = sb("m4", [QA, 2 * IMGS, 128])
        mT = sb("mT", [128, T])
        gl = sb("gl", [TT, NT, E])
        ge = sb("ge", [TT, NT, E])
        gt = sb("gt", [TT, NT, E])
        gs = sb("gs", [TT, 6, NT])
        coef = sb("coef", [TT, NT, E])
        coefT = sb("coefT", [E, T])
        bn = {k: sb(f"bn_{k}", [TT, NT, 6]) for k in ("1", "2", "3", "y", "4", "5")}
        mv = {k: sb(f"mv_{k}", [TT, NT, 2]) for k in bn}
        ve = {k: sb(f"ve_{k}", [TT, NT]) for k in bn}
        rstd = {k: sb(f"rstd_{k}", [TT, NT]) for k in bn}
        minus_half = sb("minus_half", [TT, NT])

        tokw_in = hidf[:, 0:C * PS * PS]
        trigf = trig[:, :, :, :].rearrange("p a j k -> p (a j k)")
        su = [trigf[:, 128 * i:128 * i + 128] for i in range(8)]
        lutW = trigf[0:NW, 1024:1024 + 4 * D].rearrange("n (a d) -> n a d", a=4)
        wt = trigf[:, 1536:1536 + C * PS * PS].rearrange("d (b c a) -> d b c a", b=PS, c=C)
        su_col = sb("su_col", [128, 8])

        psum = ctx.enter_context(nc.psum_tensor("psum", [128, 8, 512], F32))
        acc_ps = psum[:, 0:2, :]
        fr = psum[:, 2:4, :]
        bk = psum[:, 4:8, :]
        fr_tok = fr[0:TT].rearrange("p a b -> p (a b)")[:, 0:NT * D]
        fr_flat = fr.rearrange("p a b -> p (a b)")
        bk_flat = bk.rearrange("p a b -> p (a b)")
        acc_flat = acc_ps.rearrange("p a b -> p (a b)")

        loaded_w = sem("weights_loaded")
        copied_w = sem("patch_weights_copied")
        su_pool = sem("setup_pool")
        su_dve = sem("setup_dve")
        su_pe = sem("setup_pe")
        su_act = sem("setup_act")
        x_loaded = [sem(f"pair{p}_loaded") for p in range(2)]
        f_pe, f_act, f_dve, f_pool = sem("front_pe"), sem("front_act"), sem("front_dve"), sem("front_pool")
        t_pe, t_act, t_dve, t_pool = sem("trig_pe"), sem("trig_act"), sem("trig_dve"), sem("trig_pool")
        b_pe, b_act, b_dve, b_pool = sem("back_pe"), sem("back_act"), sem("back_dve"), sem("back_pool")
        stored = sem("stored")

        def row(ap, n=128):
            return ap.unsqueeze(0).to_broadcast([n, *ap.shape])

        W_all = W_g.rearrange("h e w -> (h e) w")
        loads = [
            (tokw_in, tok_W), (addend[:, 2:N], row(tok_pos[0, 1:NPATCH + 1, 0])),
            (su_col[:, 0:1], tok_b.unsqueeze(1)), (su_col[:, 1:2], cls_tok[0, 0].unsqueeze(1)),
            (su_col[:, 2:3], tok_cls[0, 0].unsqueeze(1)), (su_col[:, 3:4], row(tok_pos[0, 0, :])),
            (zg_w[:, 0:128].rearrange("w (h d) -> w h d", h=H), W_phi.rearrange("h w d -> w h d")),
            (zg_b[:, 0:128], row(b_phi.rearrange("h d -> (h d)"))),
            (su_col[:, 4:5], b_phi.rearrange("h d -> (h d)").unsqueeze(1)),
            (be_col[:, :], b_e.rearrange("h d -> (h d)").unsqueeze(1)),
            (su_col[:, 5:6], g_bias[0].unsqueeze(1)),
            (su[0][:, :], W_all),
            (psi_w[:, :].rearrange("w (h d) -> w h d", h=H), W_psi.rearrange("h w d -> w h d")),
            (psi_b[:, :], b_psi.rearrange("h d -> (h d)").unsqueeze(1)),
            (wh[:, :], W_h.rearrange("h e w -> (h e) w")), (hbias_row[:, :], row(h_bias[0])),
            (lutW[:, 0], ffn_W), (lutW[:, 1], ffn_B), (lutW[:, 2], ffn_cos), (lutW[:, 3], ffn_sin),
            (su[1][:, :].rearrange("d (j c i) -> d j c i", j=NJ, c=2)[:, :, 0], pcos.rearrange("d (j i) -> d j i", j=NJ)),
            (su[1][:, :].rearrange("d (j c i) -> d j c i", j=NJ, c=2)[:, :, 1], psin.rearrange("d (j i) -> d j i", j=NJ)),
            (wqq[:, 0], Wq3), (wqq[:, 1], Wq3), (wkk[:, 0], Wk3), (wkk[:, 1], Wk3),
            (bqq[0:DA, :], bq3.unsqueeze(1)), (bqq[DA:, :], bq3.unsqueeze(1)),
            (bkk[0:DA, :], bk3.unsqueeze(1)), (bkk[DA:, :], bk3.unsqueeze(1)),
            (wv3[:, :], Wv3), (bv3c[:, :], bv3.unsqueeze(1)), (gamma_row[:, :], row(gamma3)),
            (beta_row[:, :], row(beta3)), (wv4[:, :], Wv4), (su[2][:, :], Wo4), (su_col[:, 6:7], bv4.unsqueeze(1)),
            (bo_row[:, :], row(bo4)), (g5_row[:, :], row(ln_g)), (b5_row[:, :], row(ln_b)),
            (gate_w[:, :], gate_W), (gate_row[:, :], row(gate_b)), (w1[:, :, :], W1.rearrange("e d f -> d e f")),
            (b1c[:, :, :], b1.rearrange("e (k p) -> p e k", p=128)),
            (w2[:, :, :, :], W2.rearrange("e (k p) d -> p e k d", p=128)), (b2s[:, :], b2),
        ]
        padded = []
        for h in range(H):
            g, j = h // NJ, h % NJ
            padded += [
                (bd_we[HD * h:HD * h + HD, HD * h:HD * h + HD], W_e[h]),
                (wo4[32 * j:32 * j + HD, g, :], Wo4[HD * h:HD * h + HD, :]),
                (bq4c[32 * j:32 * j + HD, g:g + 1], bq4[HD * h:HD * h + HD].unsqueeze(1)),
                (bk4c[32 * j:32 * j + HD, g:g + 1], bk4[HD * h:HD * h + HD].unsqueeze(1)),
            ]
        for g in range(2):
            padded += [
                (wq4[:, g, :, 0:HD], Wq4[:, 64 * g:64 * g + 64].rearrange("d (j i) -> d j i", j=NJ)),
                (wk4[:, g, :, 0:HD], Wk4[:, 64 * g:64 * g + 64].rearrange("d (j i) -> d j i", j=NJ)),
            ]
        LOADED = 16 * (len(loads) + len(padded))
        ZEROED = 7
        out_c = out.rearrange("b n d -> (b n) d").rearrange("(c t p) d -> c p t d", t=NT, p=TT)

        dve_waited, pool_waited = sem("dve_waited"), sem("pool_waited")

        def take_waits(engine, waited):
            engine.sem_inc(waited, 1)

        block = ctx.enter_context(nc.Block())

        @block.sync
        def _(sp):
            def load_pair(p, c):
                if p:
                    need(sp, f_pe, FRONT_PE, "embed0", c)
                else:
                    need(sp, f_pe, FRONT_PE, "embed1", c - 1)
                for q in range(2):
                    for ch in range(C):
                        sp.dma_start(patches[64 * q + PS * ch:64 * q + PS * ch + PS],
                                     x[IMGS * c + 2 * p + q, ch].rearrange("(w r) k -> r w k", r=PS)
                                     ).then_inc(x_loaded[p], 16)

            def store(c):
                need(sp, b_dve, BACK_DVE, f"acc_{E - 1}", c)
                sp.dma_start(out_c[c], acc[:, :, :]).then_inc(stored, 16)

            load_pair(0, 0)
            with nc.allow_non_contiguous_dma(reason="bias columns, once"):
                for dst, src in loads:
                    sp.dma_start(dst, src).then_inc(loaded_w, 16)
            sp.wait_ge(su_dve, ZEROED)
            for dst, src in padded:
                sp.dma_start(dst, src).then_inc(loaded_w, 16)
            sp.wait_ge(su_act, 1)
            sp.dma_start(patch_w[64:64 + C * PS], patch_w[0:C * PS]).then_inc(copied_w, 16)
            load_pair(1, 0)
            load_pair(0, 1)
            load_pair(1, 1)
            store(0)
            with sp.Fori(1, CHUNKS - 1) as c:
                load_pair(0, c + 1)
                load_pair(1, c + 1)
                store(c)
            store(CHUNKS - 1)
            sp.wait_ge(stored, 16 * CHUNKS)

        @block.gpsimd
        def _(pool):
            nc.gpsimd.memset(ident[:, :], 0.0).then_inc(su_pool, 1)
            nc.gpsimd.memset(block_mask[:, :], 1.0).then_inc(su_pool, 1)
            nc.gpsimd.memset(maskA[:, :], 0.0).then_inc(su_pool, 1)
            nc.gpsimd.memset(maskB[:, :], 0.0).then_inc(su_pool, 1)
            nc.gpsimd.memset(sum_sel[:, :], 0.0).then_inc(su_pool, 1)
            nc.gpsimd.memset(neg_sel[:, :, :], 0.0).then_inc(su_pool, 1)
            for e in range(E):
                nc.gpsimd.memset(rank[:, e:e + 1], float(E - e)).then_inc(su_pool, 1)
            pool.wait_ge(su_pool, 6 + E)
            nc.gpsimd.affine_select(out=ident[:, :], in_=ident[:, :], compare_op=ALU.not_equal, fill=1.0, base=0,
                                    pattern=[[-1, 128]], channel_multiplier=1).then_inc(su_pool, 1)
            bm = block_mask[:, :].rearrange("p (g k) -> p g k", g=H)
            nc.gpsimd.affine_select(out=bm, in_=bm, compare_op=ALU.is_ge, fill=0.0, base=0,
                                    pattern=[[-HD, H], [0, HD]], channel_multiplier=1).then_inc(su_pool, 1)
            pool.wait_ge(su_pool, 8 + E)
            nc.gpsimd.affine_select(out=bm, in_=bm, compare_op=ALU.is_ge, fill=0.0, base=HD - 1,
                                    pattern=[[HD, H], [0, HD]], channel_multiplier=-1).then_inc(su_pool, 1)
            nc.gpsimd.affine_select(out=maskA[:, :], in_=maskA[:, :], compare_op=ALU.is_ge, fill=MASKED, base=0,
                                    pattern=[[-1, QA]], channel_multiplier=1).then_inc(su_pool, 1)
            nc.gpsimd.affine_select(out=maskB[:, :], in_=maskB[:, :], compare_op=ALU.is_ge, fill=MASKED, base=QA,
                                    pattern=[[-1, N]], channel_multiplier=1).then_inc(su_pool, 1)
            ss = sum_sel[:, :].rearrange("p (j k) -> p j k", j=NJ)
            nc.gpsimd.affine_select(out=ss, in_=ss, compare_op=ALU.not_equal, fill=1.0, base=-HD,
                                    pattern=[[-32, NJ], [0, 32]], channel_multiplier=1).then_inc(su_pool, 1)
            for g in range(2):
                for j in range(NJ):
                    pool.wait_ge(su_pool, 12 + E + NJ * g + j)
                    nc.gpsimd.affine_select(out=neg_sel[:, g], in_=neg_sel[:, g], compare_op=ALU.not_equal,
                                            fill=-1.0, base=-32 * j - g, pattern=[[0, QA]],
                                            channel_multiplier=1).then_inc(su_pool, 1)

            def ln(sem_in, steps_in, name, eps, c, sem_out, steps_out):
                need(pool, sem_in, steps_in, "ln" + name, c)
                take_waits(pool, pool_waited)
                nc.gpsimd.tensor_scalar(ve[name][:, :], mv[name][:, :, 1], EPS, 1.0, ALU.add,
                                        ALU.mult).then_inc(sem_out, 1)
                need(pool, sem_out, steps_out, "eps" + name, c)
                nc.gpsimd.tensor_tensor(rstd[name][:, :], ve[name][:, :], minus_half[:, :],
                                        ALU.pow).then_inc(sem_out, 1)

            def front(c):
                ln(f_dve, FRONT_DVE, "1", EPS, c, f_pool, FRONT_POOL)
                need(pool, f_act, FRONT_ACT, "h0", c)
                need(pool, f_dve, FRONT_DVE, "x1", c)
                nc.gpsimd.tensor_tensor(hb_tok[:, :, :], h0_tok[:, :, :],
                                        hbias_row[0:TT].unsqueeze(1).to_broadcast([TT, NT, D]),
                                        ALU.add).then_inc(f_pool, 1)
                ln(f_dve, FRONT_DVE, "2", EPS, c, f_pool, FRONT_POOL)
                need(pool, f_dve, FRONT_DVE, "h1", c)
                need(pool, t_pool, TRIG_POOL, "h2", c - 1)
                take_waits(pool, pool_waited)
                nc.gpsimd.tensor_copy(h1_hold[:, :, :], h1_tok[:, :, :]).then_inc(f_pool, 1)

            def trig_end(c):
                need(pool, t_act, TRIG_ACT, "silu", c)
                need(pool, f_pool, FRONT_POOL, "h1hold", c)
                nc.gpsimd.tensor_tensor(h2_tok[:, :, :], h1_hold[:, :, :], silu_tok[:, :, :],
                                        ALU.add).then_inc(t_pool, 1)

            def back(c):
                need(pool, b_pe, BACK_PE, f"pv_{IMGS - 1}", c - 1)
                take_waits(pool, pool_waited)
                nc.gpsimd.memset(s3[:, :, :, :], MASKED).then_inc(b_pool, 1)
                ln(b_dve, BACK_DVE, "3", EPS, c, b_pool, BACK_POOL)
                need(pool, b_dve, BACK_DVE, "y4", c - 1)
                need(pool, t_pool, TRIG_POOL, "h2", c)
                nc.gpsimd.tensor_tensor(hb3_tok[:, :, :], h2_tok[:, :, :],
                                        beta_row[0:TT].unsqueeze(1).to_broadcast([TT, NT, D]),
                                        ALU.add).then_inc(b_pool, 1)
                ln(b_dve, BACK_DVE, "y", EPS, c, b_pool, BACK_POOL)
                ln(b_dve, BACK_DVE, "4", EPS, c, b_pool, BACK_POOL)
                need(pool, b_dve, BACK_DVE, "x4", c)
                need(pool, b_dve, BACK_DVE, "h3", c)
                nc.gpsimd.tensor_tensor(x4b_tok[:, :, :], x4_tok[:, :, :],
                                        bo_row[0:TT].unsqueeze(1).to_broadcast([TT, NT, D]),
                                        ALU.add).then_inc(b_pool, 1)
                ln(b_dve, BACK_DVE, "5", EPS, c, b_pool, BACK_POOL)

            pool.wait_ge(loaded_w, LOADED)
            pool.wait_ge(su_dve, SU_DVE)

            def chunk(c):
                front(c)
                trig_end(c)
                back(c)

            chunk(0)
            with pool.Fori(1, CHUNKS) as c:
                chunk(c)

        @block.vector
        def _(dve):
            v = nc.vector
            v.memset(bd_we[:, :], 0.0).then_inc(su_dve, 1)
            v.memset(wo4[:, :, :], 0.0).then_inc(su_dve, 1)
            v.memset(bq4c[:, :], 0.0).then_inc(su_dve, 1)
            v.memset(bk4c[:, :], 0.0).then_inc(su_dve, 1)
            v.memset(wq4[:, :, :, :], 0.0).then_inc(su_dve, 1)
            v.memset(wk4[:, :, :, :], 0.0).then_inc(su_dve, 1)
            v.memset(trig_w[:, :], 0.0).then_inc(su_dve, 1)
            v.memset(v4[:, :, :, :, :], 1.0).then_inc(su_dve, 1)
            v.memset(m4[:, :, :], 0.0).then_inc(su_dve, 1)
            v.memset(rec3[:, :], 1.0).then_inc(su_dve, 1)
            v.memset(minus_half[:, :], -0.5).then_inc(su_dve, 1)
            v.memset(ones[:, :], 1.0).then_inc(su_dve, 1)
            dve.wait_ge(loaded_w, LOADED)
            v.tensor_scalar(addend[:, 2:N], addend[:, 2:N], su_col[:, 0:1], None, ALU.add).then_inc(su_dve, 1)
            v.tensor_copy(addend[:, 0:1], su_col[:, 1:2]).then_inc(su_dve, 1)
            v.tensor_tensor(addend[:, 1:2], su_col[:, 2:3], su_col[:, 3:4], ALU.add).then_inc(su_dve, 1)
            v.tensor_copy(wt, tokw_in.rearrange("d (a b c) -> d b c a", a=PS, b=PS)).then_inc(su_dve, 1)
            dve.wait_ge(su_pe, 2)
            v.tensor_copy(su[3][:, :], bk[:, 0, 0:128]).then_inc(su_dve, 1)
            v.tensor_copy(su[4][:, :], bk[:, 0, 128:256]).then_inc(su_dve, 1)
            v.tensor_copy(proj_w[:, :], bk[:, 0, 256:384]).then_inc(su_dve, 1)
            dve.wait_ge(su_pe, 4)
            dve.wait_ge(su_pool, POOL_SETUP)
            v.tensor_tensor(su[5][:, :], bk[:, 1, 0:128], block_mask[:, :], ALU.mult).then_inc(su_dve, 1)
            v.tensor_copy(su[6][:, :], bk[:, 1, 128:256]).then_inc(su_dve, 1)
            v.tensor_tensor(su_col[:, 7:8], bk[:, 1, 256:257], be_col[:, :], ALU.add).then_inc(su_dve, 1)
            dve.wait_ge(su_dve, 22)
            v.tensor_scalar(su[7][:, :], ones[:, :], su_col[:, 7:8], None, ALU.mult).then_inc(su_dve, 1)
            v.tensor_scalar(su[1][:, :], ones[:, :], su_col[:, 5:6], None, ALU.mult).then_inc(su_dve, 1)
            v.tensor_scalar(su[0][:, :], ones[:, :], su_col[:, 6:7], None, ALU.mult).then_inc(su_dve, 1)
            dve.wait_ge(su_pe, 7)
            v.tensor_tensor(su[4][:, :], su[3][:, :], bk[:, 2, 0:128], ALU.subtract).then_inc(su_dve, 1)
            v.tensor_scalar(zg_b[:, 128:256], bk[:, 2, 128:256], -LR_SCALE, None, ALU.mult).then_inc(su_dve, 1)
            v.tensor_tensor(bo_row[:, :], bo_row[:, :], bk[:, 2, 256:384], ALU.add).then_inc(su_dve, 1)
            dve.wait_ge(su_dve, 28)
            v.tensor_scalar(zg_w[:, 128:256], su[4][:, :], LR_SCALE, None, ALU.mult).then_inc(su_dve, 1)
            dve.wait_ge(su_pe, 8)
            lw = bk[:, 3, 0:4 * NW].rearrange("p (a n) -> p a n", a=4)
            v.tensor_scalar(lut_s[:, :], lw[:, 0], -1.0, None, ALU.mult).then_inc(su_dve, 1)
            dve.wait_ge(su_dve, 30)
            v.tensor_tensor(lut_s[:, :], lw[:, 0], lut_s[:, :], ALU.max).then_inc(su_dve, 1)
            dve.wait_ge(su_dve, 31)
            v.tensor_scalar(lut_s[:, :], lut_s[:, :], 1.0, None, ALU.add).then_inc(su_dve, 1)
            dve.wait_ge(su_dve, 32)
            v.reciprocal(lut_s[:, :], lut_s[:, :]).then_inc(su_dve, 1)
            dve.wait_ge(su_dve, 33)
            v.tensor_scalar(lut_s[:, :], lut_s[:, :], TO_LUT, None, ALU.mult).then_inc(su_dve, 1)
            v.tensor_scalar(su[2][:, 0:NW], lw[:, 1], TO_LUT, None, ALU.mult).then_inc(su_dve, 1)
            dve.wait_ge(su_dve, 35)
            v.tensor_scalar(lut_b[:, :], su[2][:, 0:NW], 1.0 / LUT, MAGIC, ALU.mult, ALU.add).then_inc(su_dve, 1)
            dve.wait_ge(su_dve, 36)
            v.tensor_scalar(lut_b[:, :], lut_b[:, :], MAGIC, -float(LUT), ALU.subtract, ALU.mult).then_inc(su_dve, 1)
            dve.wait_ge(su_dve, 37)
            v.tensor_tensor(lut_b[:, :], lut_b[:, :], su[2][:, 0:NW], ALU.add).then_inc(su_dve, 1)
            for cs in range(2):
                for j in range(NJ):
                    at = j * NI * 64 + cs * 48
                    v.tensor_scalar(trig_w[:, at:at + 65 * (NI - 1) + 1:65], lw[:, 2 + cs, NI * j:NI * j + NI], -1.0,
                                    None, ALU.mult).then_inc(su_dve, 1)

            def ln(src, name, c, sem_d, steps, sem_p, steps_p, dst):
                for t in range(NT):
                    i = v.bn_stats(bn[name][:, t], src[:, t])
                i.then_inc(sem_d, 1)
                need(dve, sem_d, steps, "bn" + name, c)
                take_waits(dve, dve_waited)
                for t in range(NT):
                    i = v.bn_aggr(mv[name][:, t], bn[name][:, t])
                i.then_inc(sem_d, 1)
                if dst is None:
                    return
                need(dve, sem_d, steps, "ln" + name, c)
                need(dve, sem_p, steps_p, "rstd" + name, c)
                for t in range(NT):
                    i = v.tensor_scalar(dst[:, t], src[:, t], mv[name][:, t, 0:1], rstd[name][:, t:t + 1],
                                        ALU.subtract, ALU.mult)
                i.then_inc(sem_d, 1)

            def front(c):
                need(dve, f_pe, FRONT_PE, "embed1", c)
                need(dve, f_pe, FRONT_PE, "attn", c - 1)
                v.tensor_copy(h0T[:, :, 0:2], addend[:, 0:2].unsqueeze(1).to_broadcast([D, IMGS, 2])).then_inc(f_dve, 1)
                for q in range(2):
                    v.tensor_tensor(h0T[:, :, :].rearrange("d (p q) n -> d p q n", q=2)[:, :, q, 2:N],
                                    fr[:, q, 0:2 * NPATCH].rearrange("d (p n) -> d p n", p=2),
                                    addend[:, 2:N].unsqueeze(1).to_broadcast([D, 2, NPATCH]),
                                    ALU.add).then_inc(f_dve, 1)
                need(dve, f_act, FRONT_ACT, "h0", c)
                ln(h0_tok, "1", c, f_dve, FRONT_DVE, f_pool, FRONT_POOL, x1_tok)
                for r in range(2):
                    need(dve, f_pe, FRONT_PE, f"zg{r}", c)
                    for t, (_, n) in enumerate(QS):
                        v.tensor_tensor(zg[0:n, t, 2 * r:2 * r + 2], fr[0:n, :, 256 * t:256 * t + 256],
                                        zg_b[0:n].unsqueeze(1).to_broadcast([n, 2, 256]), ALU.add).then_inc(f_dve, 1)
                need(dve, f_pe, FRONT_PE, "cross", c)
                v.tensor_tensor(wnew[:, :, :], fr[:, 0, :].rearrange("p (i k) -> p i k", i=IMGS),
                                block_mask[:, :].unsqueeze(1).to_broadcast([128, IMGS, 128]), ALU.mult).then_inc(f_dve, 1)
                need(dve, f_dve, FRONT_DVE, "masked", c)
                v.tensor_tensor(wnew[:, :, :], wnew[:, :, :],
                                bd_we[:, :].unsqueeze(1).to_broadcast([128, IMGS, 128]), ALU.add).then_inc(f_dve, 1)
                v.tensor_scalar(bnew[:, :], fr[:, 1, 0:IMGS], be_col[:, 0:1], None, ALU.add).then_inc(f_dve, 1)
                need(dve, f_pe, FRONT_PE, "attn", c)
                need(dve, f_pool, FRONT_POOL, "hb", c)
                need(dve, f_pool, FRONT_POOL, "h1hold", c - 1)
                v.tensor_tensor(h1_tok[:, :, :].rearrange("p t d -> p (t d)"), fr_tok,
                                hb_tok[:, :, :].rearrange("p t d -> p (t d)"), ALU.add).then_inc(f_dve, 1)
                need(dve, f_dve, FRONT_DVE, "h1", c)
                ln(h1_tok, "2", c, f_dve, FRONT_DVE, f_pool, FRONT_POOL, x1_tok)

            def trig_group(c, g):
                b = g % 2
                if g == 0:
                    need(dve, f_act, FRONT_ACT, "x2Tb", c)
                if g >= 2:
                    need(dve, t_act, TRIG_ACT, f"sin{g - 2}", c)
                else:
                    need(dve, t_act, TRIG_ACT, f"sin{NI - 2 + g}", c - 1)
                for j in range(NJ):
                    n = NI * j + g
                    i = v.tensor_scalar(kbuf[:, b, 1, j], x2T[:, :], lut_s[:, n:n + 1], lut_b[:, n:n + 1],
                                        ALU.mult, ALU.add)
                i.then_inc(t_dve, 1)
                need(dve, t_dve, TRIG_DVE, f"k{g}", c)
                v.tensor_scalar(kbuf[:, b, 0], kbuf[:, b, 1], float(LUT // 4), None, ALU.add).then_inc(t_dve, 1)
                need(dve, t_dve, TRIG_DVE, f"add{g}", c)
                v.tensor_scalar(kbuf[:, b], kbuf[:, b], LUT - 1, None, ALU.bitwise_and).then_inc(t_dve, 1)

            def back(c):
                need(dve, t_pool, TRIG_POOL, "h2", c)
                need(dve, b_pool, BACK_POOL, "x4b", c - 1)
                ln(h2_tok, "3", c, b_dve, BACK_DVE, b_pool, BACK_POOL, x3_tok)
                need(dve, b_pool, BACK_POOL, "s3", c)
                need(dve, b_pe, BACK_PE, "s3", c)
                v.tensor_tensor(s3[:, 0, :, 0:QA], bk[0:QA, 0, 0:IMGS * QA].rearrange("p (i k) -> p i k", i=IMGS),
                                maskA[:, :].unsqueeze(1).to_broadcast([QA, IMGS, QA]), ALU.add).then_inc(b_dve, 1)
                v.tensor_tensor(s3[0:QB, 1].rearrange("p (a i) k -> p a i k", a=2),
                                bk[0:QB, 1:3, 0:HALF].rearrange("p a (i k) -> p a i k", i=2),
                                maskB[:, :].unsqueeze(1).unsqueeze(1).to_broadcast([QB, 2, 2, N]),
                                ALU.add).then_inc(b_dve, 1)
                need(dve, b_dve, BACK_DVE, "mask3b", c)
                s3v = s3.rearrange("p a i k -> p (a i) k")
                e3v = e3.rearrange("p a i k -> p (a i) k")
                v.tensor_reduce(m3[:, :], s3v, AX, ALU.max).then_inc(b_dve, 1)
                need(dve, b_dve, BACK_DVE, "max3", c)
                v.tensor_tensor(e3v, s3v, m3[:, :].unsqueeze(2).to_broadcast([QA, 2 * IMGS, N]),
                                ALU.subtract).then_inc(b_dve, 1)
                need(dve, b_act, BACK_ACT, "e3", c)
                v.tensor_reduce(sum3[:, :], e3v, AX, ALU.add).then_inc(b_dve, 1)
                need(dve, b_dve, BACK_DVE, "sum3", c)
                v.reciprocal(rec3[:, :], sum3[:, :]).then_inc(b_dve, 1)
                need(dve, b_dve, BACK_DVE, "rec3", c)
                v.tensor_tensor(e3v, e3v, rec3[:, :].unsqueeze(2).to_broadcast([QA, 2 * IMGS, N]),
                                ALU.mult).then_inc(b_dve, 1)
                need(dve, b_pe, BACK_PE, "o3", c)
                v.tensor_tensor(y_tok[:, :, :].rearrange("p t d -> p (t d)"), bk_flat[0:TT, 512:512 + NT * D],
                                x3_tok[:, :, :].rearrange("p t d -> p (t d)"), ALU.add).then_inc(b_dve, 1)
                need(dve, b_dve, BACK_DVE, "y3", c)
                ln(y_tok, "y", c, b_dve, BACK_DVE, b_pool, BACK_POOL, None)
                need(dve, b_dve, BACK_DVE, "lny", c)
                for t in range(NT):
                    i = v.scalar_tensor_tensor(out=z_tok[:, t], in0=y_tok[:, t], scalar=mv["y"][:, t, 0:1],
                                               in1=gamma_row[0:TT], op0=ALU.subtract, op1=ALU.mult)
                i.then_inc(b_dve, 1)
                need(dve, b_dve, BACK_DVE, "zy", c)
                need(dve, b_pool, BACK_POOL, "rstdy", c)
                need_stored(dve, c)
                for t in range(NT):
                    i = v.scalar_tensor_tensor(out=h3_tok[:, t], in0=z_tok[:, t], scalar=rstd["y"][:, t:t + 1],
                                               in1=hb3_tok[:, t], op0=ALU.mult, op1=ALU.add)
                i.then_inc(b_dve, 1)
                need(dve, b_dve, BACK_DVE, "h3", c)
                ln(h3_tok, "4", c, b_dve, BACK_DVE, b_pool, BACK_POOL, x4_tok)
                for r in range(2 * IMGS):
                    n = QS[r % 2][1]
                    need(dve, b_pe, BACK_PE, f"s4_{r}", c)
                    v.tensor_reduce(m4[0:n, r, :].rearrange("p (j g) -> p j g", j=NJ)[:, :, 0:2],
                                    bk[0:n, :, 0:2 * N].rearrange("p j (g k) -> p j g k", g=2), AX,
                                    ALU.max).then_inc(b_dve, 1)
                need(dve, b_pe, BACK_PE, "sums", c)
                v.reciprocal(r4T.rearrange("p g (a k) -> p (g a) k", a=2), bk[:, :, 0:HALF]).then_inc(b_dve, 1)
                need(dve, b_dve, BACK_DVE, "rsum", c)
                v.tensor_tensor(on4T.rearrange("p g k -> p (g k)"), o4T.rearrange("p g k -> p (g k)"),
                                r4T.rearrange("p g k -> p (g k)"), ALU.mult).then_inc(b_dve, 1)
                need(dve, b_pe, BACK_PE, "wo", c)
                need(dve, b_pool, BACK_POOL, "x4b", c)
                v.tensor_tensor(y_tok[:, :, :].rearrange("p t d -> p (t d)"), bk_flat[0:TT, 0:NT * D],
                                x4b_tok[:, :, :].rearrange("p t d -> p (t d)"), ALU.add).then_inc(b_dve, 1)
                need(dve, b_dve, BACK_DVE, "y4", c)
                ln(y_tok, "5", c, b_dve, BACK_DVE, b_pool, BACK_POOL, None)
                need(dve, b_dve, BACK_DVE, "ln5", c)
                for t in range(NT):
                    i = v.scalar_tensor_tensor(out=z_tok[:, t], in0=y_tok[:, t], scalar=mv["5"][:, t, 0:1],
                                               in1=g5_row[0:TT], op0=ALU.subtract, op1=ALU.mult)
                i.then_inc(b_dve, 1)
                need(dve, b_dve, BACK_DVE, "z5", c)
                need(dve, b_pool, BACK_POOL, "rstd5", c)
                for t in range(NT):
                    i = v.scalar_tensor_tensor(out=z_tok[:, t], in0=z_tok[:, t], scalar=rstd["5"][:, t:t + 1],
                                               in1=b5_row[0:TT], op0=ALU.mult, op1=ALU.add)
                i.then_inc(b_dve, 1)
                gmax, gsum, gemax, grec, gsmax, gw = (gs[:, i] for i in range(6))

                def over(a):
                    return a.unsqueeze(2).to_broadcast([TT, NT, E])
                need(dve, b_pe, BACK_PE, "gate", c)
                v.tensor_tensor(gl[:, :, :], bk[0:TT, 2, 0:NT * E].rearrange("p (t e) -> p t e", t=NT),
                                gate_row[0:TT].unsqueeze(1).to_broadcast([TT, NT, E]), ALU.add).then_inc(b_dve, 1)
                need(dve, b_dve, BACK_DVE, "glog", c)
                v.tensor_reduce(gmax, gl[:, :, :], AX, ALU.max).then_inc(b_dve, 1)
                need(dve, b_dve, BACK_DVE, "gmax", c)
                v.tensor_tensor(gl[:, :, :], gl[:, :, :], over(gmax), ALU.subtract).then_inc(b_dve, 1)
                need(dve, b_act, BACK_ACT, "gexp", c)
                v.tensor_reduce(gsum, ge[:, :, :], AX, ALU.add).then_inc(b_dve, 1)
                v.tensor_reduce(gemax, ge[:, :, :], AX, ALU.max).then_inc(b_dve, 1)
                need(dve, b_dve, BACK_DVE, "gemax", c)
                v.reciprocal(grec, gsum).then_inc(b_dve, 1)
                v.tensor_tensor(gt[:, :, :], ge[:, :, :], over(gemax), ALU.is_equal).then_inc(b_dve, 1)
                need(dve, b_dve, BACK_DVE, "gmask", c)
                v.tensor_tensor(gt[:, :, :], gt[:, :, :], rank[:, :].unsqueeze(1).to_broadcast([TT, NT, E]),
                                ALU.mult).then_inc(b_dve, 1)
                need(dve, b_dve, BACK_DVE, "gscore", c)
                v.tensor_reduce(gsmax, gt[:, :, :], AX, ALU.max).then_inc(b_dve, 1)
                need(dve, b_dve, BACK_DVE, "gsmax", c)
                v.tensor_tensor(gt[:, :, :], gt[:, :, :], over(gsmax), ALU.is_equal).then_inc(b_dve, 1)
                v.tensor_tensor(gw, gemax, grec, ALU.mult).then_inc(b_dve, 1)
                need(dve, b_dve, BACK_DVE, "gw", c)
                v.tensor_tensor(coef[:, :, :], gt[:, :, :], over(gw), ALU.mult).then_inc(b_dve, 1)
                need(dve, b_pe, BACK_PE, "b2", c)
                v.tensor_tensor(acc[:, :, :].rearrange("p t d -> p (t d)"), bk_flat[0:TT, 1024:1024 + NT * D],
                                h3_tok[:, :, :].rearrange("p t d -> p (t d)"), ALU.add).then_inc(b_dve, 1)
                for e in range(E):
                    need(dve, b_dve, BACK_DVE, f"acc_{e - 1}" if e else "acc0", c)
                    need(dve, b_pe, BACK_PE, f"out_{e}", c)
                    for t in range(NT):
                        i = v.scalar_tensor_tensor(out=acc[:, t], in0=bk_flat[0:TT, 1024 + D * t:1024 + D * t + D],
                                                   scalar=coef[:, t, e:e + 1], in1=acc[:, t], op0=ALU.mult, op1=ALU.add)
                    i.then_inc(b_dve, 1)

            def need_stored(eng, c):
                if not isinstance(c, int) or c > 0:
                    eng.wait_ge(stored, 16 * c)

            dve.wait_ge(su_dve, SU_DVE)

            def chunk(c):
                front(c)
                for g in range(NI):
                    trig_group(c, g)
                back(c)

            chunk(0)
            with dve.Fori(1, CHUNKS) as c:
                chunk(c)

        @block.scalar
        def _(act):
            a = nc.scalar
            act.wait_ge(su_pe, 1)
            a.activation(patch_w[0:C * PS, :, :].rearrange("p a d -> p (a d)"), bk_flat[0:C * PS, 0:PS * D],
                         ACT.Copy).then_inc(su_act, 1)

            def front(c):
                need(act, f_pe, FRONT_PE, "h0", c)
                need(act, f_dve, FRONT_DVE, "h1", c - 1)
                a.activation(h0_tok[:, :, :].rearrange("p t d -> p (t d)"), fr_tok, ACT.Copy).then_inc(f_act, 1)
                need(act, f_pe, FRONT_PE, "x1T", c)
                evict_T(x1T, fr_flat, f_act)
                need(act, f_pe, FRONT_PE, "pT", c)
                a.activation(pT[:, :].rearrange("p (a k) -> p a k", a=2), fr[:, :, 0:HALF], ACT.Identity,
                             bias=psi_b[:, 0:1]).then_inc(f_act, 1)
                need(act, f_pe, FRONT_PE, "qT", c)
                need(act, f_dve, FRONT_DVE, "bnew", c)
                for i in range(IMGS):
                    a.activation(qT[:, N * i:N * i + N], fr[:, i // 2, N * (i % 2):N * (i % 2) + N], ACT.Identity,
                                 bias=bnew[:, i:i + 1]).then_inc(f_act, 1)
                need(act, f_pe, FRONT_PE, "x2T", c)
                need(act, t_dve, TRIG_DVE, f"k{NI - 1}", c - 1)
                evict_T(x2T, fr_flat, f_act)

            def evict_T(dst, flat, s):
                a.activation(dst[:, 0:4 * TT], flat[:, 0:4 * TT], ACT.Copy).then_inc(s, 1)
                a.activation(dst[:, 4 * TT:T], flat[:, 512:512 + TT], ACT.Copy).then_inc(s, 1)

            def trig_group(c, g):
                b = g % 2
                need(act, t_dve, TRIG_DVE, f"and{g}", c)
                for cs, s in enumerate(("mmcos", "mmsin")):
                    if g:
                        need(act, t_pe, TRIG_PE, f"{s}{g - 1}", c)
                    else:
                        need(act, t_pe, TRIG_PE, f"{s}{NI - 1}", c - 1)
                    a.activation(trig[:, cs], kbuf[:, b, cs], ACT.Sin, bias=MINUS_PI, scale=FROM_LUT).then_inc(t_act, 1)

            def trig_end(c):
                need(act, t_pe, TRIG_PE, f"mmsin{NI - 1}", c)
                a.activation(csT[:, :].rearrange("p (a k) -> p a k", a=2), acc_ps[:, :, 0:HALF],
                             ACT.Copy).then_inc(t_act, 1)
                need(act, t_pe, TRIG_PE, "proj", c)
                need(act, b_pool, BACK_POOL, "hb3", c - 1)
                need(act, b_dve, BACK_DVE, "x3", c - 1)
                a.activation(silu_tok[:, :, :].rearrange("p t d -> p (t d)"), acc_flat[0:TT, 0:NT * D],
                             ACT.Silu).then_inc(t_act, 1)

            def back(c):
                need(act, b_pe, BACK_PE, "x3T", c)
                need(act, b_pe, BACK_PE, f"hid7_{E - 1}", c - 1)
                evict_T(xT, bk_flat, b_act)
                need(act, b_pe, BACK_PE, "q3", c)
                a.activation(q3T[:, :].rearrange("p (a k) -> p a k", a=2), bk[:, 0:2, 0:HALF], ACT.Identity,
                             bias=bqq[:, 0:1]).then_inc(b_act, 1)
                need(act, b_pe, BACK_PE, "k3", c)
                a.activation(k3T[:, :].rearrange("p (a k) -> p a k", a=2), bk[:, 2:4, 0:HALF], ACT.Identity,
                             bias=bkk[:, 0:1]).then_inc(b_act, 1)
                need(act, b_pe, BACK_PE, "v3a", c)
                a.activation(v3[:, 0].rearrange("p i d -> p (i d)"), bk[0:QA, 3, :], ACT.Copy).then_inc(b_act, 1)
                need(act, b_pe, BACK_PE, "v3b", c)
                a.activation(v3[0:QB, 1].rearrange("p i d -> p (i d)"), bk[0:QB, 3, :], ACT.Copy).then_inc(b_act, 1)
                need(act, b_dve, BACK_DVE, "sub3", c)
                e3f = e3.rearrange("p a i k -> p (a i k)")
                a.activation(e3f, e3f, ACT.Exp).then_inc(b_act, 1)
                need(act, b_pe, BACK_PE, "pTa", c)
                a.activation(pTa[:, :].rearrange("p (a k) -> p a k", a=2), bk[0:QA, 0:2, 0:HALF],
                             ACT.Copy).then_inc(b_act, 1)
                a.activation(pTb[:, :], bk[0:QB, 2, 0:IMGS * QB], ACT.Copy).then_inc(b_act, 1)
                need(act, b_pe, BACK_PE, "oT", c)
                a.activation(oT.rearrange("p (a k) -> p a k", a=2), bk[:, 2:4, 0:HALF], ACT.Identity,
                             bias=bv3c[:, 0:1]).then_inc(b_act, 1)
                need(act, b_pe, BACK_PE, "x4T", c)
                evict_T(xT, bk_flat, b_act)
                need(act, b_pe, BACK_PE, "q4", c)
                for g in range(2):
                    a.activation(q4T[:, g].rearrange("p (a k) -> p a k", a=2), bk[:, 2 * g:2 * g + 2, 0:HALF],
                                 ACT.Identity, bias=bq4c[:, g:g + 1]).then_inc(b_act, 1)
                need(act, b_pe, BACK_PE, "k4", c)
                for g in range(2):
                    a.activation(k4T[:, g].rearrange("p (a k) -> p a k", a=2), bk[:, 2 * g:2 * g + 2, 0:HALF],
                                 ACT.Identity, bias=bk4c[:, g:g + 1]).then_inc(b_act, 1)
                need(act, b_pe, BACK_PE, "v4", c)
                for t, (_, n) in enumerate(QS):
                    a.activation(v4[0:n, t, :, :, 0:HD].rearrange("p i h d -> p (i h) d"),
                                 bk[0:n, t, :].rearrange("p (k d) -> p k d", d=HD), ACT.Copy).then_inc(b_act, 1)
                need(act, b_pe, BACK_PE, "mT", c)
                a.activation(mT[:, :].rearrange("p (a k) -> p a k", a=2), bk[:, 0:2, 0:HALF],
                             ACT.Copy).then_inc(b_act, 1)
                for i in range(IMGS):
                    for t, (_, n) in enumerate(QS):
                        need(act, b_pe, BACK_PE, f"st{'AB'[t]}_{i}", c)
                        a.activation(p4[0:n, t], bk[0:n, :, 0:2 * N], ACT.Exp,
                                     scale=float(HD) ** -0.5).then_inc(b_act, 1)
                    need(act, b_pe, BACK_PE, f"pv_{i}", c)
                    a.activation(o4T[:, :, N * i:N * i + N], bk[:, 0, 0:2 * N].rearrange("p (g k) -> p g k", g=2),
                                 ACT.Copy).then_inc(b_act, 1)
                need(act, b_pe, BACK_PE, "tT", c)
                evict_T(xT, bk_flat, b_act)
                need(act, b_dve, BACK_DVE, "gsub", c)
                a.activation(ge[:, :, :], gl[:, :, :], ACT.Exp).then_inc(b_act, 1)
                need(act, b_pe, BACK_PE, "coefT", c)
                a.activation(coefT[:, 0:4 * TT], bk_flat[0:E, 0:4 * TT], ACT.Copy).then_inc(b_act, 1)
                a.activation(coefT[:, 4 * TT:T], bk_flat[0:E, 512:512 + TT], ACT.Copy).then_inc(b_act, 1)
                for e in range(E):
                    for k in range(2 * FC):
                        f, half = k // 2, k % 2
                        need(act, b_pe, BACK_PE, f"hid{k}_{e}", c)
                        if k == 0 and e >= 2:
                            need(act, b_pe, BACK_PE, f"out_{e - 2}", c)
                        a.activation(hid[:, e % 2, f, HALF * half:HALF * half + HALF], bk[:, half, 0:HALF],
                                     ACT.Gelu_apprx_tanh, bias=b1c[:, e, f:f + 1]).then_inc(b_act, 1)

            act.wait_ge(loaded_w, LOADED)
            act.wait_ge(su_dve, SU_DVE)

            def chunk(c):
                front(c)
                for g in range(NI):
                    trig_group(c, g)
                trig_end(c)
                back(c)

            chunk(0)
            with act.Fori(1, CHUNKS) as c:
                chunk(c)

        @block.tensor
        def _(pe):
            mm, tr = nc.tensor.matmul, nc.tensor.transpose
            pe.wait_ge(loaded_w, LOADED)
            pe.wait_ge(su_pool, POOL_SETUP)
            pe.wait_ge(su_dve, 16)
            for p2 in range(PS):
                i = tr(bk_flat[0:C * PS, D * p2:D * p2 + D], wt[:, p2].rearrange("d c a -> d (c a)"), ident[:, :])
            i.then_inc(su_pe, 1)
            pe.wait_ge(su_act, 1)
            tr(bk[:, 0, 0:128], su[0][:, :], ident[:, :])
            tr(bk[:, 0, 128:256], zg_w[:, 0:128], ident[:, :])
            tr(bk[:, 0, 256:384], su[1][:, :], ident[:, :]).then_inc(su_pe, 1)
            pe.wait_ge(su_dve, 19)
            mm(bk[:, 1, 0:128], su[3][:, :], su[3][:, :], start=True, stop=True)
            mm(bk[:, 1, 128:256], bd_we[:, :], su[4][:, :], start=True, stop=True).then_inc(su_pe, 1)
            mm(bk[:, 1, 256:257], bd_we[:, :], su_col[:, 4:5], start=True, stop=True).then_inc(su_pe, 1)
            pe.wait_ge(su_dve, 25)
            mm(bk[:, 2, 0:128], su[6][:, :], su[5][:, :], start=True, stop=True).then_inc(su_pe, 1)
            mm(bk[:, 2, 128:256], su[7][:, :], su[5][:, :], start=True, stop=False)
            mm(bk[:, 2, 128:256], su[1][:, :], su[3][:, :], start=False, stop=True).then_inc(su_pe, 1)
            mm(bk[:, 2, 256:384], su[0][:, :], su[2][:, :], start=True, stop=True).then_inc(su_pe, 1)
            for k in range(4):
                i = tr(bk[:, 3, NW * k:NW * k + NW], lutW[:, k], ident[0:NW, 0:NW])
            i.then_inc(su_pe, 1)

            def transposed(src, flat):
                for t in range(NT):
                    at = TT * t if t < 4 else 512
                    i = tr(flat[:, at:at + TT], src[:, t], ident[0:TT, 0:TT])
                return i

            def tokens(src, flat):
                for t in range(NT):
                    i = tr(flat[0:TT, D * t:D * t + D], src[:, TT * t:TT * t + TT], ident[:, :])
                return i

            def front(c):
                need(pe, f_act, FRONT_ACT, "x2Tb", c - 1)
                for p in range(2):
                    pe.wait_ge(x_loaded[p], 96 * (c + 1))
                    for p2 in range(PS):
                        for q in range(2):
                            i = mm(fr[:, q, NPATCH * p:NPATCH * p + NPATCH], patch_w[64 * q:64 * q + C * PS, p2],
                                   patches[64 * q:64 * q + C * PS, :, p2:IW:PS], start=(p2 == 0),
                                   stop=(p2 == PS - 1))
                    i.then_inc(f_pe, 1)
                need(pe, f_dve, FRONT_DVE, "emb1", c)
                tokens(h0T[:, :, :].rearrange("d i n -> d (i n)"), fr_flat).then_inc(f_pe, 1)
                need(pe, f_dve, FRONT_DVE, "x1", c)
                transposed(x1_tok, fr_flat).then_inc(f_pe, 1)
                need(pe, f_act, FRONT_ACT, "x1Tb", c)
                for r in range(2):
                    if r:
                        need(pe, f_dve, FRONT_DVE, "zg0b", c)
                    for k in range(2):
                        for t, (q0, n) in enumerate(QS):
                            at = N * (2 * r + k) + q0
                            i = mm(fr[0:n, k, 256 * t:256 * t + 256], x1T[:, at:at + n], zg_w[:, :], start=True, stop=True)
                    i.then_inc(f_pe, 1)
                need(pe, f_dve, FRONT_DVE, "zg1b", c)
                for i in range(IMGS):
                    for t, (_, n) in enumerate(QS):
                        mm(fr[:, 0, 128 * i:128 * i + 128], zg[0:n, t, i, 0:128], zg[0:n, t, i, 128:256],
                           start=(t == 0), stop=(t == 1))
                for i in range(IMGS):
                    for t, (_, n) in enumerate(QS):
                        last = mm(fr[:, 1, i:i + 1], zg[0:n, t, i, 128:256], ones[0:n, 0:1], start=(t == 0), stop=(t == 1))
                last.then_inc(f_pe, 1)
                need(pe, f_dve, FRONT_DVE, "bnew", c)
                for k in range(2):
                    i = mm(fr[:, k, 0:HALF], psi_w[:, :], x1T[:, HALF * k:HALF * k + HALF], start=True, stop=True)
                i.then_inc(f_pe, 1)
                need(pe, f_act, FRONT_ACT, "pT", c)
                for i in range(IMGS):
                    last = mm(fr[:, i // 2, N * (i % 2):N * (i % 2) + N], wnew[:, i], pT[:, N * i:N * i + N],
                              start=True, stop=True)
                last.then_inc(f_pe, 1)
                need(pe, f_act, FRONT_ACT, "qT3", c)
                for t in range(NT):
                    i = mm(fr_flat[0:TT, D * t:D * t + D], qT[:, TT * t:TT * t + TT], wh[:, :], start=True, stop=True)
                i.then_inc(f_pe, 1)
                need(pe, f_dve, FRONT_DVE, "x2", c)
                transposed(x1_tok, fr_flat).then_inc(f_pe, 1)

            def trig_group(c, g):
                if g == 0:
                    need(pe, t_act, TRIG_ACT, "silu", c - 1)
                for cs, s in enumerate(("cos", "sin")):
                    need(pe, t_act, TRIG_ACT, f"{s}{g}", c)
                    for half in range(2):
                        for j in range(NJ):
                            at = ((NI * j + g) * 2 + cs) * 32
                            i = mm(acc_ps[32 * j:32 * j + 32, half, 0:HALF], trig_w[:, at:at + 32],
                                   trig[:, cs, j, HALF * half:HALF * half + HALF],
                                   start=(g == 0 and cs == 0), stop=(g == NI - 1 and cs == 1))
                    i.then_inc(t_pe, 1)

            def trig_end(c):
                need(pe, t_act, TRIG_ACT, "csT", c)
                for t in range(NT):
                    i = mm(acc_flat[0:TT, D * t:D * t + D], csT[:, TT * t:TT * t + TT], proj_w[:, :], start=True, stop=True)
                i.then_inc(t_pe, 1)

            def back(c):
                need(pe, b_dve, BACK_DVE, "x3", c)
                transposed(x3_tok, bk_flat).then_inc(b_pe, 1)
                need(pe, b_act, BACK_ACT, "x3Tb", c)
                need(pe, b_dve, BACK_DVE, f"acc_{E - 1}", c - 1)
                for w, k0 in ((wqq, 0), (wkk, 2)):
                    for k in range(2):
                        i = mm(bk[:, k0 + k, 0:HALF], w[:, :, :].rearrange("p a b -> p (a b)"),
                               xT[:, HALF * k:HALF * k + HALF], start=True, stop=True)
                    i.then_inc(b_pe, 1)
                need(pe, b_act, BACK_ACT, "k3", c)
                for i in range(IMGS):
                    at = N * i
                    mm(bk[0:QA, 0, QA * i:QA * i + QA], q3T[0:DA, at:at + QA], k3T[0:DA, at:at + QA], start=True, stop=True)
                    last = mm(bk[0:QB, 1 + i // 2, N * (i % 2):N * (i % 2) + N], q3T[DA:128, at + QA:at + N],
                              k3T[DA:128, at:at + N], start=True, stop=True)
                last.then_inc(b_pe, 1)
                for t, (q0, n) in enumerate(QS):
                    if t:
                        need(pe, b_act, BACK_ACT, "v3a", c)
                    for i in range(IMGS):
                        last = mm(bk[0:n, 3, D * i:D * i + D], xT[:, N * i + q0:N * i + q0 + n], wv3[:, :],
                                  start=True, stop=True)
                    last.then_inc(b_pe, 1)
                need(pe, b_dve, BACK_DVE, "p3", c)
                for i in range(IMGS):
                    at = N * (i % 2)
                    tr(bk[0:QA, i // 2, at:at + QA], e3[:, 0, i, 0:QA], ident[0:QA, 0:QA])
                    tr(bk[0:QA, i // 2, at + QA:at + N], e3[0:QB, 1, i, 0:QA], ident[0:QB, 0:QB])
                    last = tr(bk[0:QB, 2, QB * i:QB * i + QB], e3[0:QB, 1, i, QA:N], ident[0:QB, 0:QB])
                last.then_inc(b_pe, 1)
                need(pe, b_act, BACK_ACT, "pTb", c)
                for i in range(IMGS):
                    at = N * (i % 2)
                    mm(bk[:, 2 + i // 2, at:at + N], v3[:, 0, i], pTa[:, N * i:N * i + N], start=True, stop=False)
                    last = mm(bk[:, 2 + i // 2, at + QA:at + N], v3[0:QB, 1, i], pTb[:, QB * i:QB * i + QB],
                              start=False, stop=True)
                last.then_inc(b_pe, 1)
                need(pe, b_act, BACK_ACT, "oT", c)
                tokens(oT, bk_flat[:, 512:]).then_inc(b_pe, 1)
                need(pe, b_dve, BACK_DVE, "x4", c)
                transposed(x4_tok, bk_flat).then_inc(b_pe, 1)
                need(pe, b_act, BACK_ACT, "x4Tb", c)
                for w, ready in ((wq4, "q4b"), (wk4, "k4b")):
                    for g in range(2):
                        for k in range(2):
                            i = mm(bk[:, 2 * g + k, 0:HALF], w[:, g].rearrange("p j k -> p (j k)"),
                                   xT[:, HALF * k:HALF * k + HALF], start=True, stop=True)
                    i.then_inc(b_pe, 1)
                    need(pe, b_act, BACK_ACT, ready, c)
                for t, (q0, n) in enumerate(QS):
                    for i in range(IMGS):
                        last = mm(bk[0:n, t, D * i:D * i + D], xT[:, N * i + q0:N * i + q0 + n], wv4[:, :],
                                  start=True, stop=True)
                last.then_inc(b_pe, 1)
                need(pe, b_act, BACK_ACT, "v4b", c)
                for r in range(2 * IMGS):
                    q0, n = QS[r % 2]
                    at = N * (r // 2)
                    if r:
                        need(pe, b_dve, BACK_DVE, f"s4_{r - 1}", c)
                    for g in range(2):
                        for j in range(NJ):
                            i = mm(bk[0:n, j, N * g:N * g + N], q4T[32 * j:32 * j + HD, g, at + q0:at + q0 + n],
                                   k4T[32 * j:32 * j + HD, g, at:at + N], start=True, stop=True)
                    i.then_inc(b_pe, 1)
                need(pe, b_dve, BACK_DVE, f"s4_{2 * IMGS - 1}", c)
                for r in range(2 * IMGS):
                    q0, n = QS[r % 2]
                    i = r // 2
                    last = tr(bk[:, i // 2, N * (i % 2) + q0:N * (i % 2) + q0 + n], m4[0:n, r], ident[0:n, 0:n])
                last.then_inc(b_pe, 1)
                need(pe, b_act, BACK_ACT, "mT", c)
                for i in range(IMGS):
                    at = N * i
                    for t, (k0, n) in enumerate(QS):
                        if t:
                            need(pe, b_act, BACK_ACT, f"expA_{i}", c)
                        elif i:
                            need(pe, b_act, BACK_ACT, f"pv_{i - 1}", c)
                        for g in range(2):
                            for j in range(NJ):
                                mm(bk[0:n, j, N * g:N * g + N], k4T[32 * j:32 * j + HD, g, at + k0:at + k0 + n],
                                   q4T[32 * j:32 * j + HD, g, at:at + N], start=True, stop=False)
                            for j in range(NJ):
                                last = mm(bk[0:n, j, N * g:N * g + N], neg_sel[32 * j:32 * j + 2, g, 0:n],
                                          mT[32 * j:32 * j + 2, at:at + N], start=False, stop=True)
                        last.then_inc(b_pe, 1)
                    need(pe, b_act, BACK_ACT, f"expB_{i}", c)
                    for g in range(2):
                        for t, (_, n) in enumerate(QS):
                            for j in range(NJ):
                                last = mm(bk[32 * j:32 * j + 32, 0, N * g:N * g + N], v4[0:n, t, i, NJ * g + j],
                                          p4[0:n, t, j, N * g:N * g + N], start=(t == 0), stop=(t == 1))
                    last.then_inc(b_pe, 1)
                need(pe, b_act, BACK_ACT, f"pv_{IMGS - 1}", c)
                for g in range(2):
                    for k in range(2):
                        i = mm(bk[:, 2 * g + k, 0:HALF], sum_sel[:, :], o4T[:, g, HALF * k:HALF * k + HALF],
                               start=True, stop=True)
                i.then_inc(b_pe, 1)
                need(pe, b_dve, BACK_DVE, "onT", c)
                for t in range(NT):
                    for g in range(2):
                        i = mm(bk_flat[0:TT, D * t:D * t + D], on4T[:, g, TT * t:TT * t + TT], wo4[:, g],
                               start=(g == 0), stop=(g == 1))
                i.then_inc(b_pe, 1)
                need(pe, b_dve, BACK_DVE, "t5", c)
                transposed(z_tok, bk_flat).then_inc(b_pe, 1)
                need(pe, b_act, BACK_ACT, "tTb", c)
                for t in range(NT):
                    i = mm(bk[0:TT, 2, E * t:E * t + E], xT[:, TT * t:TT * t + TT], gate_w[:, :], start=True, stop=True)
                i.then_inc(b_pe, 1)
                need(pe, b_dve, BACK_DVE, "coef", c)
                for t in range(NT):
                    at = TT * t if t < 4 else 512
                    i = tr(bk_flat[0:E, at:at + TT], coef[:, t], ident[0:TT, 0:TT])
                i.then_inc(b_pe, 1)
                need(pe, b_act, BACK_ACT, "coefTb", c)
                for t in range(NT):
                    i = mm(bk_flat[0:TT, 1024 + D * t:1024 + D * t + D], coefT[:, TT * t:TT * t + TT], b2s[:, :],
                           start=True, stop=True)
                i.then_inc(b_pe, 1)
                for e in range(E):
                    for k in range(2 * FC):
                        f, half = k // 2, k % 2
                        if k >= 2:
                            need(pe, b_act, BACK_ACT, f"gelu{k - 2}_{e}", c)
                        elif e:
                            need(pe, b_act, BACK_ACT, f"gelu{k + 6}_{e - 1}", c)
                        mm(bk[:, half, 0:HALF], w1[:, e, 128 * f:128 * f + 128], xT[:, HALF * half:HALF * half + HALF],
                           start=True, stop=True).then_inc(b_pe, 1)
                    need(pe, b_act, BACK_ACT, f"gelu7_{e}", c)
                    need(pe, b_dve, BACK_DVE, f"acc_{e - 1}" if e else "acc0", c)
                    for t in range(NT):
                        for f in range(FC):
                            i = mm(bk_flat[0:TT, 1024 + D * t:1024 + D * t + D], hid[:, e % 2, f, TT * t:TT * t + TT],
                                   w2[:, e, f], start=(f == 0), stop=(f == FC - 1))
                    i.then_inc(b_pe, 1)

            pe.wait_ge(copied_w, 16)
            pe.wait_ge(su_dve, SU_DVE)

            def chunk(c):
                front(c)
                for g in range(NI):
                    trig_group(c, g)
                trig_end(c)
                back(c)

            chunk(0)
            with pe.Fori(1, CHUNKS) as c:
                chunk(c)


SU_DVE = 46
POOL_SETUP = 6 + E + 6 + 2 * NJ

_INS = ['x', 'cls_tok', 'L0_tok_W', 'L0_tok_b', 'L0_tok_cls_token', 'L0_tok_pos_emb', 'L0_attn_W_phi', 'L0_attn_b_phi',
        'L0_attn_W_e', 'L0_attn_b_e', 'L0_attn_W_g', 'L0_attn_g_bias', 'L0_attn_W_psi', 'L0_attn_b_psi', 'L0_attn_W_h',
        'L0_attn_h_bias', 'L0_ffn_W', 'L0_ffn_B_param', 'L0_ffn_attn_cos', 'L0_ffn_attn_sin', 'L0_ffn_proj_cos_w',
        'L0_ffn_proj_sin_w', 'L1_attn_Wq', 'L1_attn_bq', 'L1_attn_Wk', 'L1_attn_bk', 'L1_attn_Wv', 'L1_attn_bv',
        'L1_attn_gamma', 'L1_attn_beta', 'L1_ffn_ln1_g', 'L1_ffn_ln1_b', 'L1_ffn_Wq', 'L1_ffn_bq', 'L1_ffn_Wk',
        'L1_ffn_bk', 'L1_ffn_Wv', 'L1_ffn_bv', 'L1_ffn_Wo', 'L1_ffn_bo', 'L1_ffn_gate_W', 'L1_ffn_gate_b', 'L1_ffn_W1',
        'L1_ffn_b1', 'L1_ffn_W2', 'L1_ffn_b2']


def kernel(**inputs):
    import numpy as _np
    import concourse.bacc as _bacc
    from concourse import mybir as _mybir
    from concourse.bass_utils import run_bass_kernel_spmd as _run

    nc = _bacc.Bacc("TRN2", target_bir_lowering=False, num_devices=1)
    arrays, args = {}, []
    for name in _INS:
        a = _np.ascontiguousarray(inputs[name])
        arrays[f"in_{name}_dram"] = a
        args.append(nc.dram_tensor(f"in_{name}_dram", a.shape, _mybir.dt.from_np(a.dtype), kind="ExternalInput").ap())
    args.append(nc.dram_tensor("out_0_dram", (B, N, D), F32, kind="ExternalOutput").ap())
    vit_tower(nc, *args)
    r = _run(nc, [arrays], core_ids=[0])
    return r.results[0]["out_0_dram"]
```

```python
from contextlib import ExitStack

import numpy as np

import concourse.bass as bass
from concourse import mybir

ALU = mybir.AluOpType
ACT = mybir.ActivationFunctionType
F32 = mybir.dt.float32
I16 = mybir.dt.int16
AX = mybir.AxisListType.X

B, C, IH, IW = 64, 3, 176, 208
PS = 16
PW, PH = IH // PS, IW // PS
NPATCH = PW * PH
N = NPATCH + 2
D = 128
IMGS = 4
CHUNKS = B // IMGS
T = IMGS * N
HALF = T // 2
TT = 116
NT = T // TT
QA = 73
QB = N - QA
QS = ((0, QA), (QA, QB))
H, HD = 8, 16
E, FF = 8, 512
FC = FF // 128
DA = 64
NW = 64
NJ = 4
NI = NW // NJ
LUT = 1024
EPS = 1e-5
MASKED = -1e30
MAGIC = 12582912.0
LR_SCALE = H / (N * D)
TO_LUT = float(np.float32(LUT / (2.0 * np.pi)))
FROM_LUT = float(np.float32(2.0 * np.pi / LUT))
MINUS_PI = -3.1415925

TICKS = 2 * NI
EMB_PE = tuple(f"emb{m}" for m in range(IMGS))
EMB_DVE = ("cls", "emb01", "emb23")
FRONT_PE = ("h0", "x1T", "zg0", "zg1", "cross", "pT", "qT", "attn", "x2T")
FRONT_ACT = ("h0", "x1Ta", "x1Tb", "pT", "qT0", "qT1", "qT2", "qT3", "x2Ta", "x2Tb")
FRONT_DVE = ("bn1", "ln1", "x1", "zg0a", "zg0b", "zg1a", "zg1b", "masked", "wnew", "bnew", "h1", "bn2", "ln2", "x2")
FRONT_POOL = ("eps1", "rstd1", "hb", "eps2", "rstd2", "h1hold")
TRIG_DVE = tuple(f"{s}{g}" for g in range(NI) for s in ("k", "add", "and"))
TRIG_ACT = (*(f"{s}{g}" for g in range(NI) for s in ("cos", "sin")), "csT", "silu")
TRIG_PE = (*(f"{s}{g}" for g in range(NI) for s in ("mmcos", "mmsin")), "proj")
TRIG_POOL = ("h2",)


def softmax_steps(name):
    steps = []
    for i in range(IMGS):
        steps += [f"{name}0_{i}", f"{name}1_{i}"] + ([f"pv_{i - 1}"] if i else []) + [f"{name}2_{i}", f"{name}3_{i}"]
    return (*steps, f"pv_{IMGS - 1}")


BACK_PE = ("x3T", "q3", "k3", "s3", "v3a", "v3b", "pTa", "oT", "o3", "x4T", "q4", "k4", "v4",
           *(f"{s}_{r}" for r in range(2 * IMGS) for s in ("s4", "mT")), *softmax_steps("st"), "o4", "onT", "wo", "tT", "gate",
           *(f"hid{f}_0" for f in range(FC)), "coefT", "hid0_1", "hid1_1", "b2", "hid2_1", "hid3_1", "out_0",
           *(s for e in range(2, E) for s in (*(f"hid{f}_{e}" for f in range(FC)), f"out_{e - 1}")), f"out_{E - 1}")
BACK_ACT = ("x3Ta", "x3Tb", "q3", "k3", "v3a", "v3b", "e3", "pTa", "pTb", "oT", "x4Ta", "x4Tb",
            "q4a", "q4b", "k4a", "k4b", "v4a", "v4b", *softmax_steps("exp"), "onTa", "onTb", "tTa", "tTb", "gexp",
            *(f"gelu{f}_0" for f in range(FC)), "coefTa", "coefTb",
            *(f"gelu{f}_{e}" for e in range(1, E) for f in range(FC)))
BACK_DVE = ("bn3", "ln3", "x3", "mask3a", "mask3b", "max3", "sub3", "sum3", "rec3", "p3", "y3",
            "bny", "lny", "zy", "h3", "bn4", "ln4", "x4",
            *(f"s4_{r}" for r in range(2 * IMGS)), "qm0", "qm1", "rsum", "on", "y4", "bn5", "ln5", "z5", "t5",
            "glog", "gmax", "gsub", "gsum", "gemax", "grec", "gmask", "gscore", "gsmax", "goh", "gw", "coef",
            "acc0", *(f"acc_{e}" for e in range(E)))
BACK_POOL = ("eps3", "rstd3", "hb3", "epsy", "rstdy", "eps4", "rstd4", "x4b", "kM", "eps5", "rstd5")


def value(steps, name, chunk):
    return chunk * len(steps) + steps.index(name) + 1


def need(engine, sem, steps, name, chunk):
    v = value(steps, name, chunk)
    if not isinstance(v, int) or v > 0:
        engine.wait_ge(sem, v)


def vit_tower(nc, x, cls_tok, tok_W, tok_b, tok_cls, tok_pos, W_phi, b_phi, W_e, b_e, W_g, g_bias, W_psi, b_psi,
              W_h, h_bias, ffn_W, ffn_B, ffn_cos, ffn_sin, pcos, psin, Wq3, bq3, Wk3, bk3, Wv3, bv3, gamma3, beta3,
              ln_g, ln_b, Wq4, bq4, Wk4, bk4, Wv4, bv4, Wo4, bo4, gate_W, gate_b, W1, b1, W2, b2, out):
    with ExitStack() as ctx:
        def sb(name, shape, dt=F32):
            return ctx.enter_context(nc.sbuf_tensor(name, shape, dt))

        def sem(name):
            return ctx.enter_context(nc.semaphore(name))

        ident = sb("ident", [128, 128])
        ones = sb("ones", [128, 128])
        block_mask = sb("block_mask", [128, 128])
        maskA = sb("maskA", [QA, QA])
        maskB = sb("maskB", [QB, N])
        rank = sb("rank", [TT, E])
        head_mask = sb("head_mask", [128, NJ])
        head_neg = sb("head_neg", [128, 2, NJ])
        patch_w = sb("patch_w", [2 * C * PS, PS // 2, D])
        addend = sb("addend", [128, N])
        zg_w = sb("zg_w", [D, 256])
        zg_b = sb("zg_b", [128, 256])
        bd_we = sb("bd_we", [128, 128])
        be_col = sb("be_col", [128, 1])
        psi_w = sb("psi_w", [D, 128])
        psi_b = sb("psi_b", [128, 1])
        wh = sb("wh", [128, D])
        hbias_row = sb("hbias_row", [128, D])
        lut_s = sb("lut_s", [D, NW])
        lut_b = sb("lut_b", [D, NW])
        trig_w = sb("trig_w", [D, NW * 64 + 64])
        proj_w = sb("proj_w", [128, D])
        wqq = sb("wqq", [D, 2, DA])
        wkk = sb("wkk", [D, 2, DA])
        bqq = sb("bqq", [128, 1])
        bkk = sb("bkk", [128, 1])
        wv3 = sb("wv3", [D, D])
        bv3c = sb("bv3c", [D, 1])
        gamma_row = sb("gamma_row", [128, D])
        beta_row = sb("beta_row", [128, D])
        wq4 = sb("wq4", [D, 2, NJ, 32])
        wk4 = sb("wk4", [D, 2, NJ, 32])
        bq4c = sb("bq4c", [128, 2])
        bk4c = sb("bk4c", [128, 2])
        wv4 = sb("wv4", [D, D])
        wo4 = sb("wo4", [D, D])
        bo_row = sb("bo_row", [128, D])
        g5_row = sb("g5_row", [128, D])
        b5_row = sb("b5_row", [128, D])
        gate_w = sb("gate_w", [D, E])
        gate_row = sb("gate_row", [128, E])
        w1 = sb("w1", [D, E, FF])
        b1c = sb("b1c", [128, E, FC])
        w2 = sb("w2", [128, E, FC, D])
        b2s = sb("b2s", [E, D])

        patches = sb("patches", [2 * C * PS, 2, PW, IW])
        h0T = sb("h0T", [D, IMGS, N])
        h0_tok = sb("h0_tok", [TT, NT, D])
        hb_tok = h0_tok
        x1_room = sb("x1_room", [128, NT * D])
        x1_tok = x1_room[0:TT].rearrange("p (t d) -> p t d", t=NT)
        x1T = h0T[:, :, :].rearrange("d i n -> d (i n)")
        zg = sb("zg", [QA, 2, IMGS, 256])
        wnew = sb("wnew", [128, IMGS, 128])
        bnew = sb("bnew", [128, IMGS])
        pT = sb("pT", [128, T])
        qT = x1T
        h1_tok = sb("h1_tok", [TT, NT, D])
        h1_hold = sb("h1_hold", [TT, NT, D])
        x2T = sb("x2T", [D, T])
        kbuf = sb("kbuf", [D, 2, 2, NJ, T], I16)
        trig = sb("trig", [D, 2, NJ, T])
        csT = x1_room[:, 0:T]
        h2_tok = sb("h2_tok", [TT, NT, D])
        silu_tok = h2_tok
        x3_tok = sb("x3_tok", [TT, NT, D])
        x4_tok = x3_tok
        hid = sb("hid", [128, 2, FC, T])
        hidf = hid[:, :, :, :].rearrange("p a f k -> p (a f k)")
        q3T, k3T, oT, pTa = (hidf[0:n, T * i:T * i + T] for i, n in enumerate((128, 128, D, QA)))
        pTb = hidf[0:QB, 4 * T:4 * T + IMGS * QB]
        v3 = hidf[0:QA, 5 * T:5 * T + 2 * IMGS * D].rearrange("p (a i d) -> p a i d", a=2, i=IMGS)
        kM = hidf.rearrange("p (h k) -> p h k", h=H)
        q4T = sb("q4T", [128, 2, T])
        onT = q4T[:, 0]
        k4T = sb("k4T", [128, 2, T])
        o4T = k4T
        s3 = sb("s3", [QA, 2, IMGS, N])
        e3 = hidf[0:QA, 0:2 * IMGS * N].rearrange("p (a i k) -> p a i k", a=2, i=IMGS)
        p4 = [trig[0:QA, b].rearrange("p j k -> p (j k)").rearrange("p (t g j k) -> p t g j k", t=2, g=2, j=NJ)
              for b in range(2)]
        xT = sb("xT", [D, T])
        m3 = sb("m3", [QA, 2 * IMGS])
        sum3 = sb("sum3", [QA, 2 * IMGS])
        rec3 = sb("rec3", [QA, 2 * IMGS])
        y_tok = sb("y_tok", [TT, NT, D])
        z_tok = on_tok = y_tok
        hb3_tok = h2_tok
        x4b_tok = x4_tok
        h3_tok = sb("h3_tok", [TT, NT, D])
        acc = h3_tok
        v4 = sb("v4", [QA, 2, IMGS, H, 32])
        m4 = sb("m4", [QA, 128])
        r4 = sb("r4", [TT, NT * H])
        gl = sb("gl", [TT, NT, E])
        ge = sb("ge", [TT, NT, E])
        gt = sb("gt", [TT, NT, E])
        gs = sb("gs", [TT, 6, NT])
        coef = sb("coef", [TT, NT, E])
        coefT = pT[0:E]
        bn = {k: sb(f"bn_{k}", [TT, NT, 6]) for k in ("1", "2", "3", "y", "4", "5")}
        mv = {k: sb(f"mv_{k}", [TT, NT, 2]) for k in bn}
        ve = {k: sb(f"ve_{k}", [TT, NT]) for k in bn}
        rstd = {k: sb(f"rstd_{k}", [TT, NT]) for k in bn}
        minus_half = sb("minus_half", [TT, NT])

        tokw_in = hidf[:, 0:C * PS * PS]
        trigf = trig[:, :, :, :].rearrange("p a j k -> p (a j k)")
        su = [trigf[:, 128 * i:128 * i + 128] for i in range(8)]
        lutW = trigf[0:NW, 1024:1024 + 4 * D].rearrange("n (a d) -> n a d", a=4)
        wt = trigf[:, 1536:1536 + C * PS * PS].rearrange("d (b c a) -> d b c a", b=PS, c=C)
        su_col = sb("su_col", [128, 8])
        odd_w = hidf[0:C * PS, 1024:1024 + PS // 2 * D]

        psum = ctx.enter_context(nc.psum_tensor("psum", [128, 8, 512], F32))
        acc_ps = psum[:, 0:2, :]
        fr = psum[:, 2:4, :]
        bk = psum[:, 4:8, :]
        fr_tok = fr[0:TT].rearrange("p a b -> p (a b)")[:, 0:NT * D]
        fr_flat = fr.rearrange("p a b -> p (a b)")
        bk_flat = bk.rearrange("p a b -> p (a b)")
        acc_flat = acc_ps.rearrange("p a b -> p (a b)")
        hid_ps = (bk[:, 0:2], acc_ps)

        loaded_w = sem("weights_loaded")
        copied_w = sem("patch_weights_copied")
        su_pool = sem("setup_pool")
        su_dve = sem("setup_dve")
        su_pe = sem("setup_pe")
        su_act = sem("setup_act")
        x_loaded = [sem(f"{p}_images_loaded") for p in ("even", "odd")]
        e_pe, e_dve = sem("embed_pe"), sem("embed_dve")
        f_pe, f_act, f_dve, f_pool = sem("front_pe"), sem("front_act"), sem("front_dve"), sem("front_pool")
        t_pe, t_act, t_dve, t_pool = sem("trig_pe"), sem("trig_act"), sem("trig_dve"), sem("trig_pool")
        b_pe, b_act, b_dve, b_pool = sem("back_pe"), sem("back_act"), sem("back_dve"), sem("back_pool")
        stored = sem("stored")

        def row(ap, n=128):
            return ap.unsqueeze(0).to_broadcast([n, *ap.shape])

        W_all = W_g.rearrange("h e w -> (h e) w")
        loads = [
            (tokw_in, tok_W), (addend[:, 2:N], row(tok_pos[0, 1:NPATCH + 1, 0])),
            (su_col[:, 0:1], tok_b.unsqueeze(1)), (su_col[:, 1:2], cls_tok[0, 0].unsqueeze(1)),
            (su_col[:, 2:3], tok_cls[0, 0].unsqueeze(1)), (su_col[:, 3:4], row(tok_pos[0, 0, :])),
            (zg_w[:, 0:128].rearrange("w (h d) -> w h d", h=H), W_phi.rearrange("h w d -> w h d")),
            (zg_b[:, 0:128], row(b_phi.rearrange("h d -> (h d)"))),
            (su_col[:, 4:5], b_phi.rearrange("h d -> (h d)").unsqueeze(1)),
            (be_col[:, :], b_e.rearrange("h d -> (h d)").unsqueeze(1)),
            (su_col[:, 5:6], g_bias[0].unsqueeze(1)),
            (su[0][:, :], W_all),
            (psi_w[:, :].rearrange("w (h d) -> w h d", h=H), W_psi.rearrange("h w d -> w h d")),
            (psi_b[:, :], b_psi.rearrange("h d -> (h d)").unsqueeze(1)),
            (wh[:, :], W_h.rearrange("h e w -> (h e) w")), (hbias_row[:, :], row(h_bias[0])),
            (lutW[:, 0], ffn_W), (lutW[:, 1], ffn_B), (lutW[:, 2], ffn_cos), (lutW[:, 3], ffn_sin),
            (su[1][:, :].rearrange("d (j c i) -> d j c i", j=NJ, c=2)[:, :, 0], pcos.rearrange("d (j i) -> d j i", j=NJ)),
            (su[1][:, :].rearrange("d (j c i) -> d j c i", j=NJ, c=2)[:, :, 1], psin.rearrange("d (j i) -> d j i", j=NJ)),
            (wqq[:, 0], Wq3), (wqq[:, 1], Wq3), (wkk[:, 0], Wk3), (wkk[:, 1], Wk3),
            (bqq[0:DA, :], bq3.unsqueeze(1)), (bqq[DA:, :], bq3.unsqueeze(1)),
            (bkk[0:DA, :], bk3.unsqueeze(1)), (bkk[DA:, :], bk3.unsqueeze(1)),
            (wv3[:, :], Wv3), (bv3c[:, :], bv3.unsqueeze(1)), (gamma_row[:, :], row(gamma3)),
            (beta_row[:, :], row(beta3)), (wv4[:, :], Wv4), (wo4[:, :], Wo4), (su_col[:, 6:7], bv4.unsqueeze(1)),
            (bo_row[:, :], row(bo4)), (g5_row[:, :], row(ln_g)), (b5_row[:, :], row(ln_b)),
            (gate_w[:, :], gate_W), (gate_row[:, :], row(gate_b)), (w1[:, :, :], W1.rearrange("e d f -> d e f")),
            (b1c[:, :, :], b1.rearrange("e (k p) -> p e k", p=128)),
            (w2[:, :, :, :], W2.rearrange("e (k p) d -> p e k d", p=128)), (b2s[:, :], b2),
        ]
        padded = []
        for h in range(H):
            g, j = h // NJ, h % NJ
            padded += [
                (bd_we[HD * h:HD * h + HD, HD * h:HD * h + HD], W_e[h]),
                (bq4c[32 * j:32 * j + HD, g:g + 1], bq4[HD * h:HD * h + HD].unsqueeze(1)),
                (bk4c[32 * j:32 * j + HD, g:g + 1], bk4[HD * h:HD * h + HD].unsqueeze(1)),
            ]
        for g in range(2):
            padded += [
                (wq4[:, g, :, 0:HD], Wq4[:, 64 * g:64 * g + 64].rearrange("d (j i) -> d j i", j=NJ)),
                (wk4[:, g, :, 0:HD], Wk4[:, 64 * g:64 * g + 64].rearrange("d (j i) -> d j i", j=NJ)),
            ]
        LOADED = 16 * (len(loads) + len(padded))
        ZEROED = 6
        out_c = out.rearrange("b n d -> (b n) d").rearrange("(c t p) d -> c p t d", t=NT, p=TT)

        dve_waited, pool_waited = sem("dve_waited"), sem("pool_waited")

        def take_waits(engine, waited):
            engine.sem_inc(waited, 1)

        block = ctx.enter_context(nc.Block())

        @block.sync
        def _(sp):
            def load(m, c):
                if m < 2:
                    need(sp, e_pe, EMB_PE, f"emb{m + 2}", c - 1)
                else:
                    need(sp, e_pe, EMB_PE, f"emb{m - 2}", c)
                for q in range(2):
                    for ch in range(C):
                        at = C * PS * q + PS * ch
                        sp.dma_start(patches[at:at + PS, m % 2, :, 0:IW - q],
                                     x[IMGS * c + m, ch, :, q:IW].rearrange("(w r) k -> r w k", r=PS)
                                     ).then_inc(x_loaded[m % 2], 16)

            def store(c):
                need(sp, b_dve, BACK_DVE, f"acc_{E - 1}", c)
                sp.dma_start(out_c[c], acc[:, :, :]).then_inc(stored, 16)

            def body(i, loads=True, stores=True):
                if loads:
                    for m in range(IMGS):
                        load(m, i + 2)
                if stores:
                    store(i - 1)

            load(0, 0)
            load(1, 0)
            with nc.allow_non_contiguous_dma(reason="bias columns, once"):
                for dst, src in loads:
                    sp.dma_start(dst, src).then_inc(loaded_w, 16)
            sp.wait_ge(su_dve, ZEROED)
            for dst, src in padded:
                sp.dma_start(dst, src).then_inc(loaded_w, 16)
            sp.wait_ge(su_act, 2)
            sp.dma_start(patch_w[C * PS:].rearrange("p a d -> p (a d)"), odd_w).then_inc(copied_w, 16)
            load(2, 0)
            load(3, 0)
            for m in range(IMGS):
                load(m, 1)
            body(0, stores=False)
            body(1)
            with sp.Fori(2, CHUNKS - 2) as i:
                body(i)
            for i in range(CHUNKS - 2, CHUNKS + 1):
                body(i, loads=False)
            sp.wait_ge(stored, 16 * CHUNKS)

        @block.gpsimd
        def _(pool):
            nc.gpsimd.memset(ident[:, :], 0.0).then_inc(su_pool, 1)
            nc.gpsimd.memset(block_mask[:, :], 1.0).then_inc(su_pool, 1)
            nc.gpsimd.memset(maskA[:, :], 0.0).then_inc(su_pool, 1)
            nc.gpsimd.memset(maskB[:, :], 0.0).then_inc(su_pool, 1)
            nc.gpsimd.memset(head_mask[:, :], 1.0).then_inc(su_pool, 1)
            nc.gpsimd.memset(head_neg[:, :, :], 0.0).then_inc(su_pool, 1)
            for e in range(E):
                nc.gpsimd.memset(rank[:, e:e + 1], float(E - e)).then_inc(su_pool, 1)
            pool.wait_ge(su_pool, 6 + E)
            nc.gpsimd.affine_select(out=ident[:, :], in_=ident[:, :], compare_op=ALU.not_equal, fill=1.0, base=0,
                                    pattern=[[-1, 128]], channel_multiplier=1).then_inc(su_pool, 1)
            bm = block_mask[:, :].rearrange("p (g k) -> p g k", g=H)
            nc.gpsimd.affine_select(out=bm, in_=bm, compare_op=ALU.is_ge, fill=0.0, base=0,
                                    pattern=[[-HD, H], [0, HD]], channel_multiplier=1).then_inc(su_pool, 1)
            pool.wait_ge(su_pool, 8 + E)
            nc.gpsimd.affine_select(out=bm, in_=bm, compare_op=ALU.is_ge, fill=0.0, base=HD - 1,
                                    pattern=[[HD, H], [0, HD]], channel_multiplier=-1).then_inc(su_pool, 1)
            nc.gpsimd.affine_select(out=maskA[:, :], in_=maskA[:, :], compare_op=ALU.is_ge, fill=MASKED, base=0,
                                    pattern=[[-1, QA]], channel_multiplier=1).then_inc(su_pool, 1)
            nc.gpsimd.affine_select(out=maskB[:, :], in_=maskB[:, :], compare_op=ALU.is_ge, fill=MASKED, base=QA,
                                    pattern=[[-1, N]], channel_multiplier=1).then_inc(su_pool, 1)
            nc.gpsimd.affine_select(out=head_mask[:, :], in_=head_mask[:, :], compare_op=ALU.is_ge, fill=0.0, base=0,
                                    pattern=[[-32, NJ]], channel_multiplier=1).then_inc(su_pool, 1)
            for g in range(2):
                nc.gpsimd.affine_select(out=head_neg[:, g], in_=head_neg[:, g], compare_op=ALU.not_equal, fill=-1.0,
                                        base=-HD - g, pattern=[[-32, NJ]], channel_multiplier=1).then_inc(su_pool, 1)
            pool.wait_ge(su_pool, 14 + E)
            nc.gpsimd.affine_select(out=head_mask[:, :], in_=head_mask[:, :], compare_op=ALU.is_ge, fill=0.0,
                                    base=HD - 1, pattern=[[32, NJ]], channel_multiplier=-1).then_inc(su_pool, 1)

            def ln(sem_in, steps_in, name, eps, c, sem_out, steps_out):
                need(pool, sem_in, steps_in, "ln" + name, c)
                take_waits(pool, pool_waited)
                nc.gpsimd.tensor_scalar(ve[name][:, :], mv[name][:, :, 1], EPS, 1.0, ALU.add,
                                        ALU.mult).then_inc(sem_out, 1)
                need(pool, sem_out, steps_out, "eps" + name, c)
                nc.gpsimd.tensor_tensor(rstd[name][:, :], ve[name][:, :], minus_half[:, :],
                                        ALU.pow).then_inc(sem_out, 1)

            def front(tick, c):
                if tick == 15:
                    ln(f_dve, FRONT_DVE, "1", EPS, c, f_pool, FRONT_POOL)
                if tick == 18:
                    need(pool, f_act, FRONT_ACT, "h0", c)
                    need(pool, f_dve, FRONT_DVE, "x1", c)
                    nc.gpsimd.tensor_tensor(hb_tok[:, :, :], h0_tok[:, :, :],
                                            hbias_row[0:TT].unsqueeze(1).to_broadcast([TT, NT, D]),
                                            ALU.add).then_inc(f_pool, 1)
                if tick == 23:
                    ln(f_dve, FRONT_DVE, "2", EPS, c, f_pool, FRONT_POOL)

            def hold(c):
                need(pool, f_dve, FRONT_DVE, "ln2", c)
                need(pool, t_pool, TRIG_POOL, "h2", c - 1)
                take_waits(pool, pool_waited)
                nc.gpsimd.tensor_copy(h1_hold[:, :, :], h1_tok[:, :, :]).then_inc(f_pool, 1)

            def trig_end(c):
                need(pool, t_act, TRIG_ACT, "silu", c)
                need(pool, f_pool, FRONT_POOL, "h1hold", c)
                nc.gpsimd.tensor_tensor(h2_tok[:, :, :], h1_hold[:, :, :], silu_tok[:, :, :],
                                        ALU.add).then_inc(t_pool, 1)

            def back(tick, c):
                if tick == 0:
                    ln(b_dve, BACK_DVE, "3", EPS, c, b_pool, BACK_POOL)
                if tick == 1:
                    need(pool, b_dve, BACK_DVE, "x3", c)
                    nc.gpsimd.tensor_tensor(hb3_tok[:, :, :], h2_tok[:, :, :],
                                            beta_row[0:TT].unsqueeze(1).to_broadcast([TT, NT, D]),
                                            ALU.add).then_inc(b_pool, 1)
                if tick == 10:
                    ln(b_dve, BACK_DVE, "y", EPS, c, b_pool, BACK_POOL)
                if tick == 12:
                    ln(b_dve, BACK_DVE, "4", EPS, c, b_pool, BACK_POOL)
                if tick == 13:
                    need(pool, b_pe, BACK_PE, "x4T", c)
                    nc.gpsimd.tensor_tensor(x4b_tok[:, :, :], x4_tok[:, :, :],
                                            bo_row[0:TT].unsqueeze(1).to_broadcast([TT, NT, D]),
                                            ALU.add).then_inc(b_pool, 1)
                if tick == 16:
                    need(pool, b_act, BACK_ACT, "k4b", c)
                    take_waits(pool, pool_waited)
                    for h in range(H):
                        g, j = h // NJ, h % NJ
                        i = nc.gpsimd.tensor_scalar(kM[:, h], k4T[:, g], head_mask[:, j:j + 1], head_neg[:, g, j:j + 1],
                                                    ALU.mult, ALU.add)
                    i.then_inc(b_pool, 1)

            pool.wait_ge(loaded_w, LOADED)
            pool.wait_ge(su_dve, SU_DVE)

            def body(i, fronts=True, trigs=True, backs=True):
                for tick in range(TICKS):
                    if backs:
                        back(tick, i - 1)
                    if fronts:
                        front(tick, i + 1)
                if trigs:
                    trig_end(i)
                if fronts:
                    hold(i + 1)
                if backs:
                    ln(b_dve, BACK_DVE, "5", EPS, i - 1, b_pool, BACK_POOL)

            body(-1, trigs=False, backs=False)
            body(0, backs=False)
            body(1)
            with pool.Fori(2, CHUNKS - 1) as i:
                body(i)
            body(CHUNKS - 1, fronts=False)
            body(CHUNKS, fronts=False, trigs=False)

        @block.vector
        def _(dve):
            v = nc.vector
            v.memset(bd_we[:, :], 0.0).then_inc(su_dve, 1)
            v.memset(bq4c[:, :], 0.0).then_inc(su_dve, 1)
            v.memset(bk4c[:, :], 0.0).then_inc(su_dve, 1)
            v.memset(wq4[:, :, :, :], 0.0).then_inc(su_dve, 1)
            v.memset(wk4[:, :, :, :], 0.0).then_inc(su_dve, 1)
            v.memset(trig_w[:, :], 0.0).then_inc(su_dve, 1)
            v.memset(v4[:, :, :, :, :], 1.0).then_inc(su_dve, 1)
            v.memset(m4[:, :], 0.0).then_inc(su_dve, 1)
            v.memset(rec3[:, :], 1.0).then_inc(su_dve, 1)
            v.memset(minus_half[:, :], -0.5).then_inc(su_dve, 1)
            v.memset(s3[:, :, :, :], MASKED).then_inc(su_dve, 1)
            v.memset(ones[:, :], 1.0).then_inc(su_dve, 1)
            dve.wait_ge(loaded_w, LOADED)
            v.tensor_scalar(addend[:, 2:N], addend[:, 2:N], su_col[:, 0:1], None, ALU.add).then_inc(su_dve, 1)
            v.tensor_copy(addend[:, 0:1], su_col[:, 1:2]).then_inc(su_dve, 1)
            v.tensor_tensor(addend[:, 1:2], su_col[:, 2:3], su_col[:, 3:4], ALU.add).then_inc(su_dve, 1)
            v.tensor_copy(wt, tokw_in.rearrange("d (a b c) -> d b c a", a=PS, b=PS)).then_inc(su_dve, 1)
            dve.wait_ge(su_pe, 2)
            v.tensor_copy(su[3][:, :], bk[:, 0, 0:128]).then_inc(su_dve, 1)
            v.tensor_copy(su[4][:, :], bk[:, 0, 128:256]).then_inc(su_dve, 1)
            v.tensor_copy(proj_w[:, :], bk[:, 0, 256:384]).then_inc(su_dve, 1)
            dve.wait_ge(su_pe, 4)
            dve.wait_ge(su_pool, POOL_SETUP)
            v.tensor_tensor(su[5][:, :], bk[:, 1, 0:128], block_mask[:, :], ALU.mult).then_inc(su_dve, 1)
            v.tensor_copy(su[6][:, :], bk[:, 1, 128:256]).then_inc(su_dve, 1)
            v.tensor_tensor(su_col[:, 7:8], bk[:, 1, 256:257], be_col[:, :], ALU.add).then_inc(su_dve, 1)
            dve.wait_ge(su_dve, 22)
            v.tensor_scalar(su[7][:, :], ones[:, :], su_col[:, 7:8], None, ALU.mult).then_inc(su_dve, 1)
            v.tensor_scalar(su[1][:, :], ones[:, :], su_col[:, 5:6], None, ALU.mult).then_inc(su_dve, 1)
            v.tensor_scalar(su[0][:, :], ones[:, :], su_col[:, 6:7], None, ALU.mult).then_inc(su_dve, 1)
            dve.wait_ge(su_pe, 7)
            v.tensor_tensor(su[4][:, :], su[3][:, :], bk[:, 2, 0:128], ALU.subtract).then_inc(su_dve, 1)
            v.tensor_scalar(zg_b[:, 128:256], bk[:, 2, 128:256], -LR_SCALE, None, ALU.mult).then_inc(su_dve, 1)
            v.tensor_tensor(bo_row[:, :], bo_row[:, :], bk[:, 2, 256:384], ALU.add).then_inc(su_dve, 1)
            dve.wait_ge(su_dve, 28)
            v.tensor_scalar(zg_w[:, 128:256], su[4][:, :], LR_SCALE, None, ALU.mult).then_inc(su_dve, 1)
            dve.wait_ge(su_pe, 8)
            lw = bk[:, 3, 0:4 * NW].rearrange("p (a n) -> p a n", a=4)
            v.tensor_scalar(lut_s[:, :], lw[:, 0], -1.0, None, ALU.mult).then_inc(su_dve, 1)
            dve.wait_ge(su_dve, 30)
            v.tensor_tensor(lut_s[:, :], lw[:, 0], lut_s[:, :], ALU.max).then_inc(su_dve, 1)
            dve.wait_ge(su_dve, 31)
            v.tensor_scalar(lut_s[:, :], lut_s[:, :], 1.0, None, ALU.add).then_inc(su_dve, 1)
            dve.wait_ge(su_dve, 32)
            v.reciprocal(lut_s[:, :], lut_s[:, :]).then_inc(su_dve, 1)
            dve.wait_ge(su_dve, 33)
            v.tensor_scalar(lut_s[:, :], lut_s[:, :], TO_LUT, None, ALU.mult).then_inc(su_dve, 1)
            v.tensor_scalar(su[2][:, 0:NW], lw[:, 1], TO_LUT, None, ALU.mult).then_inc(su_dve, 1)
            dve.wait_ge(su_dve, 35)
            v.tensor_scalar(lut_b[:, :], su[2][:, 0:NW], 1.0 / LUT, MAGIC, ALU.mult, ALU.add).then_inc(su_dve, 1)
            dve.wait_ge(su_dve, 36)
            v.tensor_scalar(lut_b[:, :], lut_b[:, :], MAGIC, -float(LUT), ALU.subtract, ALU.mult).then_inc(su_dve, 1)
            dve.wait_ge(su_dve, 37)
            v.tensor_tensor(lut_b[:, :], lut_b[:, :], su[2][:, 0:NW], ALU.add).then_inc(su_dve, 1)
            for cs in range(2):
                for j in range(NJ):
                    at = j * NI * 64 + cs * 48
                    v.tensor_scalar(trig_w[:, at:at + 65 * (NI - 1) + 1:65], lw[:, 2 + cs, NI * j:NI * j + NI], -1.0,
                                    None, ALU.mult).then_inc(su_dve, 1)

            def stats(src, name, c, sem_d, steps):
                for t in range(NT):
                    i = v.bn_stats(bn[name][:, t], src[:, t])
                i.then_inc(sem_d, 1)
                need(dve, sem_d, steps, "bn" + name, c)
                take_waits(dve, dve_waited)
                for t in range(NT):
                    i = v.bn_aggr(mv[name][:, t], bn[name][:, t])
                i.then_inc(sem_d, 1)

            def normal(src, name, c, sem_d, steps, sem_p, steps_p, dst):
                need(dve, sem_d, steps, "ln" + name, c)
                need(dve, sem_p, steps_p, "rstd" + name, c)
                for t in range(NT):
                    i = v.tensor_scalar(dst[:, t], src[:, t], mv[name][:, t, 0:1], rstd[name][:, t:t + 1],
                                        ALU.subtract, ALU.mult)
                i.then_inc(sem_d, 1)

            def embed_out(c):
                need(dve, f_pe, FRONT_PE, "attn", c - 1)
                v.tensor_copy(h0T[:, :, 0:2], addend[:, 0:2].unsqueeze(1).to_broadcast([D, IMGS, 2])).then_inc(e_dve, 1)
                for k in range(2):
                    need(dve, e_pe, EMB_PE, f"emb{2 * k + 1}", c)
                    v.tensor_tensor(h0T[:, 2 * k:2 * k + 2, 2:N],
                                    fr[:, k, 0:2 * NPATCH].rearrange("d (p n) -> d p n", p=2),
                                    addend[:, 2:N].unsqueeze(1).to_broadcast([D, 2, NPATCH]),
                                    ALU.add).then_inc(e_dve, 1)

            def front(tick, c):
                if tick == 15:
                    need(dve, f_act, FRONT_ACT, "h0", c)
                    stats(h0_tok, "1", c, f_dve, FRONT_DVE)
                if tick == 16:
                    need(dve, t_pe, TRIG_PE, "proj", c - 2)
                    normal(h0_tok, "1", c, f_dve, FRONT_DVE, f_pool, FRONT_POOL, x1_tok)
                for r in range(2):
                    if tick == 18 + r:
                        need(dve, f_pe, FRONT_PE, f"zg{r}", c)
                        for t, (_, n) in enumerate(QS):
                            v.tensor_tensor(zg[0:n, t, 2 * r:2 * r + 2], fr[0:n, :, 256 * t:256 * t + 256],
                                            zg_b[0:n].unsqueeze(1).to_broadcast([n, 2, 256]), ALU.add).then_inc(f_dve, 1)
                if tick == 20:
                    need(dve, f_pe, FRONT_PE, "cross", c)
                    v.tensor_tensor(wnew[:, :, :], fr[:, 0, :].rearrange("p (i k) -> p i k", i=IMGS),
                                    block_mask[:, :].unsqueeze(1).to_broadcast([128, IMGS, 128]),
                                    ALU.mult).then_inc(f_dve, 1)
                    need(dve, f_dve, FRONT_DVE, "masked", c)
                    v.tensor_tensor(wnew[:, :, :], wnew[:, :, :],
                                    bd_we[:, :].unsqueeze(1).to_broadcast([128, IMGS, 128]), ALU.add).then_inc(f_dve, 1)
                    v.tensor_scalar(bnew[:, :], fr[:, 1, 0:IMGS], be_col[:, 0:1], None, ALU.add).then_inc(f_dve, 1)
                if tick == 23:
                    need(dve, f_pe, FRONT_PE, "attn", c)
                    need(dve, f_pool, FRONT_POOL, "hb", c)
                    need(dve, f_pool, FRONT_POOL, "h1hold", c - 1)
                    v.tensor_tensor(h1_tok[:, :, :].rearrange("p t d -> p (t d)"), fr_tok,
                                    hb_tok[:, :, :].rearrange("p t d -> p (t d)"), ALU.add).then_inc(f_dve, 1)
                    need(dve, f_dve, FRONT_DVE, "h1", c)
                    stats(h1_tok, "2", c, f_dve, FRONT_DVE)
                if tick == 24:
                    normal(h1_tok, "2", c, f_dve, FRONT_DVE, f_pool, FRONT_POOL, x1_tok)

            def trig_steps(c, g):
                b = g % 2
                if g == 0:
                    need(dve, f_act, FRONT_ACT, "x2Tb", c)
                if g >= 2:
                    need(dve, t_act, TRIG_ACT, f"sin{g - 2}", c)
                else:
                    need(dve, t_act, TRIG_ACT, f"sin{NI - 2 + g}", c - 1)
                for j in range(NJ):
                    n = NI * j + g
                    i = v.tensor_scalar(kbuf[:, b, 1, j], x2T[:, :], lut_s[:, n:n + 1], lut_b[:, n:n + 1],
                                        ALU.mult, ALU.add)
                i.then_inc(t_dve, 1)

            def trig_wrap(c, g):
                b = g % 2
                need(dve, t_dve, TRIG_DVE, f"k{g}", c)
                v.tensor_scalar(kbuf[:, b, 0], kbuf[:, b, 1], float(LUT // 4), None, ALU.add).then_inc(t_dve, 1)
                need(dve, t_dve, TRIG_DVE, f"add{g}", c)
                v.tensor_scalar(kbuf[:, b], kbuf[:, b], LUT - 1, None, ALU.bitwise_and).then_inc(t_dve, 1)

            def back(tick, c):
                if tick == 0:
                    need(dve, t_pool, TRIG_POOL, "h2", c)
                    stats(h2_tok, "3", c, b_dve, BACK_DVE)
                if tick == 1:
                    normal(h2_tok, "3", c, b_dve, BACK_DVE, b_pool, BACK_POOL, x3_tok)
                s3v = s3[:, :, :, :].rearrange("p a i k -> p (a i) k")
                e3v = e3[:, :, :, :].rearrange("p a i k -> p (a i) k")
                if tick == 4:
                    need(dve, b_pe, BACK_PE, "s3", c)
                    v.tensor_tensor(s3[:, 0, :, 0:QA], bk[0:QA, 0, 0:IMGS * QA].rearrange("p (i k) -> p i k", i=IMGS),
                                    maskA[:, :].unsqueeze(1).to_broadcast([QA, IMGS, QA]), ALU.add).then_inc(b_dve, 1)
                    v.tensor_tensor(s3[0:QB, 1].rearrange("p (a i) k -> p a i k", a=2),
                                    bk[0:QB, 1:3, 0:HALF].rearrange("p a (i k) -> p a i k", i=2),
                                    maskB[:, :].unsqueeze(1).unsqueeze(1).to_broadcast([QB, 2, 2, N]),
                                    ALU.add).then_inc(b_dve, 1)
                    need(dve, b_dve, BACK_DVE, "mask3b", c)
                    v.tensor_reduce(m3[:, :], s3v, AX, ALU.max).then_inc(b_dve, 1)
                    need(dve, b_dve, BACK_DVE, "max3", c)
                    need(dve, b_pe, BACK_PE, "s3", c)
                    v.tensor_tensor(e3v, s3v, m3[:, :].unsqueeze(2).to_broadcast([QA, 2 * IMGS, N]),
                                    ALU.subtract).then_inc(b_dve, 1)
                if tick == 6:
                    need(dve, b_act, BACK_ACT, "e3", c)
                    v.tensor_reduce(sum3[:, :], e3v, AX, ALU.add).then_inc(b_dve, 1)
                    need(dve, b_dve, BACK_DVE, "sum3", c)
                    v.reciprocal(rec3[:, :], sum3[:, :]).then_inc(b_dve, 1)
                    need(dve, b_dve, BACK_DVE, "rec3", c)
                    v.tensor_tensor(e3v, e3v, rec3[:, :].unsqueeze(2).to_broadcast([QA, 2 * IMGS, N]),
                                    ALU.mult).then_inc(b_dve, 1)
                if tick == 9:
                    need(dve, b_pe, BACK_PE, "o3", c)
                    v.tensor_tensor(y_tok[:, :, :].rearrange("p t d -> p (t d)"), bk_flat[0:TT, 512:512 + NT * D],
                                    x3_tok[:, :, :].rearrange("p t d -> p (t d)"), ALU.add).then_inc(b_dve, 1)
                    need(dve, b_dve, BACK_DVE, "y3", c)
                    stats(y_tok, "y", c, b_dve, BACK_DVE)
                if tick == 10:
                    need(dve, b_dve, BACK_DVE, "lny", c)
                    for t in range(NT):
                        i = v.scalar_tensor_tensor(out=z_tok[:, t], in0=y_tok[:, t], scalar=mv["y"][:, t, 0:1],
                                                   in1=gamma_row[0:TT], op0=ALU.subtract, op1=ALU.mult)
                    i.then_inc(b_dve, 1)
                if tick == 11:
                    need(dve, b_dve, BACK_DVE, "zy", c)
                    need(dve, b_pool, BACK_POOL, "rstdy", c)
                    need_stored(dve, c)
                    for t in range(NT):
                        i = v.scalar_tensor_tensor(out=h3_tok[:, t], in0=z_tok[:, t], scalar=rstd["y"][:, t:t + 1],
                                                   in1=hb3_tok[:, t], op0=ALU.mult, op1=ALU.add)
                    i.then_inc(b_dve, 1)
                    need(dve, b_dve, BACK_DVE, "h3", c)
                    stats(h3_tok, "4", c, b_dve, BACK_DVE)
                if tick == 12:
                    normal(h3_tok, "4", c, b_dve, BACK_DVE, b_pool, BACK_POOL, x4_tok)
                for r in range(2 * IMGS):
                    if tick == 19 + r:
                        n = QS[r % 2][1]
                        need(dve, b_pe, BACK_PE, f"s4_{r}", c)
                        if r:
                            need(dve, b_pe, BACK_PE, f"mT_{r - 1}", c)
                        v.tensor_reduce(m4[0:n, :].rearrange("p (j g) -> p j g", j=NJ)[:, :, HD:HD + 2],
                                        bk[0:n, :, 0:2 * N].rearrange("p j (g k) -> p j g k", g=2), AX,
                                        ALU.max).then_inc(b_dve, 1)
                if tick == 27:
                    need(dve, b_pe, BACK_PE, f"mT_{2 * IMGS - 1}", c)
                    for g in range(2):
                        q = q4T[:, g].rearrange("p (i k) -> p i k", i=IMGS)
                        v.tensor_tensor(q, q, bk[:, :, 2 * N:3 * N], ALU.add).then_inc(b_dve, 1)

            def softmax_end(c):
                need(dve, b_pe, BACK_PE, "o4", c)
                o4 = bk_flat[0:TT, 0:2 * NT * 128].rearrange("p (h k) -> p h k", k=32)
                v.reciprocal(r4[:, :], o4[:, :, HD]).then_inc(b_dve, 1)
                need(dve, b_dve, BACK_DVE, "rsum", c)
                v.tensor_tensor(on_tok[:, :, :].rearrange("p t (h k) -> p (t h) k", k=HD), o4[:, :, 0:HD],
                                r4[:, :].unsqueeze(2).to_broadcast([TT, NT * H, HD]), ALU.mult).then_inc(b_dve, 1)
                need(dve, b_pe, BACK_PE, "wo", c)
                need(dve, b_pool, BACK_POOL, "x4b", c)
                v.tensor_tensor(y_tok[:, :, :].rearrange("p t d -> p (t d)"), bk_flat[0:TT, 1024:1024 + NT * D],
                                x4b_tok[:, :, :].rearrange("p t d -> p (t d)"), ALU.add).then_inc(b_dve, 1)
                need(dve, b_dve, BACK_DVE, "y4", c)
                stats(y_tok, "5", c, b_dve, BACK_DVE)
                need(dve, b_dve, BACK_DVE, "ln5", c)
                for t in range(NT):
                    i = v.scalar_tensor_tensor(out=z_tok[:, t], in0=y_tok[:, t], scalar=mv["5"][:, t, 0:1],
                                               in1=g5_row[0:TT], op0=ALU.subtract, op1=ALU.mult)
                i.then_inc(b_dve, 1)
                need(dve, b_dve, BACK_DVE, "z5", c)
                need(dve, b_pool, BACK_POOL, "rstd5", c)
                for t in range(NT):
                    i = v.scalar_tensor_tensor(out=z_tok[:, t], in0=z_tok[:, t], scalar=rstd["5"][:, t:t + 1],
                                               in1=b5_row[0:TT], op0=ALU.mult, op1=ALU.add)
                i.then_inc(b_dve, 1)

            def gate(c):
                gmax, gsum, gemax, grec, gsmax, gw = (gs[:, i] for i in range(6))

                def over(a):
                    return a.unsqueeze(2).to_broadcast([TT, NT, E])
                need(dve, b_pe, BACK_PE, "gate", c)
                v.tensor_tensor(gl[:, :, :], bk[0:TT, 2, 0:NT * E].rearrange("p (t e) -> p t e", t=NT),
                                gate_row[0:TT].unsqueeze(1).to_broadcast([TT, NT, E]), ALU.add).then_inc(b_dve, 1)
                need(dve, b_dve, BACK_DVE, "glog", c)
                v.tensor_reduce(gmax, gl[:, :, :], AX, ALU.max).then_inc(b_dve, 1)
                need(dve, b_dve, BACK_DVE, "gmax", c)
                v.tensor_tensor(gl[:, :, :], gl[:, :, :], over(gmax), ALU.subtract).then_inc(b_dve, 1)
                need(dve, b_act, BACK_ACT, "gexp", c)
                v.tensor_reduce(gsum, ge[:, :, :], AX, ALU.add).then_inc(b_dve, 1)
                v.tensor_reduce(gemax, ge[:, :, :], AX, ALU.max).then_inc(b_dve, 1)
                need(dve, b_dve, BACK_DVE, "gemax", c)
                v.reciprocal(grec, gsum).then_inc(b_dve, 1)
                v.tensor_tensor(gt[:, :, :], ge[:, :, :], over(gemax), ALU.is_equal).then_inc(b_dve, 1)
                need(dve, b_dve, BACK_DVE, "gmask", c)
                v.tensor_tensor(gt[:, :, :], gt[:, :, :], rank[:, :].unsqueeze(1).to_broadcast([TT, NT, E]),
                                ALU.mult).then_inc(b_dve, 1)
                need(dve, b_dve, BACK_DVE, "gscore", c)
                v.tensor_reduce(gsmax, gt[:, :, :], AX, ALU.max).then_inc(b_dve, 1)
                need(dve, b_dve, BACK_DVE, "gsmax", c)
                v.tensor_tensor(gt[:, :, :], gt[:, :, :], over(gsmax), ALU.is_equal).then_inc(b_dve, 1)
                v.tensor_tensor(gw, gemax, grec, ALU.mult).then_inc(b_dve, 1)
                need(dve, b_dve, BACK_DVE, "gw", c)
                v.tensor_tensor(coef[:, :, :], gt[:, :, :], over(gw), ALU.mult).then_inc(b_dve, 1)

            def experts(c):
                need(dve, b_pe, BACK_PE, "b2", c)
                v.tensor_tensor(acc[:, :, :].rearrange("p t d -> p (t d)"), bk_flat[0:TT, 1024:1024 + NT * D],
                                h3_tok[:, :, :].rearrange("p t d -> p (t d)"), ALU.add).then_inc(b_dve, 1)
                for e in range(E):
                    need(dve, b_dve, BACK_DVE, f"acc_{e - 1}" if e else "acc0", c)
                    need(dve, b_pe, BACK_PE, f"out_{e}", c)
                    for t in range(NT):
                        i = v.scalar_tensor_tensor(out=acc[:, t], in0=bk_flat[0:TT, 1024 + D * t:1024 + D * t + D],
                                                   scalar=coef[:, t, e:e + 1], in1=acc[:, t], op0=ALU.mult, op1=ALU.add)
                    i.then_inc(b_dve, 1)
            def need_stored(eng, c):
                if not isinstance(c, int) or c > 0:
                    eng.wait_ge(stored, 16 * c)

            dve.wait_ge(su_dve, SU_DVE)

            def body(i, embeds=True, fronts=True, trigs=True, backs=True):
                for tick in range(TICKS):
                    if backs:
                        back(tick, i - 1)
                    if fronts:
                        front(tick, i + 1)
                    if trigs and 2 <= tick < TICKS - 2:
                        if tick % 2 == 0:
                            trig_steps(i, tick // 2 + 1)
                        else:
                            trig_wrap(i, tick // 2 + 1)

                if fronts:
                    for g in range(2):
                        trig_steps(i + 1, g)
                        trig_wrap(i + 1, g)
                if backs:
                    softmax_end(i - 1)
                    gate(i - 1)
                if embeds:
                    embed_out(i + 2)
                if backs:
                    experts(i - 1)

            embed_out(0)
            body(-1, trigs=False, backs=False)
            body(0, backs=False)
            body(1)
            with dve.Fori(2, CHUNKS - 2) as i:
                body(i)
            body(CHUNKS - 2, embeds=False)
            body(CHUNKS - 1, embeds=False, fronts=False)
            body(CHUNKS, embeds=False, fronts=False, trigs=False)

        @block.scalar
        def _(act):
            a = nc.scalar
            act.wait_ge(su_pe, 1)
            pw = bk_flat[0:C * PS, 0:PS * D].rearrange("p (a q d) -> p a q d", q=2, d=D)
            a.activation(patch_w[0:C * PS], pw[:, :, 0], ACT.Copy).then_inc(su_act, 1)
            a.activation(odd_w.rearrange("p (a d) -> p a d", d=D), pw[:, :, 1], ACT.Copy).then_inc(su_act, 1)

            def evict_T(dst, flat, s):
                a.activation(dst[:, 0:4 * TT], flat[:, 0:4 * TT], ACT.Copy).then_inc(s, 1)
                a.activation(dst[:, 4 * TT:T], flat[:, 512:512 + TT], ACT.Copy).then_inc(s, 1)

            def halves(dst):
                return dst.rearrange("p (a k) -> p a k", a=2)

            def front(tick, c):
                if tick == 15:
                    need(act, f_pe, FRONT_PE, "h0", c)
                    need(act, f_dve, FRONT_DVE, "h1", c - 1)
                    a.activation(h0_tok[:, :, :].rearrange("p t d -> p (t d)"), fr_tok, ACT.Copy).then_inc(f_act, 1)
                if tick == 17:
                    need(act, f_pe, FRONT_PE, "x1T", c)
                    evict_T(x1T, fr_flat, f_act)
                if tick == 21:
                    need(act, f_pe, FRONT_PE, "pT", c)
                    a.activation(halves(pT[:, :]), fr[:, :, 0:HALF], ACT.Identity, bias=psi_b[:, 0:1]).then_inc(f_act, 1)
                if tick == 22:
                    need(act, f_pe, FRONT_PE, "qT", c)
                    need(act, f_dve, FRONT_DVE, "bnew", c)
                    for i in range(IMGS):
                        a.activation(qT[:, N * i:N * i + N], fr[:, i // 2, N * (i % 2):N * (i % 2) + N], ACT.Identity,
                                     bias=bnew[:, i:i + 1]).then_inc(f_act, 1)
                if tick == 29:
                    need(act, f_pe, FRONT_PE, "x2T", c)
                    need(act, t_dve, TRIG_DVE, f"k{NI - 1}", c - 1)
                    evict_T(x2T, fr_flat, f_act)

            def trig_step(tick, c):
                g, cs = tick // 2, tick % 2
                s = ("mmcos", "mmsin")[cs]
                need(act, t_dve, TRIG_DVE, f"and{g}", c)
                if g:
                    need(act, t_pe, TRIG_PE, f"{s}{g - 1}", c)
                else:
                    need(act, t_pe, TRIG_PE, f"{s}{NI - 1}", c - 1)
                    need(act, b_pe, BACK_PE, f"pv_{IMGS - 1}", c - 2)
                a.activation(trig[:, cs], kbuf[:, g % 2, cs], ACT.Sin, bias=MINUS_PI, scale=FROM_LUT).then_inc(t_act, 1)

            def trig_end(c):
                need(act, t_pe, TRIG_PE, f"mmsin{NI - 1}", c)
                a.activation(halves(csT[:, :]), acc_ps[:, :, 0:HALF], ACT.Copy).then_inc(t_act, 1)
                need(act, t_pe, TRIG_PE, "proj", c)
                need(act, b_dve, BACK_DVE, "h3", c - 1)
                a.activation(silu_tok[:, :, :].rearrange("p t d -> p (t d)"), acc_flat[0:TT, 0:NT * D],
                             ACT.Silu).then_inc(t_act, 1)

            def back(tick, c):
                if tick == 2:
                    need(act, b_pe, BACK_PE, "x3T", c)
                    evict_T(xT, bk_flat, b_act)
                if tick == 3:
                    need(act, b_pe, BACK_PE, "q3", c)
                    a.activation(halves(q3T), bk[:, 0:2, 0:HALF], ACT.Identity, bias=bqq[:, 0:1]).then_inc(b_act, 1)
                    need(act, b_pe, BACK_PE, "k3", c)
                    a.activation(halves(k3T), bk[:, 2:4, 0:HALF], ACT.Identity, bias=bkk[:, 0:1]).then_inc(b_act, 1)
                if tick == 4:
                    need(act, b_pe, BACK_PE, "v3a", c)
                    a.activation(v3[:, 0].rearrange("p i d -> p (i d)"), bk[0:QA, 3, :], ACT.Copy).then_inc(b_act, 1)
                if tick == 5:
                    need(act, b_pe, BACK_PE, "v3b", c)
                    a.activation(v3[0:QB, 1].rearrange("p i d -> p (i d)"), bk[0:QB, 3, :], ACT.Copy).then_inc(b_act, 1)
                    need(act, b_dve, BACK_DVE, "sub3", c)
                    e3f = e3[:, :, :, :].rearrange("p a i k -> p (a i k)")
                    a.activation(e3f, e3f, ACT.Exp).then_inc(b_act, 1)
                if tick == 7:
                    need(act, b_pe, BACK_PE, "pTa", c)
                    a.activation(halves(pTa), bk[0:QA, 0:2, 0:HALF], ACT.Copy).then_inc(b_act, 1)
                    a.activation(pTb[:, :], bk[0:QB, 2, 0:IMGS * QB], ACT.Copy).then_inc(b_act, 1)
                if tick == 8:
                    need(act, b_pe, BACK_PE, "oT", c)
                    a.activation(halves(oT), bk[:, 2:4, 0:HALF], ACT.Identity, bias=bv3c[:, 0:1]).then_inc(b_act, 1)
                if tick == 13:
                    need(act, b_pe, BACK_PE, "x4T", c)
                    evict_T(xT, bk_flat, b_act)
                if tick == 14:
                    need(act, b_pe, BACK_PE, "q4", c)
                    for g in range(2):
                        a.activation(halves(q4T[:, g]), bk[:, 2 * g:2 * g + 2, 0:HALF], ACT.Identity,
                                     bias=bq4c[:, g:g + 1]).then_inc(b_act, 1)
                if tick == 15:
                    need(act, b_pe, BACK_PE, "k4", c)
                    for g in range(2):
                        a.activation(halves(k4T[:, g]), bk[:, 2 * g:2 * g + 2, 0:HALF], ACT.Identity,
                                     bias=bk4c[:, g:g + 1]).then_inc(b_act, 1)
                if tick == 16:
                    need(act, b_pe, BACK_PE, "v4", c)
                    for t, (_, n) in enumerate(QS):
                        a.activation(v4[0:n, t, :, :, 0:HD].rearrange("p i h d -> p (i h) d"),
                                     bk[0:n, t, :].rearrange("p (k d) -> p k d", d=HD), ACT.Copy).then_inc(b_act, 1)

            def pv_out(i, c):
                need(act, b_pe, BACK_PE, f"pv_{i}", c)
                a.activation(o4T[:, :, N * i:N * i + N], acc_ps[:, i % 2, 0:2 * N].rearrange("p (g k) -> p g k", g=2),
                             ACT.Copy).then_inc(b_act, 1)

            def gelu(e, c):
                for f in range(FC):
                    need(act, b_pe, BACK_PE, f"hid{f}_{e}", c)
                    if f == 0 and e >= 2:
                        need(act, b_pe, BACK_PE, f"out_{e - 2}", c)
                    a.activation(halves(hid[:, e % 2, f]), hid_ps[f % 2][:, :, 0:HALF],
                                 ACT.Gelu_apprx_tanh, bias=b1c[:, e, f:f + 1]).then_inc(b_act, 1)

            def back_end(c):
                for i in range(IMGS):
                    for r in range(4):
                        t, g = r // 2, r % 2
                        n = QS[t][1]
                        need(act, b_pe, BACK_PE, f"st{r}_{i}", c)
                        if i >= 2:
                            need(act, b_pe, BACK_PE, f"pv_{i - 2}", c)
                        a.activation(p4[i % 2][0:n, t, g].rearrange("p (a j) k -> p a (j k)", a=2),
                                     bk[0:n, 2 * g:2 * g + 2, 0:2 * N], ACT.Exp, scale=float(HD) ** -0.5).then_inc(b_act, 1)
                        if r == 1 and i:
                            pv_out(i - 1, c)
                pv_out(IMGS - 1, c)
                need(act, b_pe, BACK_PE, "onT", c)
                evict_T(onT, bk_flat, b_act)
                need(act, b_pe, BACK_PE, "tT", c)
                evict_T(xT, bk_flat, b_act)
                need(act, b_dve, BACK_DVE, "gsub", c)
                a.activation(ge[:, :, :], gl[:, :, :], ACT.Exp).then_inc(b_act, 1)
                gelu(0, c)
                need(act, b_pe, BACK_PE, "coefT", c)
                a.activation(coefT[:, 0:4 * TT], bk_flat[0:E, 1024:1024 + 4 * TT], ACT.Copy).then_inc(b_act, 1)
                a.activation(coefT[:, 4 * TT:T], bk_flat[0:E, 1536:1536 + TT], ACT.Copy).then_inc(b_act, 1)
                for e in range(1, E):
                    gelu(e, c)

            act.wait_ge(loaded_w, LOADED)
            act.wait_ge(su_dve, SU_DVE)

            def body(i, fronts=True, trigs=True, backs=True):
                for tick in range(TICKS):
                    if trigs:
                        trig_step(tick, i)
                    if backs:
                        back(tick, i - 1)
                    if fronts:
                        front(tick, i + 1)
                if trigs:
                    trig_end(i)
                if backs:
                    back_end(i - 1)

            body(-1, trigs=False, backs=False)
            body(0, backs=False)
            body(1)
            with act.Fori(2, CHUNKS - 1) as i:
                body(i)
            body(CHUNKS - 1, fronts=False)
            body(CHUNKS, fronts=False, trigs=False)

        @block.tensor
        def _(pe):
            mm, tr = nc.tensor.matmul, nc.tensor.transpose
            pe.wait_ge(loaded_w, LOADED)
            pe.wait_ge(su_pool, POOL_SETUP)
            pe.wait_ge(su_dve, 16)
            for p2 in range(PS):
                i = tr(bk_flat[0:C * PS, D * p2:D * p2 + D], wt[:, p2].rearrange("d c a -> d (c a)"), ident[:, :])
            i.then_inc(su_pe, 1)
            pe.wait_ge(su_act, 2)
            tr(bk[:, 0, 0:128], su[0][:, :], ident[:, :])
            tr(bk[:, 0, 128:256], zg_w[:, 0:128], ident[:, :])
            tr(bk[:, 0, 256:384], su[1][:, :], ident[:, :]).then_inc(su_pe, 1)
            pe.wait_ge(su_dve, 19)
            mm(bk[:, 1, 0:128], su[3][:, :], su[3][:, :], start=True, stop=True)
            mm(bk[:, 1, 128:256], bd_we[:, :], su[4][:, :], start=True, stop=True).then_inc(su_pe, 1)
            mm(bk[:, 1, 256:257], bd_we[:, :], su_col[:, 4:5], start=True, stop=True).then_inc(su_pe, 1)
            pe.wait_ge(su_dve, 25)
            mm(bk[:, 2, 0:128], su[6][:, :], su[5][:, :], start=True, stop=True).then_inc(su_pe, 1)
            mm(bk[:, 2, 128:256], su[7][:, :], su[5][:, :], start=True, stop=False)
            mm(bk[:, 2, 128:256], su[1][:, :], su[3][:, :], start=False, stop=True).then_inc(su_pe, 1)
            mm(bk[:, 2, 256:384], su[0][:, :], wo4[:, :], start=True, stop=True).then_inc(su_pe, 1)
            for k in range(4):
                i = tr(bk[:, 3, NW * k:NW * k + NW], lutW[:, k], ident[0:NW, 0:NW])
            i.then_inc(su_pe, 1)

            def transposed(src, flat):
                for t in range(NT):
                    at = TT * t if t < 4 else 512
                    i = tr(flat[:, at:at + TT], src[:, t], ident[0:TT, 0:TT])
                return i

            def tokens(src, flat):
                for t in range(NT):
                    i = tr(flat[0:TT, D * t:D * t + D], src[:, TT * t:TT * t + TT], ident[:, :])
                return i

            def embed(m, c):
                if m == 0:
                    need(pe, f_act, FRONT_ACT, "x2Tb", c - 1)
                pe.wait_ge(x_loaded[m % 2], 96 * (2 * c + m // 2 + 1))
                for k in range(PS // 2):
                    i = mm(fr[:, m // 2, NPATCH * (m % 2):NPATCH * (m % 2) + NPATCH], patch_w[:, k],
                           patches[:, m % 2, :, 2 * k:IW - 1:PS], start=(k == 0), stop=(k == PS // 2 - 1))
                i.then_inc(e_pe, 1)

            def front(tick, c):
                if tick == 15:
                    need(pe, e_dve, EMB_DVE, "emb23", c)
                    tokens(h0T[:, :, :].rearrange("d i n -> d (i n)"), fr_flat).then_inc(f_pe, 1)
                if tick == 17:
                    need(pe, f_dve, FRONT_DVE, "x1", c)
                    transposed(x1_tok, fr_flat).then_inc(f_pe, 1)
                for r in range(2):
                    if tick == 18 + r:
                        if r:
                            need(pe, f_dve, FRONT_DVE, "zg0b", c)
                        else:
                            need(pe, f_act, FRONT_ACT, "x1Tb", c)
                        for k in range(2):
                            for t, (q0, n) in enumerate(QS):
                                at = N * (2 * r + k) + q0
                                i = mm(fr[0:n, k, 256 * t:256 * t + 256], x1T[:, at:at + n], zg_w[:, :],
                                       start=True, stop=True)
                        i.then_inc(f_pe, 1)
                if tick == 20:
                    need(pe, f_dve, FRONT_DVE, "zg1b", c)
                    for i in range(IMGS):
                        for t, (_, n) in enumerate(QS):
                            mm(fr[:, 0, 128 * i:128 * i + 128], zg[0:n, t, i, 0:128], zg[0:n, t, i, 128:256],
                               start=(t == 0), stop=(t == 1))
                    for i in range(IMGS):
                        for t, (_, n) in enumerate(QS):
                            last = mm(fr[:, 1, i:i + 1], zg[0:n, t, i, 128:256], ones[0:n, 0:1], start=(t == 0),
                                      stop=(t == 1))
                    last.then_inc(f_pe, 1)
                if tick == 21:
                    need(pe, f_dve, FRONT_DVE, "bnew", c)
                    for k in range(2):
                        i = mm(fr[:, k, 0:HALF], psi_w[:, :], x1T[:, HALF * k:HALF * k + HALF], start=True, stop=True)
                    i.then_inc(f_pe, 1)
                if tick == 22:
                    need(pe, f_act, FRONT_ACT, "pT", c)
                    for i in range(IMGS):
                        last = mm(fr[:, i // 2, N * (i % 2):N * (i % 2) + N], wnew[:, i], pT[:, N * i:N * i + N],
                                  start=True, stop=True)
                    last.then_inc(f_pe, 1)
                if tick == 23:
                    need(pe, f_act, FRONT_ACT, "qT3", c)
                    for t in range(NT):
                        i = mm(fr_flat[0:TT, D * t:D * t + D], qT[:, TT * t:TT * t + TT], wh[:, :], start=True, stop=True)
                    i.then_inc(f_pe, 1)
                if tick == 25:
                    need(pe, f_dve, FRONT_DVE, "x2", c)
                    transposed(x1_tok, fr_flat).then_inc(f_pe, 1)

            def trig_step(tick, c):
                g, cs = tick // 2, tick % 2
                s = ("cos", "sin")[cs]
                if tick == 0:
                    need(pe, t_act, TRIG_ACT, "silu", c - 1)
                    need(pe, b_act, BACK_ACT, f"gelu{FC - 1}_{E - 1}", c - 2)
                need(pe, t_act, TRIG_ACT, f"{s}{g}", c)
                for half in range(2):
                    for j in range(NJ):
                        at = ((NI * j + g) * 2 + cs) * 32
                        i = mm(acc_ps[32 * j:32 * j + 32, half, 0:HALF], trig_w[:, at:at + 32],
                               trig[:, cs, j, HALF * half:HALF * half + HALF],
                               start=(g == 0 and cs == 0), stop=(g == NI - 1 and cs == 1))
                i.then_inc(t_pe, 1)

            def trig_end(c):
                need(pe, t_act, TRIG_ACT, "csT", c)
                for t in range(NT):
                    i = mm(acc_flat[0:TT, D * t:D * t + D], csT[:, TT * t:TT * t + TT], proj_w[:, :], start=True, stop=True)
                i.then_inc(t_pe, 1)

            def back(tick, c):
                if tick == 2:
                    need(pe, b_dve, BACK_DVE, "x3", c)
                    transposed(x3_tok, bk_flat).then_inc(b_pe, 1)
                if tick == 3:
                    need(pe, b_act, BACK_ACT, "x3Tb", c)
                    need(pe, b_dve, BACK_DVE, f"acc_{E - 1}", c - 1)
                    for w, k0 in ((wqq, 0), (wkk, 2)):
                        for k in range(2):
                            i = mm(bk[:, k0 + k, 0:HALF], w[:, :, :].rearrange("p a b -> p (a b)"),
                                   xT[:, HALF * k:HALF * k + HALF], start=True, stop=True)
                        i.then_inc(b_pe, 1)
                if tick == 4:
                    need(pe, b_act, BACK_ACT, "k3", c)
                    for i in range(IMGS):
                        at = N * i
                        mm(bk[0:QA, 0, QA * i:QA * i + QA], q3T[0:DA, at:at + QA], k3T[0:DA, at:at + QA],
                           start=True, stop=True)
                        last = mm(bk[0:QB, 1 + i // 2, N * (i % 2):N * (i % 2) + N], q3T[DA:128, at + QA:at + N],
                                  k3T[DA:128, at:at + N], start=True, stop=True)
                    last.then_inc(b_pe, 1)
                for t, (q0, n) in enumerate(QS):
                    if tick == 4 + t:
                        if t:
                            need(pe, b_act, BACK_ACT, "v3a", c)
                        for i in range(IMGS):
                            last = mm(bk[0:n, 3, D * i:D * i + D], xT[:, N * i + q0:N * i + q0 + n], wv3[:, :],
                                      start=True, stop=True)
                        last.then_inc(b_pe, 1)
                if tick == 7:
                    need(pe, b_dve, BACK_DVE, "p3", c)
                    for i in range(IMGS):
                        at = N * (i % 2)
                        tr(bk[0:QA, i // 2, at:at + QA], e3[:, 0, i, 0:QA], ident[0:QA, 0:QA])
                        tr(bk[0:QA, i // 2, at + QA:at + N], e3[0:QB, 1, i, 0:QA], ident[0:QB, 0:QB])
                        last = tr(bk[0:QB, 2, QB * i:QB * i + QB], e3[0:QB, 1, i, QA:N], ident[0:QB, 0:QB])
                    last.then_inc(b_pe, 1)
                if tick == 8:
                    need(pe, b_act, BACK_ACT, "pTb", c)
                    for i in range(IMGS):
                        at = N * (i % 2)
                        mm(bk[:, 2 + i // 2, at:at + N], v3[:, 0, i], pTa[:, N * i:N * i + N], start=True, stop=False)
                        last = mm(bk[:, 2 + i // 2, at + QA:at + N], v3[0:QB, 1, i], pTb[:, QB * i:QB * i + QB],
                                  start=False, stop=True)
                    last.then_inc(b_pe, 1)
                if tick == 9:
                    need(pe, b_act, BACK_ACT, "oT", c)
                    tokens(oT, bk_flat[:, 512:]).then_inc(b_pe, 1)
                if tick == 13:
                    need(pe, b_dve, BACK_DVE, "x4", c)
                    transposed(x4_tok, bk_flat).then_inc(b_pe, 1)
                for k, (w, ready) in enumerate(((wq4, "x4Tb"), (wk4, "q4b"))):
                    if tick == 14 + k:
                        need(pe, b_act, BACK_ACT, ready, c)
                        for g in range(2):
                            for half in range(2):
                                i = mm(bk[:, 2 * g + half, 0:HALF], w[:, g].rearrange("p j k -> p (j k)"),
                                       xT[:, HALF * half:HALF * half + HALF], start=True, stop=True)
                        i.then_inc(b_pe, 1)
                if tick == 16:
                    need(pe, b_act, BACK_ACT, "k4b", c)
                    for t, (q0, n) in enumerate(QS):
                        for i in range(IMGS):
                            last = mm(bk[0:n, t, D * i:D * i + D], xT[:, N * i + q0:N * i + q0 + n], wv4[:, :],
                                      start=True, stop=True)
                    last.then_inc(b_pe, 1)
                for r in range(2 * IMGS):
                    q0, n = QS[r % 2]
                    at = N * (r // 2)
                    if tick == 19 + r:
                        if r == 0:
                            need(pe, b_act, BACK_ACT, "v4b", c)
                            need(pe, b_pool, BACK_POOL, "kM", c)
                        for g in range(2):
                            for j in range(NJ):
                                i = mm(bk[0:n, j, N * g:N * g + N], q4T[:, g, at + q0:at + q0 + n],
                                       kM[:, NJ * g + j, at:at + N], start=True, stop=True)
                        i.then_inc(b_pe, 1)
                    if tick == 20 + r:
                        need(pe, b_dve, BACK_DVE, f"s4_{r}", c)
                        tr(bk[:, r // 2, 2 * N + q0:2 * N + q0 + n], m4[0:n], ident[0:n, 0:n]).then_inc(b_pe, 1)

            def scores(r, i, c):
                t, g = r // 2, r % 2
                k0, n = QS[t]
                at = N * i
                if i or t:
                    need(pe, b_act, BACK_ACT, f"exp{r - 2}_{i}" if t else f"exp{r + 2}_{i - 1}", c)
                else:
                    need(pe, b_dve, BACK_DVE, "qm1", c)
                for j in range(NJ):
                    k = mm(bk[0:n, 2 * g + j // 2, N * (j % 2):N * (j % 2) + N], kM[:, NJ * g + j, at + k0:at + k0 + n],
                           q4T[:, g, at:at + N], start=True, stop=True)
                k.then_inc(b_pe, 1)

            def weighted(i, c, trig_c):
                need(pe, b_act, BACK_ACT, f"exp3_{i}", c)
                if i >= 2:
                    need(pe, b_act, BACK_ACT, f"pv_{i - 2}", c)
                else:
                    need(pe, t_act, TRIG_ACT, "silu", trig_c)
                for g in range(2):
                    for t, (_, n) in enumerate(QS):
                        for j in range(NJ):
                            last = mm(acc_ps[32 * j:32 * j + 32, i % 2, N * g:N * g + N], v4[0:n, t, i, NJ * g + j],
                                      p4[i % 2][0:n, t, g, j], start=(t == 0), stop=(t == 1))
                last.then_inc(b_pe, 1)

            def hidden(f, e, c):
                if f >= 2:
                    need(pe, b_act, BACK_ACT, f"gelu{f - 2}_{e}", c)
                elif e:
                    need(pe, b_act, BACK_ACT, f"gelu{f + 2}_{e - 1}", c)
                for half in range(2):
                    i = mm(hid_ps[f % 2][:, half, 0:HALF], w1[:, e, 128 * f:128 * f + 128],
                           xT[:, HALF * half:HALF * half + HALF], start=True, stop=True)
                i.then_inc(b_pe, 1)

            def expert_out(e, c):
                need(pe, b_act, BACK_ACT, f"gelu{FC - 1}_{e}", c)
                need(pe, b_dve, BACK_DVE, f"acc_{e - 1}" if e else "acc0", c)
                for t in range(NT):
                    for f in range(FC):
                        i = mm(bk_flat[0:TT, 1024 + D * t:1024 + D * t + D], hid[:, e % 2, f, TT * t:TT * t + TT],
                               w2[:, e, f], start=(f == 0), stop=(f == FC - 1))
                i.then_inc(b_pe, 1)

            def back_end(c, trig_c, fill):
                for i in range(IMGS):
                    for r in range(4):
                        scores(r, i, c)
                        if i == 0 and r == 0:
                            fill(0)
                        if r == 1 and i:
                            weighted(i - 1, c, trig_c)
                fill(1)
                weighted(IMGS - 1, c, trig_c)
                need(pe, b_act, BACK_ACT, f"pv_{IMGS - 1}", c)
                for t in range(NT):
                    for g in range(2):
                        i = tr(bk_flat[0:TT, 128 * (2 * t + g):128 * (2 * t + g) + 128], o4T[:, g, TT * t:TT * t + TT],
                               ident[:, :])
                i.then_inc(b_pe, 1)
                fill(2)
                need(pe, b_dve, BACK_DVE, "on", c)
                transposed(on_tok, bk_flat).then_inc(b_pe, 1)
                need(pe, b_act, BACK_ACT, "onTb", c)
                for t in range(NT):
                    i = mm(bk_flat[0:TT, 1024 + D * t:1024 + D * t + D], onT[:, TT * t:TT * t + TT], wo4[:, :],
                           start=True, stop=True)
                i.then_inc(b_pe, 1)
                fill(3)
                need(pe, b_dve, BACK_DVE, "t5", c)
                transposed(z_tok, bk_flat).then_inc(b_pe, 1)
                need(pe, b_act, BACK_ACT, "tTb", c)
                for t in range(NT):
                    i = mm(bk[0:TT, 2, E * t:E * t + E], xT[:, TT * t:TT * t + TT], gate_w[:, :], start=True, stop=True)
                i.then_inc(b_pe, 1)
                for f in range(FC):
                    hidden(f, 0, c)
                need(pe, b_dve, BACK_DVE, "coef", c)
                for t in range(NT):
                    at = 1024 + (TT * t if t < 4 else 512)
                    i = tr(bk_flat[0:E, at:at + TT], coef[:, t], ident[0:TT, 0:TT])
                i.then_inc(b_pe, 1)
                for f in range(FC):
                    if f == 2:
                        need(pe, b_act, BACK_ACT, "coefTb", c)
                        for t in range(NT):
                            i = mm(bk_flat[0:TT, 1024 + D * t:1024 + D * t + D], coefT[:, TT * t:TT * t + TT], b2s[:, :],
                                   start=True, stop=True)
                        i.then_inc(b_pe, 1)
                    hidden(f, 1, c)
                expert_out(0, c)
                for e in range(2, E):
                    for f in range(FC):
                        hidden(f, e, c)
                    expert_out(e - 1, c)
                expert_out(E - 1, c)

            pe.wait_ge(copied_w, 16)
            pe.wait_ge(su_dve, SU_DVE)

            def body(i, embeds=True, fronts=True, trigs=True, backs=True):
                for tick in range(TICKS):
                    if backs:
                        back(tick, i - 1)
                    if fronts:
                        front(tick, i + 1)
                    if trigs:
                        trig_step(tick, i)

                def fill(k):
                    if k == 0 and trigs:
                        trig_end(i)
                    if k and embeds:
                        for m in ((0,), (1,), (2, 3))[k - 1]:
                            embed(m, i + 2)
                if backs:
                    back_end(i - 1, i if trigs else i - 1, fill)
                else:
                    for k in range(4):
                        fill(k)

            for m in range(IMGS):
                embed(m, 0)
            body(-1, trigs=False, backs=False)
            body(0, backs=False)
            body(1)
            with pe.Fori(2, CHUNKS - 2) as i:
                body(i)
            body(CHUNKS - 2, embeds=False)
            body(CHUNKS - 1, embeds=False, fronts=False)
            body(CHUNKS, embeds=False, fronts=False, trigs=False)


SU_DVE = 46
POOL_SETUP = 6 + E + 9

_INS = ['x', 'cls_tok', 'L0_tok_W', 'L0_tok_b', 'L0_tok_cls_token', 'L0_tok_pos_emb', 'L0_attn_W_phi', 'L0_attn_b_phi',
        'L0_attn_W_e', 'L0_attn_b_e', 'L0_attn_W_g', 'L0_attn_g_bias', 'L0_attn_W_psi', 'L0_attn_b_psi', 'L0_attn_W_h',
        'L0_attn_h_bias', 'L0_ffn_W', 'L0_ffn_B_param', 'L0_ffn_attn_cos', 'L0_ffn_attn_sin', 'L0_ffn_proj_cos_w',
        'L0_ffn_proj_sin_w', 'L1_attn_Wq', 'L1_attn_bq', 'L1_attn_Wk', 'L1_attn_bk', 'L1_attn_Wv', 'L1_attn_bv',
        'L1_attn_gamma', 'L1_attn_beta', 'L1_ffn_ln1_g', 'L1_ffn_ln1_b', 'L1_ffn_Wq', 'L1_ffn_bq', 'L1_ffn_Wk',
        'L1_ffn_bk', 'L1_ffn_Wv', 'L1_ffn_bv', 'L1_ffn_Wo', 'L1_ffn_bo', 'L1_ffn_gate_W', 'L1_ffn_gate_b', 'L1_ffn_W1',
        'L1_ffn_b1', 'L1_ffn_W2', 'L1_ffn_b2']


def kernel(**inputs):
    import numpy as _np
    import concourse.bacc as _bacc
    from concourse import mybir as _mybir
    from concourse.bass_utils import run_bass_kernel_spmd as _run

    nc = _bacc.Bacc("TRN2", target_bir_lowering=False, num_devices=1)
    arrays, args = {}, []
    for name in _INS:
        a = _np.ascontiguousarray(inputs[name])
        arrays[f"in_{name}_dram"] = a
        args.append(nc.dram_tensor(f"in_{name}_dram", a.shape, _mybir.dt.from_np(a.dtype), kind="ExternalInput").ap())
    args.append(nc.dram_tensor("out_0_dram", (B, N, D), F32, kind="ExternalOutput").ap())
    vit_tower(nc, *args)
    r = _run(nc, [arrays], core_ids=[0])
    return r.results[0]["out_0_dram"]
```

```python
from contextlib import ExitStack

import numpy as np

import concourse.bass as bass
from concourse import mybir

ALU = mybir.AluOpType
ACT = mybir.ActivationFunctionType
F32 = mybir.dt.float32
I32 = mybir.dt.int32
I16 = mybir.dt.int16
AX = mybir.AxisListType.X

B, C, IH, IW = 64, 3, 176, 208
PS = 16
PW, PH = IH // PS, IW // PS
NPATCH = PW * PH
N = NPATCH + 2
D = 128
IMGS = 4
CHUNKS = B // IMGS
T = IMGS * N
HALF = T // 2
TT = 116
NT = T // TT
QA = 73
QB = N - QA
QS = ((0, QA), (QA, QB))
H, HD = 8, 16
E, FF = 8, 512
FC = FF // 128
DA = 64
NW = 64
NJ = 4
NI = NW // NJ
LUT = 1024
EPS = 1e-5
MASKED = -1e30
MAGIC = 12582912.0
LR_SCALE = H / (N * D)
TO_LUT = float(np.float32(LUT / (2.0 * np.pi)))
FROM_LUT = float(np.float32(2.0 * np.pi / LUT))
KB = 4
ROW = 2 * D + 2
MT = 256
TOKENS = B * N
REGION = TOKENS + MT
TILES = (TOKENS + E * (MT - 1)) // MT
TILES += -TILES % 4
NOWHERE = 16384
MINUS_PI = -3.1415925

TICKS = 2 * NI
STEP_TICKS = (1, 4, 8, 9, 12, 13, 17, 18, 21, 23, 25, 27)
EMB_PE = tuple(f"emb{m}" for m in range(IMGS))
EMB_DVE = ("cls", "emb01", "emb23")
FRONT_PE = ("h0", "x1T", "zg0", "zg1", "cross", "pT", "qT", "attn", "x2T")
FRONT_ACT = ("h0", "x1Ta", "x1Tb", "pT", "qT0", "qT1", "qT2", "qT3", "x2Ta", "x2Tb")
FRONT_DVE = ("bn1", "ln1", "x1", "zg0a", "zg0b", "zg1a", "zg1b", "masked", "wnew", "bnew", "h1", "bn2", "ln2", "x2")
FRONT_POOL = ("eps1", "rstd1", "hb", "eps2", "rstd2", "h1hold")
TRIG_DVE = tuple(f"{s}{g}" for g in range(NI) for s in ("k", "add", "and"))
TRIG_ACT = (*(f"{s}{g}" for g in range(NI) for s in ("cos", "sin")), "csT", "silu")
TRIG_PE = (*(f"{s}{g}" for g in range(NI) for s in ("mmcos", "mmsin")), "proj")
TRIG_POOL = ("h2",)
NORM_DVE = ("bn3", "ln3", "x3")
NORM_POOL = ("eps3", "rstd3", "hb3")


def softmax_steps(name):
    steps = []
    for i in range(IMGS):
        steps += [f"{name}0_{i}", f"{name}1_{i}"] + ([f"pv_{i - 1}"] if i else []) + [f"{name}2_{i}", f"{name}3_{i}"]
    return (*steps, f"pv_{IMGS - 1}")


BACK_PE = ("x3T", "q3", "k3", "s3", "v3a", "v3b", "pTa", "oT", "o3", "x4T", "q4", "k4", "v4",
           *(f"{s}_{r}" for r in range(2 * IMGS) for s in ("s4a", "s4b", "mT")), *softmax_steps("st"), "o4", "onT", "wo")
BACK_ACT = ("x3Ta", "x3Tb", "q3", "k3", "v3a", "v3b", "e3", "pTa", "pTb", "oT", "x4Ta", "x4Tb",
            "q4a", "q4b", "k4a", "k4b", "v4a", "v4b", *softmax_steps("exp"), "onTa", "onTb")
BACK_DVE = ("mask3a", "mask3b", "max3", "sub3", "sum3", "rec3", "p3", "y3",
            "bny", "lny", "zy", "h3", "bn4", "ln4", "x4",
            *(f"s4{h}_{r}" for r in range(2 * IMGS) for h in "ab"), "qm0", "qm1", "rsum", "on")
BACK_POOL = ("epsy", "rstdy", "eps4", "rstd4", "x4b", "kMa", "kMb")
ROUTE_PE = ("tT", "gate", "rank")
ROUTE_ACT = ("tTa", "tTb", "gexp")
ROUTE_DVE = ("y4", "bn5", "ln5", "z5", "t5", "glog", "gmax", "gsub",
             "gsum", "gemax", "grec", "gmask", "gscore", "gsmax", "goh", "gw",
             "slots", "slot", "pos", "index", "token", "next", "run")
ROUTE_POOL = ("eps5", "rstd5")


def value(steps, name, chunk):
    return chunk * len(steps) + steps.index(name) + 1


def need(engine, sem, steps, name, chunk):
    v = value(steps, name, chunk)
    if not isinstance(v, int) or v > 0:
        engine.wait_ge(sem, v)


def vit_tower(nc, x, cls_tok, tok_W, tok_b, tok_cls, tok_pos, W_phi, b_phi, W_e, b_e, W_g, g_bias, W_psi, b_psi,
              W_h, h_bias, ffn_W, ffn_B, ffn_cos, ffn_sin, pcos, psin, Wq3, bq3, Wk3, bk3, Wv3, bv3, gamma3, beta3,
              ln_g, ln_b, Wq4, bq4, Wk4, bk4, Wv4, bv4, Wo4, bo4, gate_W, gate_b, W1, b1, W2, b2, out, expert_rows,
              b1_cols):
    with ExitStack() as ctx:
        def sb(name, shape, dt=F32):
            return ctx.enter_context(nc.sbuf_tensor(name, shape, dt))

        def sem(name):
            return ctx.enter_context(nc.semaphore(name))

        ident = sb("ident", [128, 128])
        ones = sb("ones", [128, 128])
        block_mask = sb("block_mask", [128, 128])
        maskA = sb("maskA", [QA, QA])
        maskB = sb("maskB", [QB, N])
        rank = sb("rank", [TT, E])
        head_mask = sb("head_mask", [128, NJ])
        head_neg = sb("head_neg", [128, 2, NJ])
        patch_w = sb("patch_w", [2 * C * PS, PS // 2, D])
        addend = sb("addend", [128, N])
        zg_w = sb("zg_w", [D, 256])
        zg_b = sb("zg_b", [128, 256])
        bd_we = sb("bd_we", [128, 128])
        be_col = sb("be_col", [128, 1])
        psi_w = sb("psi_w", [D, 128])
        psi_b = sb("psi_b", [128, 1])
        wh = sb("wh", [128, D])
        hbias_row = sb("hbias_row", [128, D])
        lut_s = sb("lut_s", [D, NW])
        lut_b = sb("lut_b", [D, NW])
        trig_w = sb("trig_w", [D, NW * 64 + 64])
        proj_w = sb("proj_w", [128, D])
        wqq = sb("wqq", [D, 2, DA])
        wkk = sb("wkk", [D, 2, DA])
        bqq = sb("bqq", [128, 1])
        bkk = sb("bkk", [128, 1])
        wv3 = sb("wv3", [D, D])
        bv3c = sb("bv3c", [D, 1])
        gamma_row = sb("gamma_row", [128, D])
        beta_row = sb("beta_row", [128, D])
        wq4 = sb("wq4", [D, 2, NJ, 32])
        wk4 = sb("wk4", [D, 2, NJ, 32])
        bq4c = sb("bq4c", [128, 2])
        bk4c = sb("bk4c", [128, 2])
        wv4 = sb("wv4", [D, D])
        wo4 = sb("wo4", [D, D])
        bo_row = sb("bo_row", [128, D])
        g5_row = sb("g5_row", [128, D])
        b5_row = sb("b5_row", [128, D])
        gate_w = sb("gate_w", [D, E])
        gate_row = sb("gate_row", [128, E])
        b1c = sb("b1c", [128, E, FC])
        before = sb("before", [TT, 128])
        patches = sb("patches", [2 * C * PS, 2, PW, IW])
        h0T = sb("h0T", [D, IMGS, N])
        h0_tok = sb("h0_tok", [TT, NT, D])
        hb_tok = h0_tok
        x1_room = sb("x1_room", [128, NT * D])
        x1_tok = x1_room[0:TT].rearrange("p (t d) -> p t d", t=NT)
        x1T = h0T[:, :, :].rearrange("d i n -> d (i n)")
        qk_room = sb("qk_room", [128, 4 * T])
        zg = qk_room[0:QA, 0:2 * IMGS * 256].rearrange("p (a i k) -> p a i k", a=2, i=IMGS)
        wnew = sb("wnew", [128, IMGS, 128])
        bnew = sb("bnew", [128, IMGS])
        pT = sb("pT", [128, T])
        tT = pT
        qT = x1T
        h1_tok = sb("h1_tok", [TT, NT, D])
        h1_hold = sb("h1_hold", [TT, NT, D])
        x2T = sb("x2T", [D, T])
        kbuf = sb("kbuf", [D, KB, 2, NJ, T], I16)
        trig_buf = sb("trig_buf", [D, 2, 2, NJ, T])
        trig = trig_buf[:, 0]
        csT = x1_room[:, 0:T]
        h2_tok = sb("h2_tok", [TT, NT, D])
        silu_tok = h2_tok
        x3_tok = sb("x3_tok", [TT, NT, D])
        x4_tok = x3_tok
        attn_room = sb("attn_room", [128, H * T])
        attn_flat = attn_room[:, :]
        q3T, k3T, oT, pTa = (attn_flat[0:n, T * i:T * i + T] for i, n in enumerate((128, 128, D, QA)))
        pTb = attn_flat[0:QB, 4 * T:4 * T + IMGS * QB]
        v3 = attn_flat[0:QA, 5 * T:5 * T + 2 * IMGS * D].rearrange("p (a i d) -> p a i d", a=2, i=IMGS)
        kM = attn_flat.rearrange("p (h k) -> p h k", h=H)
        q4T = qk_room[:, 0:2 * T].rearrange("p (g k) -> p g k", g=2)
        onT = q4T[:, 0]
        k4T = qk_room[:, 2 * T:4 * T].rearrange("p (g k) -> p g k", g=2)
        o4T = k4T
        s3 = sb("s3", [QA, 2, IMGS, N])
        e3 = attn_flat[0:QA, 0:2 * IMGS * N].rearrange("p (a i k) -> p a i k", a=2, i=IMGS)
        p4 = [trig[0:QA, b].rearrange("p j k -> p (j k)").rearrange("p (t g j k) -> p t g j k", t=2, g=2, j=NJ)
              for b in range(2)]
        xT = sb("xT", [D, T])
        m3 = sb("m3", [QA, 2 * IMGS])
        sum3 = sb("sum3", [QA, 2 * IMGS])
        rec3 = sb("rec3", [QA, 2 * IMGS])
        y_tok = sb("y_tok", [TT, NT, D])
        z_tok = on_tok = y_tok
        hb3_tok = h2_tok
        x4b_tok = x4_tok
        rows = sb("rows", [TT, NT, ROW])
        t_tok = rows[:, :, 0:D]
        h3_tok = rows[:, :, D:2 * D]
        v4 = sb("v4", [QA, 2, IMGS, H, 32])
        m4 = sb("m4", [QA, 2, 128])
        r4 = sb("r4", [TT, NT * H])
        gl = sb("gl", [TT, NT, E])
        ge = sb("ge", [TT, NT, E])
        gt_room = sb("gt_room", [TT, NT + 1, E])
        gt = gt_room[:, 1:]
        gs = sb("gs", [TT, 6, NT])
        slots = sb("slots", [TT, NT, E])
        slot = sb("slot", [TT, NT])
        row_index = sb("row_index", [TT, NT], I32)
        run = sb("run", [128, E])
        token = sb("token", [TT, NT])
        bn = {k: sb(f"bn_{k}", [TT, NT, 6]) for k in ("1", "2", "3", "y", "4", "5")}
        mv = {k: sb(f"mv_{k}", [TT, NT, 2]) for k in bn}
        ve = {k: sb(f"ve_{k}", [TT, NT]) for k in bn}
        rstd = {k: sb(f"rstd_{k}", [TT, NT]) for k in bn}
        minus_half = sb("minus_half", [TT, NT])

        tokw_in = attn_flat[:, 0:C * PS * PS]
        trigf = trig.rearrange("p a j k -> p (a j k)")
        su = [trigf[:, 128 * i:128 * i + 128] for i in range(8)]
        lutW = trigf[0:NW, 1024:1024 + 4 * D].rearrange("n (a d) -> n a d", a=4)
        wt = trigf[:, 1536:1536 + C * PS * PS].rearrange("d (b c a) -> d b c a", b=PS, c=C)
        su_col = sb("su_col", [128, 8])
        we_col = sb("we_col", [128, HD])
        bq_row = sb("bq_row", [1, 2, NJ, 32])
        bk_row = sb("bk_row", [1, 2, NJ, 32])
        odd_w = attn_flat[0:C * PS, 1024:1024 + PS // 2 * D]

        TB = 4
        tailf = [trig_buf[:, k].rearrange("p a j k -> p (a j k)") for k in range(2)]

        def tail(b, at, n):
            return tailf[b // 2][:, at + n * (b % 2):at + n * (b % 2) + n]

        tail_w = [tail(b, 0, 1024) for b in range(TB)]
        tail_rows = [tail(b, 2048, 2 * ROW).rearrange("p (a c) -> p a c", a=2) for b in range(TB)]
        tail_b2 = [tail(b, 3088, D) for b in range(TB)]
        tail_b1 = [tail(b, 3344, FC) for b in range(TB)]
        tail_tT = [tail(b, 3352, MT) for b in range(2)]
        tail_hid = [attn_flat[:, 1024 * b:1024 * b + 1024].rearrange("p (f k) -> p f k", f=FC) for b in range(2)]
        tail_out = [attn_flat[:, 2048 + MT * b:2048 + MT * b + MT].rearrange("p (a d) -> p a d", a=2) for b in range(TB)]
        tail_ids = sb("tail_ids", [128, TB, 2], I32)
        pad_rows = sb("pad_rows", [128, ROW])
        pad_at = sb("pad_at", [128, 2])
        pad_slot = sb("pad_slot", [128, 2, E])
        pad_index = sb("pad_index", [128, 2, E], I32)
        region = sb("region", [1, E])
        cum = sb("cum", [1, E])
        tile_no = sb("tile_no", [1, 1])
        past = sb("past", [1, E])
        past_cum = sb("past_cum", [1, E])
        where = sb("where", [1, 4])
        where_i = sb("where_i", [1, TB, 2], I32)

        psum = ctx.enter_context(nc.psum_tensor("psum", [128, 8, 512], F32))
        acc_ps = psum[:, 0:2, :]
        fr = psum[:, 2:4, :]
        bk = psum[:, 4:8, :]
        fr_tok = fr[0:TT].rearrange("p a b -> p (a b)")[:, 0:NT * D]
        fr_flat = fr.rearrange("p a b -> p (a b)")
        bk_flat = bk.rearrange("p a b -> p (a b)")
        acc_flat = acc_ps.rearrange("p a b -> p (a b)")

        tile_hid_ps = [(bk, acc_ps)[f // 2][:, f % 2, 0:MT] for f in range(FC)]
        tile_T_ps = [fr[:, b, 0:MT] for b in range(2)]
        tile_mm_ps = [bk[:, 2 + b, 0:MT] for b in range(2)]

        loaded_e = sem("embedding_weights_loaded")
        loaded_w = sem("weights_loaded")
        copied_w = sem("patch_weights_copied")
        su_pool = sem("setup_pool")
        su_dve = sem("setup_dve")
        su_pe = sem("setup_pe")
        su_act = sem("setup_act")
        x_loaded = [sem(f"{p}_images_loaded") for p in ("even", "odd")]
        e_pe, e_dve = sem("embed_pe"), sem("embed_dve")
        f_pe, f_act, f_dve, f_pool = sem("front_pe"), sem("front_act"), sem("front_dve"), sem("front_pool")
        t_pe, t_act, t_dve, t_pool = sem("trig_pe"), sem("trig_act"), sem("trig_dve"), sem("trig_pool")
        b_pe, b_act, b_dve, b_pool = sem("back_pe"), sem("back_act"), sem("back_dve"), sem("back_pool")
        n_dve, n_pool = sem("norm_dve"), sem("norm_pool")
        r_pe, r_act, r_dve, r_pool = sem("route_pe"), sem("route_act"), sem("route_dve"), sem("route_pool")
        routed = sem("rows_routed")
        scratch_set = sem("scratch_set")
        padded_at = sem("padding_rows_placed")
        tile_at, tile_loaded = sem("tile_placed"), [sem(f"tile_{b}_loaded") for b in range(TB)]
        tile_T, tile_tT = sem("tile_transposed"), sem("tile_transposed_out")
        tile_hid, tile_gelu, tile_mm = sem("tile_hidden"), sem("tile_gelu"), sem("tile_product")
        tile_ids, tile_done, tile_sum, place = sem("tile_tokens"), sem("tile_done"), sem("tile_sum"), sem("placing")
        stored = [sem(f"tile_{b}_stored") for b in range(TB)]

        def row(ap, n=128):
            return ap.unsqueeze(0).to_broadcast([n, *ap.shape])

        W_all = W_g.rearrange("h e w -> (h e) w")
        first_loads = [
            (tokw_in, tok_W), (addend[:, 2:N], row(tok_pos[0, 1:NPATCH + 1, 0])),
            (su_col[:, 0:1], tok_b.unsqueeze(1)), (su_col[:, 1:2], cls_tok[0, 0].unsqueeze(1)),
            (su_col[:, 2:3], tok_cls[0, 0].unsqueeze(1)), (su_col[:, 3:4], row(tok_pos[0, 0, :])),
        ]
        loads = [
            (we_col[:, :], W_e.rearrange("h d e -> (h d) e")),
            (zg_w[:, 0:128].rearrange("w (h d) -> w h d", h=H), W_phi.rearrange("h w d -> w h d")),
            (zg_b[:, 0:128], row(b_phi.rearrange("h d -> (h d)"))),
            (su_col[:, 4:5], b_phi.rearrange("h d -> (h d)").unsqueeze(1)),
            (be_col[:, :], b_e.rearrange("h d -> (h d)").unsqueeze(1)),
            (su_col[:, 5:6], g_bias[0].unsqueeze(1)),
            (su[0][:, :], W_all),
            (psi_w[:, :].rearrange("w (h d) -> w h d", h=H), W_psi.rearrange("h w d -> w h d")),
            (psi_b[:, :], b_psi.rearrange("h d -> (h d)").unsqueeze(1)),
            (wh[:, :], W_h.rearrange("h e w -> (h e) w")), (hbias_row[:, :], row(h_bias[0])),
            (lutW[:, 0], ffn_W), (lutW[:, 1], ffn_B), (lutW[:, 2], ffn_cos), (lutW[:, 3], ffn_sin),
            (su[1][:, :].rearrange("d (j c i) -> d j c i", j=NJ, c=2)[:, :, 0], pcos.rearrange("d (j i) -> d j i", j=NJ)),
            (su[1][:, :].rearrange("d (j c i) -> d j c i", j=NJ, c=2)[:, :, 1], psin.rearrange("d (j i) -> d j i", j=NJ)),
            (wqq[:, 0], Wq3), (wqq[:, 1], Wq3), (wkk[:, 0], Wk3), (wkk[:, 1], Wk3),
            (bqq[0:DA, :], bq3.unsqueeze(1)), (bqq[DA:, :], bq3.unsqueeze(1)),
            (bkk[0:DA, :], bk3.unsqueeze(1)), (bkk[DA:, :], bk3.unsqueeze(1)),
            (wv3[:, :], Wv3), (bv3c[:, :], bv3.unsqueeze(1)), (gamma_row[:, :], row(gamma3)),
            (beta_row[:, :], row(beta3)), (wv4[:, :], Wv4), (wo4[:, :], Wo4), (su_col[:, 6:7], bv4.unsqueeze(1)),
            (bo_row[:, :], row(bo4)), (g5_row[:, :], row(ln_g)), (b5_row[:, :], row(ln_b)),
            (gate_w[:, :], gate_W), (gate_row[:, :], row(gate_b)),
            (b1c[:, :, :], b1.rearrange("e (k p) -> p e k", p=128)),
        ]
        padded = [
            (bq_row[:, :, :, 0:HD], bq4.rearrange("(a g j i) -> a g j i", a=1, g=2, j=NJ)),
            (bk_row[:, :, :, 0:HD], bk4.rearrange("(a g j i) -> a g j i", a=1, g=2, j=NJ)),
        ]
        for g in range(2):
            padded += [
                (wq4[:, g, :, 0:HD], Wq4[:, 64 * g:64 * g + 64].rearrange("d (j i) -> d j i", j=NJ)),
                (wk4[:, g, :, 0:HD], Wk4[:, 64 * g:64 * g + 64].rearrange("d (j i) -> d j i", j=NJ)),
            ]
        LOADED = 16 * (len(loads) + len(padded))
        ZEROED = 6
        out_rows = out.rearrange("b n d -> (b n) d")

        dve_waited, pool_waited, sp_waited = sem("dve_waited"), sem("pool_waited"), sem("sync_waited")

        def take_waits(engine, waited):
            engine.sem_inc(waited, 1)

        def loads_of_tile(k, b):
            return 80 * (k // TB + 1) if isinstance(k, int) else 80 // TB * (k - b) + 80

        block = ctx.enter_context(nc.Block())

        @block.sync
        def _(sp):
            def load(m, c):
                if m < 2:
                    need(sp, e_pe, EMB_PE, f"emb{m + 2}", c - 1)
                else:
                    need(sp, e_pe, EMB_PE, f"emb{m - 2}", c)
                for q in range(2):
                    for ch in range(C):
                        at = C * PS * q + PS * ch
                        sp.dma_start(patches[at:at + PS, m % 2, :, 0:IW - q],
                                     x[IMGS * c + m, ch, :, q:IW].rearrange("(w r) k -> r w k", r=PS)
                                     ).then_inc(x_loaded[m % 2], 16)

            def body(i):
                for m in range(IMGS):
                    load(m, i + 2)

            with nc.allow_non_contiguous_dma(reason="bias columns, once"):
                for dst, src in first_loads:
                    sp.dma_start(dst, src).then_inc(loaded_e, 16)
            load(0, 0)
            load(1, 0)
            with nc.allow_non_contiguous_dma(reason="bias columns, once"):
                for dst, src in loads:
                    sp.dma_start(dst, src).then_inc(loaded_w, 16)
            sp.wait_ge(su_dve, ZEROED)
            for dst, src in padded:
                sp.dma_start(dst, src).then_inc(loaded_w, 16)
            load(2, 0)
            load(3, 0)
            for m in range(IMGS):
                load(m, 1)
            with nc.allow_non_contiguous_dma(reason="16 bytes a partition, once"):
                sp.dma_start(b1_cols.rearrange("e p k -> p e k"), b1c[:, :, :]).then_inc(scratch_set, 16)
            sp.wait_ge(su_dve, SU_DVE)
            for a in range(2):
                sp.dma_start(expert_rows[E * REGION + 128 * a:E * REGION + 128 * a + 128],
                             pad_rows[:, :]).then_inc(scratch_set, 16)
            body(0)
            body(1)
            with sp.Fori(2, CHUNKS - 2) as i:
                body(i)

            def load_tile(k, b, first):
                if not first:
                    sp.wait_ge(tile_mm, k - TB + 1)
                    take_waits(sp, sp_waited)
                    sp.wait_ge(tile_done, k - TB + 1)
                    take_waits(sp, sp_waited)
                sp.wait_ge(tile_at, k + 1)
                take_waits(sp, sp_waited)
                start = sp.value_load(where_i[0:1, b, 0:1], min_val=0, max_val=E * REGION)
                e = sp.value_load(where_i[0:1, b, 1:2], min_val=0, max_val=E - 1)
                loaded = tile_loaded[b]
                sp.dma_start(tail_w[b][:, 0:FF], W1[bass.ds(e, 1)].rearrange("e d f -> d (e f)")).then_inc(loaded, 16)
                sp.dma_start(tail_w[b][:, FF:].rearrange("p (k d) -> p k d", k=FC),
                             W2[bass.ds(e, 1)].rearrange("e (k p) d -> p (e k) d", p=128)).then_inc(loaded, 16)
                sp.dma_start(tail_b1[b], b1_cols[bass.ds(e, 1)].rearrange("e p k -> p (e k)")).then_inc(loaded, 16)
                sp.dma_start(tail_b2[b], b2[bass.ds(e, 1)].to_broadcast([128, D])).then_inc(loaded, 16)
                if first:
                    sp.wait_ge(routed, 80 * CHUNKS + 16 * 2 * E)
                sp.dma_start(tail_rows[b], expert_rows[bass.ds(start, MT)].rearrange("(a p) c -> p a c", a=2)
                             ).then_inc(loaded, 16)

            sp.wait_ge(scratch_set, 48)
            for b in range(TB):
                load_tile(b, b, True)
            with sp.Fori(1, TILES // TB) as i:
                for b in range(TB):
                    load_tile(TB * i + b, b, False)
            for b in range(TB):
                sp.wait_ge(stored[b], 32 * (TILES // TB))

        @block.gpsimd
        def _(pool):
            nc.gpsimd.memset(ident[:, :], 0.0).then_inc(su_pool, 1)
            nc.gpsimd.memset(block_mask[:, :], 1.0).then_inc(su_pool, 1)
            nc.gpsimd.memset(maskA[:, :], 0.0).then_inc(su_pool, 1)
            nc.gpsimd.memset(maskB[:, :], 0.0).then_inc(su_pool, 1)
            nc.gpsimd.memset(head_mask[:, :], 1.0).then_inc(su_pool, 1)
            nc.gpsimd.memset(head_neg[:, :, :], 0.0).then_inc(su_pool, 1)
            for e in range(E):
                nc.gpsimd.memset(rank[:, e:e + 1], float(E - e)).then_inc(su_pool, 1)
            nc.gpsimd.memset(before[:, :], 1.0).then_inc(su_pool, 1)
            nc.gpsimd.memset(pad_rows[:, 0:ROW - 1], 0.0).then_inc(su_pool, 1)
            iota = dict(channel_multiplier=1, allow_small_or_imprecise_dtypes=True)
            nc.gpsimd.iota(pad_rows[:, ROW - 1:ROW], pattern=[[0, 1]], base=NOWHERE, **iota).then_inc(su_pool, 1)
            nc.gpsimd.iota(pad_at[:, :], pattern=[[128, 2]], base=0, **iota).then_inc(su_pool, 1)
            nc.gpsimd.iota(token[:, :], pattern=[[TT, NT]], base=0, **iota).then_inc(su_pool, 1)
            for e in range(E):
                nc.gpsimd.memset(run[:, e:e + 1], float(REGION * e)).then_inc(su_pool, 1)
                nc.gpsimd.memset(region[:, e:e + 1], float(REGION * e)).then_inc(su_pool, 1)
            pool.wait_ge(su_pool, 6 + E + 5 + 2 * E)
            nc.gpsimd.affine_select(out=before[:, :], in_=before[:, :], compare_op=ALU.is_gt, fill=0.0, base=0,
                                    pattern=[[1, 128]], channel_multiplier=-1).then_inc(su_pool, 1)
            nc.gpsimd.affine_select(out=ident[:, :], in_=ident[:, :], compare_op=ALU.not_equal, fill=1.0, base=0,
                                    pattern=[[-1, 128]], channel_multiplier=1).then_inc(su_pool, 1)
            bm = block_mask[:, :].rearrange("p (g k) -> p g k", g=H)
            nc.gpsimd.affine_select(out=bm, in_=bm, compare_op=ALU.is_ge, fill=0.0, base=0,
                                    pattern=[[-HD, H], [0, HD]], channel_multiplier=1).then_inc(su_pool, 1)
            pool.wait_ge(su_pool, 14 + 3 * E)
            nc.gpsimd.affine_select(out=bm, in_=bm, compare_op=ALU.is_ge, fill=0.0, base=HD - 1,
                                    pattern=[[HD, H], [0, HD]], channel_multiplier=-1).then_inc(su_pool, 1)
            nc.gpsimd.affine_select(out=maskA[:, :], in_=maskA[:, :], compare_op=ALU.is_ge, fill=MASKED, base=0,
                                    pattern=[[-1, QA]], channel_multiplier=1).then_inc(su_pool, 1)
            nc.gpsimd.affine_select(out=maskB[:, :], in_=maskB[:, :], compare_op=ALU.is_ge, fill=MASKED, base=QA,
                                    pattern=[[-1, N]], channel_multiplier=1).then_inc(su_pool, 1)
            nc.gpsimd.affine_select(out=head_mask[:, :], in_=head_mask[:, :], compare_op=ALU.is_ge, fill=0.0, base=0,
                                    pattern=[[-32, NJ]], channel_multiplier=1).then_inc(su_pool, 1)
            for g in range(2):
                nc.gpsimd.affine_select(out=head_neg[:, g], in_=head_neg[:, g], compare_op=ALU.not_equal, fill=-1.0,
                                        base=-HD - g, pattern=[[-32, NJ]], channel_multiplier=1).then_inc(su_pool, 1)
            pool.wait_ge(su_pool, 20 + 3 * E)
            nc.gpsimd.affine_select(out=head_mask[:, :], in_=head_mask[:, :], compare_op=ALU.is_ge, fill=0.0,
                                    base=HD - 1, pattern=[[32, NJ]], channel_multiplier=-1).then_inc(su_pool, 1)

            def ln(sem_in, steps_in, name, eps, c, sem_out, steps_out):
                need(pool, sem_in, steps_in, "ln" + name, c)
                take_waits(pool, pool_waited)
                nc.gpsimd.tensor_scalar(ve[name][:, :], mv[name][:, :, 1], EPS, 1.0, ALU.add,
                                        ALU.mult).then_inc(sem_out, 1)
                need(pool, sem_out, steps_out, "eps" + name, c)
                nc.gpsimd.tensor_tensor(rstd[name][:, :], ve[name][:, :], minus_half[:, :],
                                        ALU.pow).then_inc(sem_out, 1)

            def front(tick, c):
                if tick == 5:
                    ln(f_dve, FRONT_DVE, "1", EPS, c, f_pool, FRONT_POOL)
                if tick == 8:
                    need(pool, f_act, FRONT_ACT, "h0", c)
                    need(pool, f_dve, FRONT_DVE, "x1", c)
                    nc.gpsimd.tensor_tensor(hb_tok[:, :, :], h0_tok[:, :, :],
                                            hbias_row[0:TT].unsqueeze(1).to_broadcast([TT, NT, D]),
                                            ALU.add).then_inc(f_pool, 1)
                if tick == 14:
                    ln(f_dve, FRONT_DVE, "2", EPS, c, f_pool, FRONT_POOL)

            def hold(c):
                need(pool, f_dve, FRONT_DVE, "ln2", c)
                need(pool, t_pool, TRIG_POOL, "h2", c - 1)
                take_waits(pool, pool_waited)
                nc.gpsimd.tensor_copy(h1_hold[:, :, :], h1_tok[:, :, :]).then_inc(f_pool, 1)

            def trig_end(c):
                need(pool, t_act, TRIG_ACT, "silu", c)
                need(pool, f_pool, FRONT_POOL, "h1hold", c)
                nc.gpsimd.tensor_tensor(h2_tok[:, :, :], h1_hold[:, :, :], silu_tok[:, :, :],
                                        ALU.add).then_inc(t_pool, 1)

            def back(tick, c):
                if tick == 0:
                    need(pool, n_dve, NORM_DVE, "x3", c)
                    nc.gpsimd.tensor_tensor(hb3_tok[:, :, :], h2_tok[:, :, :],
                                            beta_row[0:TT].unsqueeze(1).to_broadcast([TT, NT, D]),
                                            ALU.add).then_inc(n_pool, 1)
                if tick == 11:
                    ln(b_dve, BACK_DVE, "y", EPS, c, b_pool, BACK_POOL)
                if tick == 13:
                    ln(b_dve, BACK_DVE, "4", EPS, c, b_pool, BACK_POOL)
                if tick == 14:
                    need(pool, b_pe, BACK_PE, "x4T", c)
                    nc.gpsimd.tensor_tensor(x4b_tok[:, :, :], x4_tok[:, :, :],
                                            bo_row[0:TT].unsqueeze(1).to_broadcast([TT, NT, D]),
                                            ALU.add).then_inc(b_pool, 1)
                if tick == 18:
                    for g in range(2):
                        need(pool, b_act, BACK_ACT, f"k4{'ab'[g]}", c)
                        take_waits(pool, pool_waited)
                        for j in range(NJ):
                            i = nc.gpsimd.tensor_scalar(kM[:, NJ * g + j], k4T[:, g], head_mask[:, j:j + 1],
                                                        head_neg[:, g, j:j + 1], ALU.mult, ALU.add)
                        i.then_inc(b_pool, 1)

            def route(tick, c):
                if tick == 9:
                    need(pool, r_dve, ROUTE_DVE, "run", c)
                    take_waits(pool, pool_waited)
                    for t in range(NT):
                        nc.gpsimd.indirect_dma_start(
                            out=expert_rows, out_offset=bass.IndirectOffsetOnAxis(ap=row_index[:, t:t + 1], axis=0),
                            in_=rows[:, t], in_offset=None).then_inc(routed, 16)

            pool.wait_ge(loaded_w, LOADED)
            pool.wait_ge(su_dve, SU_DVE)

            def body(i, fronts=True, trigs=True, backs=True, routes=True):
                for tick in range(TICKS):
                    if routes:
                        route(tick, i - 2)
                    if backs:
                        back(tick, i - 1)
                    if fronts:
                        front(tick, i + 1)
                if trigs:
                    trig_end(i)
                    ln(n_dve, NORM_DVE, "3", EPS, i, n_pool, NORM_POOL)
                if fronts:
                    hold(i + 1)
                if backs:
                    ln(r_dve, ROUTE_DVE, "5", EPS, i - 1, r_pool, ROUTE_POOL)

            body(-1, trigs=False, backs=False, routes=False)
            body(0, backs=False, routes=False)
            body(1, routes=False)
            body(2)
            with pool.Fori(3, CHUNKS - 1) as i:
                body(i)
            body(CHUNKS - 1, fronts=False)
            body(CHUNKS, fronts=False, trigs=False)
            body(CHUNKS + 1, fronts=False, trigs=False, backs=False)

            pool.wait_ge(padded_at, 1)
            for a in range(2):
                for e in range(E):
                    nc.gpsimd.indirect_dma_start(
                        out=expert_rows, out_offset=bass.IndirectOffsetOnAxis(ap=pad_index[:, a, e:e + 1], axis=0),
                        in_=pad_rows[:, :], in_offset=None).then_inc(routed, 16)

            def store_tile(k, b):
                pool.wait_ge(tile_done, k + 1)
                take_waits(pool, pool_waited)
                for a in range(2):
                    nc.gpsimd.indirect_dma_start(
                        out=out_rows, out_offset=bass.IndirectOffsetOnAxis(ap=tail_ids[:, b, a:a + 1], axis=0),
                        in_=tail_out[b][:, a], in_offset=None, bounds_check=TOKENS - 1,
                        oob_is_err=False).then_inc(stored[b], 16)

            with pool.Fori(0, TILES // TB) as i:
                for b in range(TB):
                    store_tile(TB * i + b, b)

        @block.vector
        def _(dve):
            v = nc.vector
            v.memset(gt_room[:, 0], 0.0).then_inc(su_dve, 1)
            v.memset(bq_row[:, :, :, :], 0.0).then_inc(su_dve, 1)
            v.memset(bk_row[:, :, :, :], 0.0).then_inc(su_dve, 1)
            v.memset(wq4[:, :, :, :], 0.0).then_inc(su_dve, 1)
            v.memset(wk4[:, :, :, :], 0.0).then_inc(su_dve, 1)
            v.memset(trig_w[:, :], 0.0).then_inc(su_dve, 1)
            v.memset(v4[:, :, :, :, :], 1.0).then_inc(su_dve, 1)
            v.memset(m4[:, :, :], 0.0).then_inc(su_dve, 1)
            v.memset(rec3[:, :], 1.0).then_inc(su_dve, 1)
            v.memset(minus_half[:, :], -0.5).then_inc(su_dve, 1)
            v.memset(s3[:, :, :, :], MASKED).then_inc(su_dve, 1)
            v.memset(ones[:, :], 1.0).then_inc(su_dve, 1)
            dve.wait_ge(loaded_e, 16 * len(first_loads))
            v.tensor_scalar(addend[:, 2:N], addend[:, 2:N], su_col[:, 0:1], None, ALU.add).then_inc(su_dve, 1)
            v.tensor_copy(addend[:, 0:1], su_col[:, 1:2]).then_inc(su_dve, 1)
            v.tensor_tensor(addend[:, 1:2], su_col[:, 2:3], su_col[:, 3:4], ALU.add).then_inc(su_dve, 1)
            v.tensor_copy(wt, tokw_in.rearrange("d (a b c) -> d b c a", a=PS, b=PS)).then_inc(su_dve, 1)
            dve.wait_ge(loaded_w, LOADED)
            dve.wait_ge(su_pool, POOL_SETUP)
            v.tensor_tensor(bd_we[:, :].rearrange("p (h e) -> p h e", h=H), we_col[:, :].unsqueeze(1).to_broadcast([128, H, HD]),
                            block_mask[:, :].rearrange("p (h e) -> p h e", h=H), ALU.mult)
            dve.wait_ge(su_pe, 2)
            v.tensor_copy(su[3][:, :], bk[:, 0, 0:128]).then_inc(su_dve, 1)
            v.tensor_copy(su[4][:, :], bk[:, 0, 128:256]).then_inc(su_dve, 1)
            v.tensor_copy(proj_w[:, :], bk[:, 0, 256:384]).then_inc(su_dve, 1)
            dve.wait_ge(su_pe, 4)
            v.tensor_tensor(su[5][:, :], bk[:, 1, 0:128], block_mask[:, :], ALU.mult).then_inc(su_dve, 1)
            v.tensor_copy(su[6][:, :], bk[:, 1, 128:256]).then_inc(su_dve, 1)
            v.tensor_tensor(su_col[:, 7:8], bk[:, 1, 256:257], be_col[:, :], ALU.add).then_inc(su_dve, 1)
            dve.wait_ge(su_dve, 22)
            v.tensor_scalar(su[7][:, :], ones[:, :], su_col[:, 7:8], None, ALU.mult).then_inc(su_dve, 1)
            v.tensor_scalar(su[1][:, :], ones[:, :], su_col[:, 5:6], None, ALU.mult).then_inc(su_dve, 1)
            v.tensor_scalar(su[0][:, :], ones[:, :], su_col[:, 6:7], None, ALU.mult).then_inc(su_dve, 1)
            dve.wait_ge(su_pe, 7)
            v.tensor_copy(bq4c[:, :], bk[:, 2, 384:386])
            v.tensor_copy(bk4c[:, :], bk[:, 2, 386:388])
            dve.wait_ge(su_pe, 7)
            v.tensor_tensor(su[4][:, :], su[3][:, :], bk[:, 2, 0:128], ALU.subtract).then_inc(su_dve, 1)
            v.tensor_scalar(zg_b[:, 128:256], bk[:, 2, 128:256], -LR_SCALE, None, ALU.mult).then_inc(su_dve, 1)
            v.tensor_tensor(bo_row[:, :], bo_row[:, :], bk[:, 2, 256:384], ALU.add).then_inc(su_dve, 1)
            dve.wait_ge(su_dve, 28)
            v.tensor_scalar(zg_w[:, 128:256], su[4][:, :], LR_SCALE, None, ALU.mult).then_inc(su_dve, 1)
            dve.wait_ge(su_pe, 8)
            lw = bk[:, 3, 0:4 * NW].rearrange("p (a n) -> p a n", a=4)
            v.tensor_scalar(lut_s[:, :], lw[:, 0], -1.0, None, ALU.mult).then_inc(su_dve, 1)
            dve.wait_ge(su_dve, 30)
            v.tensor_tensor(lut_s[:, :], lw[:, 0], lut_s[:, :], ALU.max).then_inc(su_dve, 1)
            dve.wait_ge(su_dve, 31)
            v.tensor_scalar(lut_s[:, :], lut_s[:, :], 1.0, None, ALU.add).then_inc(su_dve, 1)
            dve.wait_ge(su_dve, 32)
            v.reciprocal(lut_s[:, :], lut_s[:, :]).then_inc(su_dve, 1)
            dve.wait_ge(su_dve, 33)
            v.tensor_scalar(lut_s[:, :], lut_s[:, :], TO_LUT, None, ALU.mult).then_inc(su_dve, 1)
            v.tensor_scalar(su[2][:, 0:NW], lw[:, 1], TO_LUT, None, ALU.mult).then_inc(su_dve, 1)
            dve.wait_ge(su_dve, 35)
            v.tensor_scalar(lut_b[:, :], su[2][:, 0:NW], 1.0 / LUT, MAGIC, ALU.mult, ALU.add).then_inc(su_dve, 1)
            dve.wait_ge(su_dve, 36)
            v.tensor_scalar(lut_b[:, :], lut_b[:, :], MAGIC, -float(LUT), ALU.subtract, ALU.mult).then_inc(su_dve, 1)
            dve.wait_ge(su_dve, 37)
            v.tensor_tensor(lut_b[:, :], lut_b[:, :], su[2][:, 0:NW], ALU.add).then_inc(su_dve, 1)
            for cs in range(2):
                for j in range(NJ):
                    at = j * NI * 64 + cs * 48
                    v.tensor_scalar(trig_w[:, at:at + 65 * (NI - 1) + 1:65], lw[:, 2 + cs, NI * j:NI * j + NI], -1.0,
                                    None, ALU.mult).then_inc(su_dve, 1)

            def stats(src, name, c, sem_d, steps):
                for t in range(NT):
                    i = v.bn_stats(bn[name][:, t], src[:, t])
                i.then_inc(sem_d, 1)
                need(dve, sem_d, steps, "bn" + name, c)
                take_waits(dve, dve_waited)
                for t in range(NT):
                    i = v.bn_aggr(mv[name][:, t], bn[name][:, t])
                i.then_inc(sem_d, 1)

            def normal(src, name, c, sem_d, steps, sem_p, steps_p, dst):
                need(dve, sem_d, steps, "ln" + name, c)
                need(dve, sem_p, steps_p, "rstd" + name, c)
                for t in range(NT):
                    i = v.tensor_scalar(dst[:, t], src[:, t], mv[name][:, t, 0:1], rstd[name][:, t:t + 1],
                                        ALU.subtract, ALU.mult)
                i.then_inc(sem_d, 1)

            def embed_out(c):
                need(dve, f_pe, FRONT_PE, "attn", c - 1)
                v.tensor_copy(h0T[:, :, 0:2], addend[:, 0:2].unsqueeze(1).to_broadcast([D, IMGS, 2])).then_inc(e_dve, 1)
                for k in range(2):
                    need(dve, e_pe, EMB_PE, f"emb{2 * k + 1}", c)
                    v.tensor_tensor(h0T[:, 2 * k:2 * k + 2, 2:N],
                                    fr[:, k, 0:2 * NPATCH].rearrange("d (p n) -> d p n", p=2),
                                    addend[:, 2:N].unsqueeze(1).to_broadcast([D, 2, NPATCH]),
                                    ALU.add).then_inc(e_dve, 1)

            def front(tick, c):
                if tick == 5:
                    need(dve, f_act, FRONT_ACT, "h0", c)
                    stats(h0_tok, "1", c, f_dve, FRONT_DVE)
                if tick == 6:
                    need(dve, t_pe, TRIG_PE, "proj", c - 2)
                    normal(h0_tok, "1", c, f_dve, FRONT_DVE, f_pool, FRONT_POOL, x1_tok)
                for r in range(2):
                    if tick == 8 + r:
                        need(dve, f_pe, FRONT_PE, f"zg{r}", c)
                        for t, (_, n) in enumerate(QS):
                            v.tensor_tensor(zg[0:n, t, 2 * r:2 * r + 2], fr[0:n, :, 256 * t:256 * t + 256],
                                            zg_b[0:n].unsqueeze(1).to_broadcast([n, 2, 256]), ALU.add).then_inc(f_dve, 1)
                if tick == 10:
                    need(dve, f_pe, FRONT_PE, "cross", c)
                    v.tensor_tensor(wnew[:, :, :], fr[:, 0, :].rearrange("p (i k) -> p i k", i=IMGS),
                                    block_mask[:, :].unsqueeze(1).to_broadcast([128, IMGS, 128]),
                                    ALU.mult).then_inc(f_dve, 1)
                    need(dve, f_dve, FRONT_DVE, "masked", c)
                    v.tensor_tensor(wnew[:, :, :], wnew[:, :, :],
                                    bd_we[:, :].unsqueeze(1).to_broadcast([128, IMGS, 128]), ALU.add).then_inc(f_dve, 1)
                    v.tensor_scalar(bnew[:, :], fr[:, 1, 0:IMGS], be_col[:, 0:1], None, ALU.add).then_inc(f_dve, 1)
                if tick == 14:
                    need(dve, f_pe, FRONT_PE, "attn", c)
                    need(dve, f_pool, FRONT_POOL, "hb", c)
                    need(dve, f_pool, FRONT_POOL, "h1hold", c - 1)
                    v.tensor_tensor(h1_tok[:, :, :].rearrange("p t d -> p (t d)"), fr_tok,
                                    hb_tok[:, :, :].rearrange("p t d -> p (t d)"), ALU.add).then_inc(f_dve, 1)
                    need(dve, f_dve, FRONT_DVE, "h1", c)
                    stats(h1_tok, "2", c, f_dve, FRONT_DVE)
                if tick == 17:
                    normal(h1_tok, "2", c, f_dve, FRONT_DVE, f_pool, FRONT_POOL, x1_tok)

            def trig_steps(c, g):
                b = g % KB
                if g == 0:
                    need(dve, f_act, FRONT_ACT, "x2Tb", c)
                if g >= KB:
                    need(dve, t_act, TRIG_ACT, f"sin{g - KB}", c)
                else:
                    need(dve, t_act, TRIG_ACT, f"sin{max(k for k in range(NI) if k % KB == b)}", c - 1)
                for j in range(NJ):
                    n = NI * j + g
                    i = v.tensor_scalar(kbuf[:, b, 1, j], x2T[:, :], lut_s[:, n:n + 1], lut_b[:, n:n + 1],
                                        ALU.mult, ALU.add)
                i.then_inc(t_dve, 1)

            def trig_wrap(c, g):
                b = g % KB
                need(dve, t_dve, TRIG_DVE, f"k{g}", c)
                v.tensor_scalar(kbuf[:, b, 0], kbuf[:, b, 1], float(LUT // 4), None, ALU.add).then_inc(t_dve, 1)
                need(dve, t_dve, TRIG_DVE, f"add{g}", c)
                v.tensor_scalar(kbuf[:, b], kbuf[:, b], LUT - 1, None, ALU.bitwise_and).then_inc(t_dve, 1)

            def back(tick, c):
                s3v = s3[:, :, :, :].rearrange("p a i k -> p (a i) k")
                e3v = e3[:, :, :, :].rearrange("p a i k -> p (a i) k")
                if tick == 3:
                    need(dve, b_pe, BACK_PE, "s3", c)
                    v.tensor_tensor(s3[:, 0, :, 0:QA], bk[0:QA, 0, 0:IMGS * QA].rearrange("p (i k) -> p i k", i=IMGS),
                                    maskA[:, :].unsqueeze(1).to_broadcast([QA, IMGS, QA]), ALU.add).then_inc(b_dve, 1)
                    v.tensor_tensor(s3[0:QB, 1].rearrange("p (a i) k -> p a i k", a=2),
                                    bk[0:QB, 1:3, 0:HALF].rearrange("p a (i k) -> p a i k", i=2),
                                    maskB[:, :].unsqueeze(1).unsqueeze(1).to_broadcast([QB, 2, 2, N]),
                                    ALU.add).then_inc(b_dve, 1)
                    need(dve, b_dve, BACK_DVE, "mask3b", c)
                    v.tensor_reduce(m3[:, :], s3v, AX, ALU.max).then_inc(b_dve, 1)
                    need(dve, b_dve, BACK_DVE, "max3", c)
                    need(dve, b_pe, BACK_PE, "s3", c)
                    v.tensor_tensor(e3v, s3v, m3[:, :].unsqueeze(2).to_broadcast([QA, 2 * IMGS, N]),
                                    ALU.subtract).then_inc(b_dve, 1)
                if tick == 8:
                    need(dve, b_act, BACK_ACT, "e3", c)
                    v.tensor_reduce(sum3[:, :], e3v, AX, ALU.add).then_inc(b_dve, 1)
                    need(dve, b_dve, BACK_DVE, "sum3", c)
                    v.reciprocal(rec3[:, :], sum3[:, :]).then_inc(b_dve, 1)
                    need(dve, b_dve, BACK_DVE, "rec3", c)
                    v.tensor_tensor(e3v, e3v, rec3[:, :].unsqueeze(2).to_broadcast([QA, 2 * IMGS, N]),
                                    ALU.mult).then_inc(b_dve, 1)
                if tick == 11:
                    need(dve, b_pe, BACK_PE, "o3", c)
                    v.tensor_tensor(y_tok[:, :, :].rearrange("p t d -> p (t d)"), bk_flat[0:TT, 512:512 + NT * D],
                                    x3_tok[:, :, :].rearrange("p t d -> p (t d)"), ALU.add).then_inc(b_dve, 1)
                    need(dve, b_dve, BACK_DVE, "y3", c)
                    stats(y_tok, "y", c, b_dve, BACK_DVE)
                    need(dve, b_dve, BACK_DVE, "lny", c)
                    for t in range(NT):
                        i = v.scalar_tensor_tensor(out=z_tok[:, t], in0=y_tok[:, t], scalar=mv["y"][:, t, 0:1],
                                                   in1=gamma_row[0:TT], op0=ALU.subtract, op1=ALU.mult)
                    i.then_inc(b_dve, 1)
                if tick == 12:
                    need(dve, b_dve, BACK_DVE, "zy", c)
                    need(dve, b_pool, BACK_POOL, "rstdy", c)
                    need(dve, n_pool, NORM_POOL, "hb3", c)
                    need_routed(dve, c)
                    for t in range(NT):
                        i = v.scalar_tensor_tensor(out=h3_tok[:, t], in0=z_tok[:, t], scalar=rstd["y"][:, t:t + 1],
                                                   in1=hb3_tok[:, t], op0=ALU.mult, op1=ALU.add)
                    i.then_inc(b_dve, 1)
                    need(dve, b_dve, BACK_DVE, "h3", c)
                    stats(h3_tok, "4", c, b_dve, BACK_DVE)
                if tick == 13:
                    normal(h3_tok, "4", c, b_dve, BACK_DVE, b_pool, BACK_POOL, x4_tok)
                for r in range(2 * IMGS):
                    if tick == 23 + r:
                        n = QS[r % 2][1]
                        if r >= 2:
                            need(dve, b_pe, BACK_PE, f"mT_{r - 2}", c)
                        for g in range(2):
                            need(dve, b_pe, BACK_PE, f"s4{'ab'[g]}_{r}", c)
                            v.tensor_reduce(m4[0:n, r % 2, :].rearrange("p (j g) -> p j g", j=NJ)[:, :, HD + g],
                                            bk[0:n, 2 * g:2 * g + 2, 0:2 * N].rearrange("p a (j k) -> p a j k", j=2), AX,
                                            ALU.max).then_inc(b_dve, 1)
                if tick == 31:
                    need(dve, b_pe, BACK_PE, f"mT_{2 * IMGS - 1}", c)
                    for g in range(2):
                        q = q4T[:, g].rearrange("p (i k) -> p i k", i=IMGS)
                        v.tensor_tensor(q, q, bk[:, :, 2 * N:3 * N], ALU.add).then_inc(b_dve, 1)

            def softmax_end(c):
                need(dve, b_pe, BACK_PE, "o4", c)
                o4 = bk_flat[0:TT, 0:2 * NT * 128].rearrange("p (h k) -> p h k", k=32)
                v.reciprocal(r4[:, :], o4[:, :, HD]).then_inc(b_dve, 1)
                need(dve, b_dve, BACK_DVE, "rsum", c)
                v.tensor_tensor(on_tok[:, :, :].rearrange("p t (h k) -> p (t h) k", k=HD), o4[:, :, 0:HD],
                                r4[:, :].unsqueeze(2).to_broadcast([TT, NT * H, HD]), ALU.mult).then_inc(b_dve, 1)

            def norm_stats(c):
                need(dve, t_pool, TRIG_POOL, "h2", c)
                stats(h2_tok, "3", c, n_dve, NORM_DVE)

            def norm_out(c):
                need(dve, r_dve, ROUTE_DVE, "y4", c - 1)
                normal(h2_tok, "3", c, n_dve, NORM_DVE, n_pool, NORM_POOL, x3_tok)

            def y4_stats(c):
                need(dve, b_pe, BACK_PE, "wo", c)
                need(dve, b_pool, BACK_POOL, "x4b", c)
                v.tensor_tensor(y_tok[:, :, :].rearrange("p t d -> p (t d)"), bk_flat[0:TT, 1024:1024 + NT * D],
                                x4b_tok[:, :, :].rearrange("p t d -> p (t d)"), ALU.add).then_inc(r_dve, 1)
                need(dve, r_dve, ROUTE_DVE, "y4", c)
                stats(y_tok, "5", c, r_dve, ROUTE_DVE)
                need(dve, r_dve, ROUTE_DVE, "ln5", c)
                for t in range(NT):
                    i = v.scalar_tensor_tensor(out=z_tok[:, t], in0=y_tok[:, t], scalar=mv["5"][:, t, 0:1],
                                               in1=g5_row[0:TT], op0=ALU.subtract, op1=ALU.mult)
                i.then_inc(r_dve, 1)

            def t_out(c):
                need(dve, r_dve, ROUTE_DVE, "z5", c)
                need(dve, r_pool, ROUTE_POOL, "rstd5", c)
                for t in range(NT):
                    i = v.scalar_tensor_tensor(out=t_tok[:, t], in0=z_tok[:, t], scalar=rstd["5"][:, t:t + 1],
                                               in1=b5_row[0:TT], op0=ALU.mult, op1=ALU.add)
                i.then_inc(r_dve, 1)

            def route(tick, c):
                gmax, gsum, gemax, grec, gsmax = (gs[:, i] for i in range(5))

                def over(a):
                    return a.unsqueeze(2).to_broadcast([TT, NT, E])
                if tick == 6:
                    need(dve, r_pe, ROUTE_PE, "gate", c)
                    v.tensor_tensor(gl[:, :, :], bk[0:TT, 2, 0:NT * E].rearrange("p (t e) -> p t e", t=NT),
                                    gate_row[0:TT].unsqueeze(1).to_broadcast([TT, NT, E]), ALU.add).then_inc(r_dve, 1)
                    need(dve, r_dve, ROUTE_DVE, "glog", c)
                    v.tensor_reduce(gmax, gl[:, :, :], AX, ALU.max).then_inc(r_dve, 1)
                    need(dve, r_dve, ROUTE_DVE, "gmax", c)
                    v.tensor_tensor(gl[:, :, :], gl[:, :, :], over(gmax), ALU.subtract).then_inc(r_dve, 1)
                if tick == 8:
                    need(dve, r_act, ROUTE_ACT, "gexp", c)
                    v.tensor_reduce(gsum, ge[:, :, :], AX, ALU.add).then_inc(r_dve, 1)
                    v.tensor_reduce(gemax, ge[:, :, :], AX, ALU.max).then_inc(r_dve, 1)
                    need(dve, r_dve, ROUTE_DVE, "gemax", c)
                    v.reciprocal(grec, gsum).then_inc(r_dve, 1)
                    v.tensor_tensor(gt[:, :, :], ge[:, :, :], over(gemax), ALU.is_equal).then_inc(r_dve, 1)
                    need(dve, r_dve, ROUTE_DVE, "gmask", c)
                    v.tensor_tensor(gt[:, :, :], gt[:, :, :], rank[:, :].unsqueeze(1).to_broadcast([TT, NT, E]),
                                    ALU.mult).then_inc(r_dve, 1)
                    need(dve, r_dve, ROUTE_DVE, "gscore", c)
                    v.tensor_reduce(gsmax, gt[:, :, :], AX, ALU.max).then_inc(r_dve, 1)
                    need(dve, r_dve, ROUTE_DVE, "gsmax", c)
                    v.tensor_tensor(gt[:, :, :], gt[:, :, :], over(gsmax), ALU.is_equal).then_inc(r_dve, 1)
                    v.tensor_tensor(rows[:, :, 2 * D], gemax, grec, ALU.mult).then_inc(r_dve, 1)
                if tick == 9:
                    need(dve, r_pe, ROUTE_PE, "rank", c)
                    v.tensor_tensor(slots[:, :, :], bk[0:TT, 3, 0:NT * E].rearrange("p (t e) -> p t e", t=NT),
                                    run[0:TT].unsqueeze(1).to_broadcast([TT, NT, E]), ALU.add).then_inc(r_dve, 1)
                    need(dve, r_dve, ROUTE_DVE, "slots", c)
                    v.tensor_tensor(slots[:, :, :], slots[:, :, :], gt[:, :, :], ALU.mult).then_inc(r_dve, 1)
                    need(dve, r_dve, ROUTE_DVE, "slot", c)
                    v.tensor_reduce(slot[:, :], slots[:, :, :], AX, ALU.add).then_inc(r_dve, 1)
                    need(dve, r_dve, ROUTE_DVE, "pos", c)
                    v.tensor_copy(row_index[:, :], slot[:, :]).then_inc(r_dve, 1)
                    v.tensor_copy(rows[:, :, 2 * D + 1], token[:, :]).then_inc(r_dve, 1)
                    need(dve, r_dve, ROUTE_DVE, "token", c)
                    v.tensor_scalar(token[:, :], token[:, :], float(T), None, ALU.add).then_inc(r_dve, 1)
                    v.tensor_tensor(run[:, :], run[:, :], bk[:, 3, NT * E:(NT + 1) * E], ALU.add).then_inc(r_dve, 1)

            def need_routed(eng, c):
                if not isinstance(c, int) or c > 0:
                    eng.wait_ge(routed, 80 * c)

            dve.wait_ge(su_dve, SU_DVE)

            def body(i, fronts=True, trigs=True, backs=True, routes=True):
                for tick in range(TICKS):
                    if fronts and tick == 2:
                        embed_out(i + 1)
                    if routes:
                        route(tick, i - 2)
                    if backs:
                        back(tick, i - 1)
                    if fronts:
                        front(tick, i + 1)
                    for g in range(KB, NI):
                        if trigs and tick == STEP_TICKS[g - KB]:
                            trig_steps(i, g)
                        if trigs and tick == STEP_TICKS[g - KB] + 1:
                            trig_wrap(i, g)
                for g in range(KB):
                    if fronts:
                        trig_steps(i + 1, g)
                        trig_wrap(i + 1, g)
                    if trigs and g == 0:
                        norm_stats(i)
                if backs:
                    softmax_end(i - 1)
                    y4_stats(i - 1)
                if trigs:
                    norm_out(i)
                if backs:
                    t_out(i - 1)

            body(-1, trigs=False, backs=False, routes=False)
            body(0, backs=False, routes=False)
            body(1, routes=False)
            body(2)
            with dve.Fori(3, CHUNKS - 1) as i:
                body(i)
            body(CHUNKS - 1, fronts=False)
            body(CHUNKS, fronts=False, trigs=False)
            body(CHUNKS + 1, fronts=False, trigs=False, backs=False)

            need(dve, r_dve, ROUTE_DVE, "run", CHUNKS - 1)
            for a in range(2):
                v.tensor_scalar(pad_slot[:, a], run[:, :], pad_at[:, a:a + 1], None, ALU.add).then_inc(place, 1)
            v.tensor_tensor(cum[:, :], run[0:1], region[:, :], ALU.subtract).then_inc(place, 1)
            v.memset(tile_no[:, :], -1.0).then_inc(place, 1)
            dve.wait_ge(place, 4)
            v.tensor_copy(pad_index[:, :, :], pad_slot[:, :, :]).then_inc(padded_at, 1)
            v.tensor_scalar(cum[:, :], cum[:, :], 1.0 / MT, (MT - 0.5) / MT - 0.5, ALU.mult, ALU.add).then_inc(place, 1)
            dve.wait_ge(place, 5)
            v.tensor_scalar(cum[:, :], cum[:, :], MAGIC, None, ALU.add).then_inc(place, 1)
            dve.wait_ge(place, 6)
            v.tensor_scalar(cum[:, :], cum[:, :], MAGIC, None, ALU.subtract).then_inc(place, 1)
            for e in range(1, E):
                dve.wait_ge(place, 6 + e)
                v.tensor_tensor(cum[:, e:e + 1], cum[:, e - 1:e], cum[:, e:e + 1], ALU.add).then_inc(place, 1)

            def place_tile(k, b):
                at = 6 + E + PLACE * k
                dve.wait_ge(place, at)
                v.tensor_scalar(tile_no[:, :], tile_no[:, :], 1.0, None, ALU.add).then_inc(place, 1)
                dve.wait_ge(place, at + 1)
                v.tensor_scalar(past[:, :], cum[:, :], tile_no[:, 0:1], None, ALU.is_le).then_inc(place, 1)
                dve.wait_ge(place, at + 2)
                v.tensor_reduce(where[:, 0:1], past[:, :], AX, ALU.add).then_inc(place, 1)
                v.tensor_tensor(past_cum[:, :], past[:, :], cum[:, :], ALU.mult).then_inc(place, 1)
                dve.wait_ge(place, at + 4)
                v.tensor_reduce(where[:, 1:2], past_cum[:, :], AX, ALU.max).then_inc(place, 1)
                v.tensor_scalar(where[:, 3:4], where[:, 0:1], float(E - 1), None, ALU.min).then_inc(place, 1)
                dve.wait_ge(place, at + 6)
                v.tensor_tensor(where[:, 1:2], tile_no[:, :], where[:, 1:2], ALU.subtract).then_inc(place, 1)
                v.tensor_scalar(where[:, 2:3], where[:, 0:1], float(REGION), None, ALU.mult).then_inc(place, 1)
                dve.wait_ge(place, at + 8)
                v.scalar_tensor_tensor(out=where[:, 2:3], in0=where[:, 1:2], scalar=float(MT), in1=where[:, 2:3],
                                       op0=ALU.mult, op1=ALU.add).then_inc(place, 1)
                dve.wait_ge(place, at + 9)
                v.tensor_scalar(where_i[:, b, :], where[:, 2:4], float(E * REGION), None, ALU.min).then_inc(tile_at, 1)
                v.memset(past_cum[:, 0:1], 0.0).then_inc(place, 1)

            def tile_in(k, b):
                dve.wait_ge(tile_T, k + 1)
                if not isinstance(k, int) or k >= 2:
                    dve.wait_ge(tile_hid, FC * (k - 1))
                v.tensor_copy(tail_tT[b % 2], tile_T_ps[b % 2]).then_inc(tile_tT, 1)
                if not isinstance(k, int):
                    dve.wait_ge(stored[b], 32 // TB * (k - b))
                v.tensor_copy(tail_ids[:, b], tail_rows[b][:, :, 2 * D + 1]).then_inc(tile_ids, 1)

            def tile_end(k, b):
                dve.wait_ge(tile_mm, k + 1)
                out_b = tail_out[b]
                v.tensor_tensor(out_b, tile_mm_ps[b % 2].rearrange("p (a d) -> p a d", a=2),
                                tail_b2[b].unsqueeze(1).to_broadcast([128, 2, D]), ALU.add).then_inc(tile_sum, 1)
                dve.wait_ge(tile_sum, k + 1)
                dve.wait_ge(tile_ids, k + 1)
                for a in range(2):
                    i = v.scalar_tensor_tensor(out=out_b[:, a], in0=out_b[:, a],
                                               scalar=tail_rows[b][:, a, 2 * D:2 * D + 1],
                                               in1=tail_rows[b][:, a, D:2 * D], op0=ALU.mult, op1=ALU.add)
                i.then_inc(tile_done, 1)

            def tile(k, b):
                tile_in(k, b)
                if not isinstance(k, int) or k >= 2:
                    tile_end(k - 2, (b - 2) % TB)
                dve.wait_ge(tile_loaded[b], loads_of_tile(k, b))
                place_tile(k + TB, b)

            for b in range(TB):
                place_tile(b, b)
            for b in range(TB):
                tile(b, b)
            with dve.Fori(1, TILES // TB) as i:
                for b in range(TB):
                    tile(TB * i + b, b)
            tile_end(TILES - 2, TB - 2)
            tile_end(TILES - 1, TB - 1)

        @block.scalar
        def _(act):
            a = nc.scalar
            act.wait_ge(su_pe, 1)
            pw = bk_flat[0:C * PS, 0:PS * D].rearrange("p (a q d) -> p a q d", q=2, d=D)
            a.activation(patch_w[0:C * PS], pw[:, :, 0], ACT.Copy).then_inc(su_act, 1)
            a.activation(odd_w.rearrange("p (a d) -> p a d", d=D), pw[:, :, 1], ACT.Copy).then_inc(su_act, 1)
            act.wait_ge(su_act, 2)
            act.dma_start(patch_w[C * PS:].rearrange("p a d -> p (a d)"), odd_w).then_inc(copied_w, 16)

            def evict_T(dst, flat, s):
                a.activation(dst[:, 0:4 * TT], flat[:, 0:4 * TT], ACT.Copy).then_inc(s, 1)
                a.activation(dst[:, 4 * TT:T], flat[:, 512:512 + TT], ACT.Copy).then_inc(s, 1)

            def halves(dst):
                return dst.rearrange("p (a k) -> p a k", a=2)

            def front(tick, c):
                if tick == 5:
                    need(act, f_pe, FRONT_PE, "h0", c)
                    need(act, f_dve, FRONT_DVE, "h1", c - 1)
                    a.activation(h0_tok[:, :, :].rearrange("p t d -> p (t d)"), fr_tok, ACT.Copy).then_inc(f_act, 1)
                if tick == 7:
                    need(act, f_pe, FRONT_PE, "x1T", c)
                    evict_T(x1T, fr_flat, f_act)
                if tick == 13:
                    need(act, f_pe, FRONT_PE, "pT", c)
                    need(act, r_pe, ROUTE_PE, "gate", c - 3)
                    a.activation(halves(pT[:, :]), fr[:, :, 0:HALF], ACT.Identity, bias=psi_b[:, 0:1]).then_inc(f_act, 1)
                if tick == 13:
                    need(act, f_pe, FRONT_PE, "qT", c)
                    need(act, f_dve, FRONT_DVE, "bnew", c)
                    for i in range(IMGS):
                        a.activation(qT[:, N * i:N * i + N], fr[:, i // 2, N * (i % 2):N * (i % 2) + N], ACT.Identity,
                                     bias=bnew[:, i:i + 1]).then_inc(f_act, 1)
                if tick == 31:
                    need(act, f_pe, FRONT_PE, "x2T", c)
                    need(act, t_dve, TRIG_DVE, f"k{NI - 1}", c - 1)
                    evict_T(x2T, fr_flat, f_act)

            def trig_step(tick, c):
                g, cs = tick // 2, tick % 2
                s = ("mmcos", "mmsin")[cs]
                need(act, t_dve, TRIG_DVE, f"and{g}", c)
                if g >= 2:
                    need(act, t_pe, TRIG_PE, f"{s}{g - 2}", c)
                else:
                    need(act, t_pe, TRIG_PE, f"{s}{NI - 2 + g}", c - 1)
                    need(act, b_pe, BACK_PE, f"pv_{IMGS - 1}", c - 2)
                a.activation(trig_buf[:, g % 2, cs], kbuf[:, g % KB, cs], ACT.Sin, bias=MINUS_PI,
                             scale=FROM_LUT).then_inc(t_act, 1)

            def trig_end(c):
                need(act, t_pe, TRIG_PE, f"mmsin{NI - 1}", c)
                a.activation(halves(csT[:, :]), acc_ps[:, :, 0:HALF], ACT.Copy).then_inc(t_act, 1)
                need(act, t_pe, TRIG_PE, "proj", c)
                need(act, b_dve, BACK_DVE, "h3", c - 1)
                a.activation(silu_tok[:, :, :].rearrange("p t d -> p (t d)"), acc_flat[0:TT, 0:NT * D],
                             ACT.Silu).then_inc(t_act, 1)

            def back(tick, c):
                if tick == 1:
                    need(act, b_pe, BACK_PE, "x3T", c)
                    evict_T(xT, bk_flat, b_act)
                if tick == 2:
                    need(act, b_pe, BACK_PE, "q3", c)
                    a.activation(halves(q3T), bk[:, 0:2, 0:HALF], ACT.Identity, bias=bqq[:, 0:1]).then_inc(b_act, 1)
                    need(act, b_pe, BACK_PE, "k3", c)
                    a.activation(halves(k3T), bk[:, 2:4, 0:HALF], ACT.Identity, bias=bkk[:, 0:1]).then_inc(b_act, 1)
                if tick == 3:
                    need(act, b_pe, BACK_PE, "v3a", c)
                    a.activation(v3[:, 0].rearrange("p i d -> p (i d)"), bk[0:QA, 3, :], ACT.Copy).then_inc(b_act, 1)
                if tick == 4:
                    need(act, b_pe, BACK_PE, "v3b", c)
                    a.activation(v3[0:QB, 1].rearrange("p i d -> p (i d)"), bk[0:QB, 3, :], ACT.Copy).then_inc(b_act, 1)
                if tick == 7:
                    need(act, b_dve, BACK_DVE, "sub3", c)
                    e3f = e3[:, :, :, :].rearrange("p a i k -> p (a i k)")
                    a.activation(e3f, e3f, ACT.Exp).then_inc(b_act, 1)
                if tick == 9:
                    need(act, b_pe, BACK_PE, "pTa", c)
                    a.activation(halves(pTa), bk[0:QA, 0:2, 0:HALF], ACT.Copy).then_inc(b_act, 1)
                    a.activation(pTb[:, :], bk[0:QB, 2, 0:IMGS * QB], ACT.Copy).then_inc(b_act, 1)
                if tick == 10:
                    need(act, b_pe, BACK_PE, "oT", c)
                    a.activation(halves(oT), bk[:, 2:4, 0:HALF], ACT.Identity, bias=bv3c[:, 0:1]).then_inc(b_act, 1)
                if tick == 14:
                    need(act, b_pe, BACK_PE, "x4T", c)
                    evict_T(xT, bk_flat, b_act)
                if tick == 16:
                    need(act, b_pe, BACK_PE, "q4", c)
                    for g in range(2):
                        a.activation(halves(q4T[:, g]), bk[:, 2 * g:2 * g + 2, 0:HALF], ACT.Identity,
                                     bias=bq4c[:, g:g + 1]).then_inc(b_act, 1)
                if tick == 17:
                    need(act, b_pe, BACK_PE, "k4", c)
                    for g in range(2):
                        a.activation(halves(k4T[:, g]), bk[:, 2 * g:2 * g + 2, 0:HALF], ACT.Identity,
                                     bias=bk4c[:, g:g + 1]).then_inc(b_act, 1)
                if tick == 18:
                    need(act, b_pe, BACK_PE, "v4", c)
                    for t, (_, n) in enumerate(QS):
                        a.activation(v4[0:n, t, :, :, 0:HD].rearrange("p i h d -> p (i h) d"),
                                     bk[0:n, t, :].rearrange("p (k d) -> p k d", d=HD), ACT.Copy).then_inc(b_act, 1)

            def pv_out(i, c):
                need(act, b_pe, BACK_PE, f"pv_{i}", c)
                a.activation(o4T[:, :, N * i:N * i + N], acc_ps[:, i % 2, 0:2 * N].rearrange("p (g k) -> p g k", g=2),
                             ACT.Copy).then_inc(b_act, 1)

            def back_end(c):
                for i in range(IMGS):
                    for r in range(4):
                        t, g = r // 2, r % 2
                        n = QS[t][1]
                        need(act, b_pe, BACK_PE, f"st{r}_{i}", c)
                        if i >= 2:
                            need(act, b_pe, BACK_PE, f"pv_{i - 2}", c)
                        a.activation(p4[i % 2][0:n, t, g].rearrange("p (a j) k -> p a (j k)", a=2),
                                     bk[0:n, 2 * g:2 * g + 2, 0:2 * N], ACT.Exp, scale=float(HD) ** -0.5).then_inc(b_act, 1)
                        if r == 1 and i:
                            pv_out(i - 1, c)
                pv_out(IMGS - 1, c)
                need(act, b_pe, BACK_PE, "onT", c)
                evict_T(onT, bk_flat, b_act)

            def route(tick, c):
                if tick == 4:
                    need(act, r_pe, ROUTE_PE, "tT", c)
                    evict_T(tT, bk_flat, r_act)
                if tick == 7:
                    need(act, r_dve, ROUTE_DVE, "gsub", c)
                    a.activation(ge[:, :, :], gl[:, :, :], ACT.Exp).then_inc(r_act, 1)

            act.wait_ge(loaded_w, LOADED)
            act.wait_ge(su_dve, SU_DVE)

            def body(i, fronts=True, trigs=True, backs=True, routes=True):
                for tick in range(TICKS):
                    if trigs:
                        trig_step(tick, i)
                    if backs:
                        back(tick, i - 1)
                    if routes:
                        route(tick, i - 2)
                    if fronts:
                        front(tick, i + 1)
                if trigs:
                    trig_end(i)
                if backs:
                    back_end(i - 1)

            body(-1, trigs=False, backs=False, routes=False)
            body(0, backs=False, routes=False)
            body(1, routes=False)
            body(2)
            with act.Fori(3, CHUNKS - 1) as i:
                body(i)
            body(CHUNKS - 1, fronts=False)
            body(CHUNKS, fronts=False, trigs=False)
            body(CHUNKS + 1, fronts=False, trigs=False, backs=False)

            def gelu(k, b, first):
                if not first:
                    act.wait_ge(tile_mm, k - 1)
                for f in range(FC):
                    act.wait_ge(tile_hid, FC * k + f + 1)
                    a.activation(tail_hid[b % 2][:, f], tile_hid_ps[f], ACT.Gelu_apprx_tanh,
                                 bias=tail_b1[b][:, f:f + 1]).then_inc(tile_gelu, 1)

            for b in range(TB):
                gelu(b, b, b < 2)
            with act.Fori(1, TILES // TB) as i:
                for b in range(TB):
                    gelu(TB * i + b, b, False)

        @block.tensor
        def _(pe):
            mm, tr = nc.tensor.matmul, nc.tensor.transpose
            pe.wait_ge(su_pool, POOL_SETUP)
            pe.wait_ge(su_dve, 16)
            for p2 in range(PS):
                i = tr(bk_flat[0:C * PS, D * p2:D * p2 + D], wt[:, p2].rearrange("d c a -> d (c a)"), ident[:, :])
            i.then_inc(su_pe, 1)

            def weights():
                pe.wait_ge(su_act, 2)
                pe.wait_ge(loaded_w, LOADED)
                tr(bk[:, 0, 0:128], su[0][:, :], ident[:, :])
                tr(bk[:, 0, 128:256], zg_w[:, 0:128], ident[:, :])
                tr(bk[:, 0, 256:384], su[1][:, :], ident[:, :]).then_inc(su_pe, 1)
                pe.wait_ge(su_dve, 19)
                mm(bk[:, 1, 0:128], su[3][:, :], su[3][:, :], start=True, stop=True)
                mm(bk[:, 1, 128:256], bd_we[:, :], su[4][:, :], start=True, stop=True).then_inc(su_pe, 1)
                mm(bk[:, 1, 256:257], bd_we[:, :], su_col[:, 4:5], start=True, stop=True).then_inc(su_pe, 1)
                pe.wait_ge(su_dve, 25)
                mm(bk[:, 2, 0:128], su[6][:, :], su[5][:, :], start=True, stop=True).then_inc(su_pe, 1)
                mm(bk[:, 2, 128:256], su[7][:, :], su[5][:, :], start=True, stop=False)
                mm(bk[:, 2, 128:256], su[1][:, :], su[3][:, :], start=False, stop=True).then_inc(su_pe, 1)
                for k, b_row in enumerate((bq_row, bk_row)):
                    for g in range(2):
                        mm(bk[:, 2, 384 + 2 * k + g:385 + 2 * k + g], b_row[:, g].rearrange("p j k -> p (j k)"),
                           ones[0:1, 0:1], start=True, stop=True)
                mm(bk[:, 2, 256:384], su[0][:, :], wo4[:, :], start=True, stop=True).then_inc(su_pe, 1)
                for k in range(4):
                    i = tr(bk[:, 3, NW * k:NW * k + NW], lutW[:, k], ident[0:NW, 0:NW])
                i.then_inc(su_pe, 1)

            def transposed(src, flat):
                for t in range(NT):
                    at = TT * t if t < 4 else 512
                    i = tr(flat[:, at:at + TT], src[:, t], ident[0:TT, 0:TT])
                return i

            def tokens(src, flat):
                for t in range(NT):
                    i = tr(flat[0:TT, D * t:D * t + D], src[:, TT * t:TT * t + TT], ident[:, :])
                return i

            def embed(m, c):
                if m == 0:
                    need(pe, f_act, FRONT_ACT, "x2Tb", c - 1)
                pe.wait_ge(x_loaded[m % 2], 96 * (2 * c + m // 2 + 1))
                for k in range(PS // 2):
                    i = mm(fr[:, m // 2, NPATCH * (m % 2):NPATCH * (m % 2) + NPATCH], patch_w[:, k],
                           patches[:, m % 2, :, 2 * k:IW - 1:PS], start=(k == 0), stop=(k == PS // 2 - 1))
                i.then_inc(e_pe, 1)

            def front(tick, c):
                if tick == 5:
                    need(pe, e_dve, EMB_DVE, "emb23", c)
                    tokens(h0T[:, :, :].rearrange("d i n -> d (i n)"), fr_flat).then_inc(f_pe, 1)
                if tick == 7:
                    need(pe, f_dve, FRONT_DVE, "x1", c)
                    transposed(x1_tok, fr_flat).then_inc(f_pe, 1)
                for r in range(2):
                    if tick == 8 + r:
                        if r:
                            need(pe, f_dve, FRONT_DVE, "zg0b", c)
                        else:
                            need(pe, f_act, FRONT_ACT, "x1Tb", c)
                        for k in range(2):
                            for t, (q0, n) in enumerate(QS):
                                at = N * (2 * r + k) + q0
                                i = mm(fr[0:n, k, 256 * t:256 * t + 256], x1T[:, at:at + n], zg_w[:, :],
                                       start=True, stop=True)
                        i.then_inc(f_pe, 1)
                if tick == 10:
                    need(pe, f_dve, FRONT_DVE, "zg1b", c)
                    for i in range(IMGS):
                        for t, (_, n) in enumerate(QS):
                            mm(fr[:, 0, 128 * i:128 * i + 128], zg[0:n, t, i, 0:128], zg[0:n, t, i, 128:256],
                               start=(t == 0), stop=(t == 1))
                    for i in range(IMGS):
                        for t, (_, n) in enumerate(QS):
                            last = mm(fr[:, 1, i:i + 1], zg[0:n, t, i, 128:256], ones[0:n, 0:1], start=(t == 0),
                                      stop=(t == 1))
                    last.then_inc(f_pe, 1)
                if tick == 13:
                    need(pe, f_dve, FRONT_DVE, "bnew", c)
                    for k in range(2):
                        i = mm(fr[:, k, 0:HALF], psi_w[:, :], x1T[:, HALF * k:HALF * k + HALF], start=True, stop=True)
                    i.then_inc(f_pe, 1)
                if tick == 13:
                    need(pe, f_act, FRONT_ACT, "pT", c)
                    for i in range(IMGS):
                        last = mm(fr[:, i // 2, N * (i % 2):N * (i % 2) + N], wnew[:, i], pT[:, N * i:N * i + N],
                                  start=True, stop=True)
                    last.then_inc(f_pe, 1)
                if tick == 14:
                    need(pe, f_act, FRONT_ACT, "qT3", c)
                    for t in range(NT):
                        i = mm(fr_flat[0:TT, D * t:D * t + D], qT[:, TT * t:TT * t + TT], wh[:, :], start=True, stop=True)
                    i.then_inc(f_pe, 1)
                if tick == 17:
                    need(pe, f_dve, FRONT_DVE, "x2", c)
                    transposed(x1_tok, fr_flat).then_inc(f_pe, 1)

            def trig_step(tick, c):
                g, cs = tick // 2, tick % 2
                s = ("cos", "sin")[cs]
                if tick == 0:
                    need(pe, t_act, TRIG_ACT, "silu", c - 1)
                    need(pe, b_act, BACK_ACT, f"pv_{IMGS - 1}", c - 2)
                need(pe, t_act, TRIG_ACT, f"{s}{g}", c)
                for half in range(2):
                    for j in range(NJ):
                        at = ((NI * j + g) * 2 + cs) * 32
                        i = mm(acc_ps[32 * j:32 * j + 32, half, 0:HALF], trig_w[:, at:at + 32],
                               trig_buf[:, g % 2, cs, j, HALF * half:HALF * half + HALF],
                               start=(g == 0 and cs == 0), stop=(g == NI - 1 and cs == 1))
                i.then_inc(t_pe, 1)

            def trig_end(c):
                need(pe, t_act, TRIG_ACT, "csT", c)
                for t in range(NT):
                    i = mm(acc_flat[0:TT, D * t:D * t + D], csT[:, TT * t:TT * t + TT], proj_w[:, :], start=True, stop=True)
                i.then_inc(t_pe, 1)

            def back(tick, c):
                if tick == 1:
                    need(pe, n_dve, NORM_DVE, "x3", c)
                    transposed(x3_tok, bk_flat).then_inc(b_pe, 1)
                if tick == 2:
                    need(pe, b_act, BACK_ACT, "x3Tb", c)
                    need(pe, r_dve, ROUTE_DVE, "y4", c - 1)
                    for w, k0 in ((wqq, 0), (wkk, 2)):
                        for k in range(2):
                            i = mm(bk[:, k0 + k, 0:HALF], w[:, :, :].rearrange("p a b -> p (a b)"),
                                   xT[:, HALF * k:HALF * k + HALF], start=True, stop=True)
                        i.then_inc(b_pe, 1)
                if tick == 3:
                    need(pe, b_act, BACK_ACT, "k3", c)
                    for i in range(IMGS):
                        at = N * i
                        mm(bk[0:QA, 0, QA * i:QA * i + QA], q3T[0:DA, at:at + QA], k3T[0:DA, at:at + QA],
                           start=True, stop=True)
                        last = mm(bk[0:QB, 1 + i // 2, N * (i % 2):N * (i % 2) + N], q3T[DA:128, at + QA:at + N],
                                  k3T[DA:128, at:at + N], start=True, stop=True)
                    last.then_inc(b_pe, 1)
                for t, (q0, n) in enumerate(QS):
                    if tick == 3 + t:
                        if t:
                            need(pe, b_act, BACK_ACT, "v3a", c)
                        for i in range(IMGS):
                            last = mm(bk[0:n, 3, D * i:D * i + D], xT[:, N * i + q0:N * i + q0 + n], wv3[:, :],
                                      start=True, stop=True)
                        last.then_inc(b_pe, 1)
                if tick == 9:
                    need(pe, b_dve, BACK_DVE, "p3", c)
                    need(pe, r_dve, ROUTE_DVE, "glog", c - 1)
                    need(pe, r_act, ROUTE_ACT, "tTb", c - 1)
                    for i in range(IMGS):
                        at = N * (i % 2)
                        tr(bk[0:QA, i // 2, at:at + QA], e3[:, 0, i, 0:QA], ident[0:QA, 0:QA])
                        tr(bk[0:QA, i // 2, at + QA:at + N], e3[0:QB, 1, i, 0:QA], ident[0:QB, 0:QB])
                        last = tr(bk[0:QB, 2, QB * i:QB * i + QB], e3[0:QB, 1, i, QA:N], ident[0:QB, 0:QB])
                    last.then_inc(b_pe, 1)
                if tick == 10:
                    need(pe, b_act, BACK_ACT, "pTb", c)
                    need(pe, r_dve, ROUTE_DVE, "run", c - 1)
                    for i in range(IMGS):
                        at = N * (i % 2)
                        mm(bk[:, 2 + i // 2, at:at + N], v3[:, 0, i], pTa[:, N * i:N * i + N], start=True, stop=False)
                        last = mm(bk[:, 2 + i // 2, at + QA:at + N], v3[0:QB, 1, i], pTb[:, QB * i:QB * i + QB],
                                  start=False, stop=True)
                    last.then_inc(b_pe, 1)
                if tick == 11:
                    need(pe, b_act, BACK_ACT, "oT", c)
                    tokens(oT, bk_flat[:, 512:]).then_inc(b_pe, 1)
                if tick == 14:
                    need(pe, b_dve, BACK_DVE, "x4", c)
                    transposed(x4_tok, bk_flat).then_inc(b_pe, 1)
                for k, (w, ready) in enumerate(((wq4, "x4Tb"), (wk4, "q4b"))):
                    if tick == 16 + k:
                        need(pe, b_act, BACK_ACT, ready, c)
                        for g in range(2):
                            for half in range(2):
                                i = mm(bk[:, 2 * g + half, 0:HALF], w[:, g].rearrange("p j k -> p (j k)"),
                                       xT[:, HALF * half:HALF * half + HALF], start=True, stop=True)
                        i.then_inc(b_pe, 1)
                if tick == 18:
                    need(pe, b_act, BACK_ACT, "k4b", c)
                    for t, (q0, n) in enumerate(QS):
                        for i in range(IMGS):
                            last = mm(bk[0:n, t, D * i:D * i + D], xT[:, N * i + q0:N * i + q0 + n], wv4[:, :],
                                      start=True, stop=True)
                    last.then_inc(b_pe, 1)
                for r in range(2 * IMGS):
                    q0, n = QS[r % 2]
                    at = N * (r // 2)
                    if tick == 23 + r:
                        for g in range(2):
                            if r:
                                need(pe, b_dve, BACK_DVE, f"s4{'ab'[g]}_{r - 1}", c)
                            else:
                                need(pe, b_act, BACK_ACT, "v4b", c)
                                need(pe, b_pool, BACK_POOL, f"kM{'ab'[g]}", c)
                            for j in range(NJ):
                                i = mm(bk[0:n, 2 * g + j // 2, N * (j % 2):N * (j % 2) + N], q4T[:, g, at + q0:at + q0 + n],
                                       kM[:, NJ * g + j, at:at + N], start=True, stop=True)
                            i.then_inc(b_pe, 1)
                    if tick == 24 + r:
                        need(pe, b_dve, BACK_DVE, f"s4b_{r}", c)
                        tr(bk[:, r // 2, 2 * N + q0:2 * N + q0 + n], m4[0:n, r % 2], ident[0:n, 0:n]).then_inc(b_pe, 1)

            def scores(r, i, c):
                t, g = r // 2, r % 2
                k0, n = QS[t]
                at = N * i
                if i or t:
                    need(pe, b_act, BACK_ACT, f"exp{r - 2}_{i}" if t else f"exp{r + 2}_{i - 1}", c)
                else:
                    need(pe, b_dve, BACK_DVE, "qm1", c)
                for j in range(NJ):
                    k = mm(bk[0:n, 2 * g + j // 2, N * (j % 2):N * (j % 2) + N], kM[:, NJ * g + j, at + k0:at + k0 + n],
                           q4T[:, g, at:at + N], start=True, stop=True)
                k.then_inc(b_pe, 1)

            def weighted(i, c, trig_c):
                need(pe, b_act, BACK_ACT, f"exp3_{i}", c)
                if i >= 2:
                    need(pe, b_act, BACK_ACT, f"pv_{i - 2}", c)
                else:
                    need(pe, t_act, TRIG_ACT, "silu", trig_c)
                for g in range(2):
                    for t, (_, n) in enumerate(QS):
                        for j in range(NJ):
                            last = mm(acc_ps[32 * j:32 * j + 32, i % 2, N * g:N * g + N], v4[0:n, t, i, NJ * g + j],
                                      p4[i % 2][0:n, t, g, j], start=(t == 0), stop=(t == 1))
                last.then_inc(b_pe, 1)

            def route(tick, c, back_c):
                if tick == 4:
                    need(pe, r_dve, ROUTE_DVE, "t5", c)
                    need(pe, b_dve, BACK_DVE, "mask3b", back_c)
                    transposed(t_tok, bk_flat).then_inc(r_pe, 1)
                if tick == 6:
                    need(pe, r_act, ROUTE_ACT, "tTb", c)
                    for t in range(NT):
                        i = mm(bk[0:TT, 2, E * t:E * t + E], tT[:, TT * t:TT * t + TT], gate_w[:, :], start=True, stop=True)
                    i.then_inc(r_pe, 1)
                if tick == 9:
                    need(pe, r_dve, ROUTE_DVE, "goh", c)
                    need(pe, b_act, BACK_ACT, "v3b", back_c)
                    g_all = gt_room[:, :, :].rearrange("p t e -> p (t e)")
                    mm(bk[:, 3, 0:E * (NT + 1)], ones[0:TT, :], g_all, start=True, stop=False)
                    mm(bk[:, 3, 0:E * NT], before[:, :], g_all[:, E:], start=False, stop=False)
                    for u in range(2, NT + 1):
                        i = mm(bk[:, 3, E * u:E * (NT + 1)], ones[0:TT, :], g_all[:, E:E * (NT + 2 - u)],
                               start=False, stop=(u == NT))
                    i.then_inc(r_pe, 1)

            def back_end(c, trig_c, fill):
                for i in range(IMGS):
                    for r in range(4):
                        scores(r, i, c)
                        if i == 0 and r < 2:
                            fill(r)
                        if r == 1 and i:
                            weighted(i - 1, c, trig_c)
                weighted(IMGS - 1, c, trig_c)
                need(pe, b_act, BACK_ACT, f"pv_{IMGS - 1}", c)
                for t in range(NT):
                    for g in range(2):
                        i = tr(bk_flat[0:TT, 128 * (2 * t + g):128 * (2 * t + g) + 128], o4T[:, g, TT * t:TT * t + TT],
                               ident[:, :])
                i.then_inc(b_pe, 1)
                fill(2)
                need(pe, b_dve, BACK_DVE, "on", c)
                transposed(on_tok, bk_flat).then_inc(b_pe, 1)
                fill(3)
                need(pe, b_act, BACK_ACT, "onTb", c)
                for t in range(NT):
                    i = mm(bk_flat[0:TT, 1024 + D * t:1024 + D * t + D], onT[:, TT * t:TT * t + TT], wo4[:, :],
                           start=True, stop=True)
                i.then_inc(b_pe, 1)

            pe.wait_ge(copied_w, 16)
            for m in range(IMGS - 1):
                embed(m, 0)
            weights()
            pe.wait_ge(su_dve, SU_DVE)

            def body(i, embeds=True, fronts=True, trigs=True, backs=True, routes=True):
                for tick in range(TICKS):
                    if fronts and tick == 1:
                        embed(IMGS - 1, i + 1)
                    if backs:
                        back(tick, i - 1)
                    if routes:
                        route(tick, i - 2, i - 1 if backs else i - 2)
                    if fronts:
                        front(tick, i + 1)
                    if trigs:
                        trig_step(tick, i)

                def fill(k):
                    if k == 0 and trigs:
                        trig_end(i)
                    if k and embeds:
                        embed(k - 1, i + 2)
                if backs:
                    back_end(i - 1, i if trigs else i - 1, fill)
                else:
                    for k in range(IMGS):
                        fill(k)

            body(-1, trigs=False, backs=False, routes=False)
            body(0, backs=False, routes=False)
            body(1, routes=False)
            body(2)
            with pe.Fori(3, CHUNKS - 2) as i:
                body(i)
            body(CHUNKS - 2, embeds=False)
            body(CHUNKS - 1, embeds=False, fronts=False)
            body(CHUNKS, embeds=False, fronts=False, trigs=False)
            body(CHUNKS + 1, embeds=False, fronts=False, trigs=False, backs=False)

            def product(k, b):
                pe.wait_ge(tile_gelu, FC * (k + 1))
                if not isinstance(k, int) or k >= 2:
                    pe.wait_ge(tile_sum, k - 1)
                for a in range(2):
                    for f in range(FC):
                        i = mm(tile_mm_ps[b % 2][:, D * a:D * a + D], tail_hid[b % 2][:, f, 128 * a:128 * a + 128],
                               tail_w[b][:, FF + D * f:FF + D * f + D], start=(f == 0), stop=(f == FC - 1))
                i.then_inc(tile_mm, 1)

            def hidden(k, b):
                pe.wait_ge(tile_tT, k + 1)
                for f in range(FC):
                    if not isinstance(k, int) or k > 0:
                        pe.wait_ge(tile_gelu, FC * (k - 1) + f + 1)
                    mm(tile_hid_ps[f], tail_w[b][:, 128 * f:128 * f + 128], tail_tT[b % 2], start=True,
                       stop=True).then_inc(tile_hid, 1)

            def tile(k, b):
                if not isinstance(k, int) or k >= 1:
                    hidden(k - 1, (b - 1) % TB)
                pe.wait_ge(tile_loaded[b], loads_of_tile(k, b))
                if not isinstance(k, int) or k >= 2:
                    pe.wait_ge(tile_tT, k - 1)
                for a in range(2):
                    i = tr(tile_T_ps[b % 2][:, 128 * a:128 * a + 128], tail_rows[b][:, a, 0:D], ident[:, :])
                i.then_inc(tile_T, 1)
                if not isinstance(k, int) or k >= 2:
                    product(k - 2, (b - 2) % TB)

            for b in range(TB):
                tile(b, b)
            with pe.Fori(1, TILES // TB) as i:
                for b in range(TB):
                    tile(TB * i + b, b)
            hidden(TILES - 1, TB - 1)
            product(TILES - 2, TB - 2)
            product(TILES - 1, TB - 1)


PLACE = 10
SU_DVE = 46
POOL_SETUP = 21 + 3 * E

_INS = ['x', 'cls_tok', 'L0_tok_W', 'L0_tok_b', 'L0_tok_cls_token', 'L0_tok_pos_emb', 'L0_attn_W_phi', 'L0_attn_b_phi',
        'L0_attn_W_e', 'L0_attn_b_e', 'L0_attn_W_g', 'L0_attn_g_bias', 'L0_attn_W_psi', 'L0_attn_b_psi', 'L0_attn_W_h',
        'L0_attn_h_bias', 'L0_ffn_W', 'L0_ffn_B_param', 'L0_ffn_attn_cos', 'L0_ffn_attn_sin', 'L0_ffn_proj_cos_w',
        'L0_ffn_proj_sin_w', 'L1_attn_Wq', 'L1_attn_bq', 'L1_attn_Wk', 'L1_attn_bk', 'L1_attn_Wv', 'L1_attn_bv',
        'L1_attn_gamma', 'L1_attn_beta', 'L1_ffn_ln1_g', 'L1_ffn_ln1_b', 'L1_ffn_Wq', 'L1_ffn_bq', 'L1_ffn_Wk',
        'L1_ffn_bk', 'L1_ffn_Wv', 'L1_ffn_bv', 'L1_ffn_Wo', 'L1_ffn_bo', 'L1_ffn_gate_W', 'L1_ffn_gate_b', 'L1_ffn_W1',
        'L1_ffn_b1', 'L1_ffn_W2', 'L1_ffn_b2']


def kernel(**inputs):
    import numpy as _np
    import concourse.bacc as _bacc
    from concourse import mybir as _mybir
    from concourse.bass_utils import run_bass_kernel_spmd as _run

    nc = _bacc.Bacc("TRN2", target_bir_lowering=False, num_devices=1)
    arrays, args = {}, []
    for name in _INS:
        a = _np.ascontiguousarray(inputs[name])
        arrays[f"in_{name}_dram"] = a
        args.append(nc.dram_tensor(f"in_{name}_dram", a.shape, _mybir.dt.from_np(a.dtype), kind="ExternalInput").ap())
    args.append(nc.dram_tensor("out_0_dram", (B, N, D), F32, kind="ExternalOutput").ap())
    args.append(nc.dram_tensor("expert_rows", (E * REGION + MT, ROW), F32, kind="Internal").ap())
    args.append(nc.dram_tensor("b1_cols", (E, 128, FC), F32, kind="Internal").ap())
    vit_tower(nc, *args)
    r = _run(nc, [arrays], core_ids=[0])
    return r.results[0]["out_0_dram"]
```
